# Optimizing a Trainium2 kernel written in Bass

```python
import numpy as np
import jax
import jax.numpy as jnp

def _softmax(x, axis=-1):
    return jax.nn.softmax(x, axis=axis)

def _gelu(x):
    return jax.nn.gelu(x, approximate=True)

def _silu(x):
    return jax.nn.silu(x)

def _sigmoid(x):
    return jax.nn.sigmoid(x)

def _layernorm(x, axis=-1, eps=1e-05):
    m = jnp.mean(x, axis=axis, keepdims=True)
    v = jnp.var(x, axis=axis, keepdims=True)
    return (x - m) / jnp.sqrt(v + eps)

def _scatter_add(tgt, idx, src, axis=0):
    return tgt.at[idx].add(src)

def _segment_sum(src, seg, n):
    return jax.ops.segment_sum(src, seg, n)
kernel_name = 'mk_conv_seq_d2_conv_nhwc768_r4_cd877f'

def setup_inputs(seed: int=0):
    np.random.seed(seed)
    _w = jnp.asarray

    def _rec_inputs():
        import jax
        import jax.numpy as jnp
        _gk = jax.random.key(seed)
        x = -0.0002221 + 1 * jax.random.normal(jax.random.fold_in(_gk, 1), (8, 16, 16, 192), jnp.float32)
        return x
    x = _rec_inputs()

    def _L0_conv_setup():
        import jax, jax.numpy as jnp
        import numpy as np
        B, H, W, D = (8, 16, 16, 192)
        HEADS, WS = (12, 14)
        HD = D // HEADS
        MLP = 4 * D
        LREL = 2 * WS - 1
        EPS = 1e-05

        def _layer_norm(x, w, b):
            mu = jnp.mean(x, axis=-1, keepdims=True)
            var = jnp.mean(jnp.square(x - mu), axis=-1, keepdims=True)
            return (x - mu) * jax.lax.rsqrt(var + EPS) * w + b
        key = jax.random.key(seed)
        ks = jax.random.split(key, 12)
        s = 0.02
        return {'x': jax.random.normal(ks[0], (B, H, W, D), jnp.float32), 'qkv_w': jax.random.normal(ks[1], (D, 3 * D), jnp.float32) * s, 'qkv_b': jax.random.normal(ks[2], (3 * D,), jnp.float32) * s, 'proj_w': jax.random.normal(ks[3], (D, D), jnp.float32) * s, 'proj_b': jax.random.normal(ks[4], (D,), jnp.float32) * s, 'rel_pos_h': jax.random.normal(ks[5], (LREL, HD), jnp.float32) * s, 'rel_pos_w': jax.random.normal(ks[6], (LREL, HD), jnp.float32) * s, 'norm1_w': jnp.ones((D,), jnp.float32), 'norm1_b': jnp.zeros((D,), jnp.float32), 'norm2_w': jnp.ones((D,), jnp.float32), 'norm2_b': jnp.zeros((D,), jnp.float32), 'fc1_w': jax.random.normal(ks[7], (D, MLP), jnp.float32) * s, 'fc1_b': jax.random.normal(ks[8], (MLP,), jnp.float32) * s, 'fc2_w': jax.random.normal(ks[9], (MLP, D), jnp.float32) * s, 'fc2_b': jax.random.normal(ks[10], (D,), jnp.float32) * s}
    _L0_conv_all = _L0_conv_setup()
    _L0_conv_in = {k: v for k, v in _L0_conv_all.items() if k in ('qkv_w', 'qkv_b', 'proj_w', 'proj_b', 'rel_pos_h', 'rel_pos_w', 'norm1_w', 'norm1_b', 'norm2_w', 'norm2_b', 'fc1_w', 'fc1_b', 'fc2_w', 'fc2_b')}
    del _L0_conv_all

    def _L1_conv_setup():
        import jax, jax.numpy as jnp
        import numpy as np
        B, H, W, C = (8, 16, 16, 192)
        WIN = 16
        NH, HD = (12, 48)

        def _layer_norm(x, scale, offset, eps=1e-05):
            m = jnp.mean(x, axis=-1, keepdims=True)
            v = jnp.var(x, axis=-1, keepdims=True)
            return (x - m) * jax.lax.rsqrt(v + eps) * scale + offset
        key = jax.random.key(seed)
        ks = jax.random.split(key, 10)
        s = 0.02
        return {'x': jax.random.normal(ks[0], (B, H, W, C), jnp.float32), 'wq': jax.random.normal(ks[1], (C, NH * HD), jnp.float32) * s, 'bq': jnp.zeros((NH * HD,), jnp.float32), 'wk': jax.random.normal(ks[2], (C, NH * HD), jnp.float32) * s, 'bk': jnp.zeros((NH * HD,), jnp.float32), 'wv': jax.random.normal(ks[3], (C, NH * HD), jnp.float32) * s, 'bv': jnp.zeros((NH * HD,), jnp.float32), 'rel_pos_0': jax.random.normal(ks[4], (2 * WIN - 1, HD), jnp.float32) * s, 'rel_pos_1': jax.random.normal(ks[5], (2 * WIN - 1, HD), jnp.float32) * s, 'wo': jax.random.normal(ks[6], (NH * HD, C), jnp.float32) * s, 'bo': jnp.zeros((C,), jnp.float32), 'ln1_scale': jnp.ones((C,), jnp.float32), 'ln1_offset': jnp.zeros((C,), jnp.float32), 'ln2_scale': jnp.ones((C,), jnp.float32), 'ln2_offset': jnp.zeros((C,), jnp.float32), 'w1': jax.random.normal(ks[7], (C, 4 * C), jnp.float32) * s, 'b1': jnp.zeros((4 * C,), jnp.float32), 'w2': jax.random.normal(ks[8], (4 * C, C), jnp.float32) * s, 'b2': jnp.zeros((C,), jnp.float32)}
    _L1_conv_all = _L1_conv_setup()
    _L1_conv_in = {k: v for k, v in _L1_conv_all.items() if k in ('wq', 'bq', 'wk', 'bk', 'wv', 'bv', 'rel_pos_0', 'rel_pos_1', 'wo', 'bo', 'ln1_scale', 'ln1_offset', 'ln2_scale', 'ln2_offset', 'w1', 'b1', 'w2', 'b2')}
    del _L1_conv_all
    return {'x': x, 'L0_conv_qkv_w': _L0_conv_in['qkv_w'], 'L0_conv_qkv_b': _L0_conv_in['qkv_b'], 'L0_conv_proj_w': _L0_conv_in['proj_w'], 'L0_conv_proj_b': _L0_conv_in['proj_b'], 'L0_conv_rel_pos_h': _L0_conv_in['rel_pos_h'], 'L0_conv_rel_pos_w': _L0_conv_in['rel_pos_w'], 'L0_conv_norm1_w': _L0_conv_in['norm1_w'], 'L0_conv_norm1_b': _L0_conv_in['norm1_b'], 'L0_conv_norm2_w': _L0_conv_in['norm2_w'], 'L0_conv_norm2_b': _L0_conv_in['norm2_b'], 'L0_conv_fc1_w': _L0_conv_in['fc1_w'], 'L0_conv_fc1_b': _L0_conv_in['fc1_b'], 'L0_conv_fc2_w': _L0_conv_in['fc2_w'], 'L0_conv_fc2_b': _L0_conv_in['fc2_b'], 'L1_conv_wq': _L1_conv_in['wq'], 'L1_conv_bq': _L1_conv_in['bq'], 'L1_conv_wk': _L1_conv_in['wk'], 'L1_conv_bk': _L1_conv_in['bk'], 'L1_conv_wv': _L1_conv_in['wv'], 'L1_conv_bv': _L1_conv_in['bv'], 'L1_conv_rel_pos_0': _L1_conv_in['rel_pos_0'], 'L1_conv_rel_pos_1': _L1_conv_in['rel_pos_1'], 'L1_conv_wo': _L1_conv_in['wo'], 'L1_conv_bo': _L1_conv_in['bo'], 'L1_conv_ln1_scale': _L1_conv_in['ln1_scale'], 'L1_conv_ln1_offset': _L1_conv_in['ln1_offset'], 'L1_conv_ln2_scale': _L1_conv_in['ln2_scale'], 'L1_conv_ln2_offset': _L1_conv_in['ln2_offset'], 'L1_conv_w1': _L1_conv_in['w1'], 'L1_conv_b1': _L1_conv_in['b1'], 'L1_conv_w2': _L1_conv_in['w2'], 'L1_conv_b2': _L1_conv_in['b2']}

def reference(x, L0_conv_qkv_w, L0_conv_qkv_b, L0_conv_proj_w, L0_conv_proj_b, L0_conv_rel_pos_h, L0_conv_rel_pos_w, L0_conv_norm1_w, L0_conv_norm1_b, L0_conv_norm2_w, L0_conv_norm2_b, L0_conv_fc1_w, L0_conv_fc1_b, L0_conv_fc2_w, L0_conv_fc2_b, L1_conv_wq, L1_conv_bq, L1_conv_wk, L1_conv_bk, L1_conv_wv, L1_conv_bv, L1_conv_rel_pos_0, L1_conv_rel_pos_1, L1_conv_wo, L1_conv_bo, L1_conv_ln1_scale, L1_conv_ln1_offset, L1_conv_ln2_scale, L1_conv_ln2_offset, L1_conv_w1, L1_conv_b1, L1_conv_w2, L1_conv_b2):
    import jax
    import jax.numpy as jnp

    def _L0_conv_ref(x, qkv_w, qkv_b, proj_w, proj_b, rel_pos_h, rel_pos_w, norm1_w, norm1_b, norm2_w, norm2_b, fc1_w, fc1_b, fc2_w, fc2_b):
        import jax, jax.numpy as jnp
        import numpy as np
        B, H, W, D = (8, 16, 16, 192)
        HEADS, WS = (12, 14)
        HD = D // HEADS
        MLP = 4 * D
        LREL = 2 * WS - 1
        EPS = 1e-05

        def _layer_norm(x, w, b):
            mu = jnp.mean(x, axis=-1, keepdims=True)
            var = jnp.mean(jnp.square(x - mu), axis=-1, keepdims=True)
            return (x - mu) * jax.lax.rsqrt(var + EPS) * w + b
        shortcut = x
        xn = _layer_norm(x, norm1_w, norm1_b)
        pad_h = (WS - H % WS) % WS
        pad_w = (WS - W % WS) % WS
        Hp, Wp = (H + pad_h, W + pad_w)
        xp = jnp.pad(xn, ((0, 0), (0, pad_h), (0, pad_w), (0, 0)))
        win = xp.reshape(B, Hp // WS, WS, Wp // WS, WS, D)
        win = win.transpose(0, 1, 3, 2, 4, 5).reshape(-1, WS, WS, D)
        Bn = win.shape[0]
        N = WS * WS
        qkv = win.reshape(Bn, N, D) @ qkv_w + qkv_b
        qkv = qkv.reshape(Bn, N, 3, HEADS, HD).transpose(2, 0, 3, 1, 4)
        qkv = qkv.reshape(3, Bn * HEADS, N, HD)
        q, k, v = (qkv[0], qkv[1], qkv[2])
        scale = HD ** (-0.5)
        attn = jnp.einsum('bqc,bkc->bqk', q * scale, k)
        coords = jnp.arange(WS)[:, None] - jnp.arange(WS)[None, :] + (WS - 1)
        Rh = rel_pos_h[coords]
        Rw = rel_pos_w[coords]
        r_q = q.reshape(-1, WS, WS, HD)
        rel_h = jnp.einsum('bhwc,hkc->bhwk', r_q, Rh)
        rel_w = jnp.einsum('bhwc,wkc->bhwk', r_q, Rw)
        attn = (attn.reshape(-1, WS, WS, WS, WS) + rel_h[:, :, :, :, None] + rel_w[:, :, :, None, :]).reshape(-1, N, N)
        attn = jax.nn.softmax(attn, axis=-1)
        out = jnp.einsum('bqk,bkc->bqc', attn, v)
        out = out.reshape(Bn, HEADS, WS, WS, HD).transpose(0, 2, 3, 1, 4).reshape(Bn, WS, WS, D)
        out = out @ proj_w + proj_b
        out = out.reshape(B, Hp // WS, Wp // WS, WS, WS, D)
        out = out.transpose(0, 1, 3, 2, 4, 5).reshape(B, Hp, Wp, D)[:, :H, :W, :]
        x = shortcut + out
        xn2 = _layer_norm(x, norm2_w, norm2_b)
        h = jax.nn.gelu(xn2 @ fc1_w + fc1_b, approximate=False)
        x = x + (h @ fc2_w + fc2_b)
        return x

    def _L1_conv_ref(x, wq, bq, wk, bk, wv, bv, rel_pos_0, rel_pos_1, wo, bo, ln1_scale, ln1_offset, ln2_scale, ln2_offset, w1, b1, w2, b2):
        import jax, jax.numpy as jnp
        import numpy as np
        B, H, W, C = (8, 16, 16, 192)
        WIN = 16
        NH, HD = (12, 48)

        def _layer_norm(x, scale, offset, eps=1e-05):
            m = jnp.mean(x, axis=-1, keepdims=True)
            v = jnp.var(x, axis=-1, keepdims=True)
            return (x - m) * jax.lax.rsqrt(v + eps) * scale + offset
        b, h, w, c = x.shape
        wh = ww = WIN
        nH, nW = (h // wh, w // ww)
        T = wh * ww
        shortcut = x
        xn = _layer_norm(x, ln1_scale, ln1_offset)
        xw = xn.reshape(b, nH, wh, nW, ww, c).transpose(0, 1, 3, 2, 4, 5)
        xw = xw.reshape(b * nH * nW, T, c)
        q = (xw @ wq + bq).reshape(-1, T, NH, HD)
        k = (xw @ wk + bk).reshape(-1, T, NH, HD)
        v = (xw @ wv + bv).reshape(-1, T, NH, HD)
        logits = jnp.einsum('nthd,nThd->nhtT', q, k) / np.float32(np.sqrt(HD))
        coords = jnp.arange(WIN)[:, None] - jnp.arange(WIN)[None, :] + (WIN - 1)
        Rh = rel_pos_0[coords]
        Rw = rel_pos_1[coords]
        qg = q.reshape(-1, wh, ww, NH, HD)
        bias_h = jnp.einsum('nabhd,akd->nhabk', qg, Rh)
        bias_w = jnp.einsum('nabhd,bkd->nhabk', qg, Rw)
        logits = logits.reshape(-1, NH, wh, ww, wh, ww)
        logits = logits + bias_h[..., :, None] + bias_w[..., None, :]
        logits = logits.reshape(-1, NH, T, T)
        attn = jax.nn.softmax(logits, axis=-1)
        out = jnp.einsum('nhtT,nThd->nthd', attn, v).reshape(-1, T, NH * HD)
        out = out @ wo + bo
        out = out.reshape(b, nH, nW, wh, ww, c).transpose(0, 1, 3, 2, 4, 5)
        out = out.reshape(b, h, w, c)
        x2 = shortcut + out
        mlp_in = _layer_norm(x2, ln2_scale, ln2_offset)
        mlp = jax.nn.gelu(mlp_in @ w1 + b1) @ w2 + b2
        return x2 + mlp

    def _gn(v, G=32, eps=1e-05):
        B_, H_, W_, C_ = v.shape
        g = v.reshape(B_, H_, W_, G, C_ // G)
        m = jnp.mean(g, axis=(1, 2, 4), keepdims=True)
        s = jnp.var(g, axis=(1, 2, 4), keepdims=True)
        return ((g - m) / jnp.sqrt(s + eps)).reshape(v.shape)

    def _ln_c(v, eps=1e-06):
        m = jnp.mean(v, axis=-1, keepdims=True)
        s = jnp.var(v, axis=-1, keepdims=True)
        return (v - m) / jnp.sqrt(s + eps)

    def _ln_t(v, eps=1e-05):
        m = jnp.mean(v, axis=-1, keepdims=True)
        s = jnp.var(v, axis=-1, keepdims=True)
        return (v - m) / jnp.sqrt(s + eps)

    def _to_tokens(v):
        B_, H_, W_, C_ = v.shape
        return v.reshape(B_, H_ * W_, C_)

    def _from_tokens(t, like):
        return t.reshape(like.shape)
    x = _L0_conv_ref(x, L0_conv_qkv_w, L0_conv_qkv_b, L0_conv_proj_w, L0_conv_proj_b, L0_conv_rel_pos_h, L0_conv_rel_pos_w, L0_conv_norm1_w, L0_conv_norm1_b, L0_conv_norm2_w, L0_conv_norm2_b, L0_conv_fc1_w, L0_conv_fc1_b, L0_conv_fc2_w, L0_conv_fc2_b)
    x = _L1_conv_ref(x, L1_conv_wq, L1_conv_bq, L1_conv_wk, L1_conv_bk, L1_conv_wv, L1_conv_bv, L1_conv_rel_pos_0, L1_conv_rel_pos_1, L1_conv_wo, L1_conv_bo, L1_conv_ln1_scale, L1_conv_ln1_offset, L1_conv_ln2_scale, L1_conv_ln2_offset, L1_conv_w1, L1_conv_b1, L1_conv_w2, L1_conv_b2)
    return x

_drawn_inputs = setup_inputs


def setup_inputs(seed=0):
    import zlib

    import numpy as np

    out = dict(_drawn_inputs(seed))
    spreads = {'L0_conv_norm1_w': (1.0, 0.6),
     'L0_conv_norm1_b': (0.0, 0.8),
     'L0_conv_norm2_w': (1.0, 0.6),
     'L0_conv_norm2_b': (0.0, 2.0),
     'L1_conv_bq': (0.0, 0.8),
     'L1_conv_bk': (0.0, 2.0),
     'L1_conv_bv': (0.0, 0.628),
     'L1_conv_bo': (0.0, 0.316),
     'L1_conv_ln1_scale': (1.0, 0.6),
     'L1_conv_ln1_offset': (0.0, 0.58),
     'L1_conv_ln2_scale': (1.0, 0.6),
     'L1_conv_ln2_offset': (0.0, 2.0),
     'L1_conv_b1': (0.0, 0.8),
     'L1_conv_b2': (0.0, 0.306)}
    factors = {'L0_conv_qkv_w': 6.086,
     'L0_conv_qkv_b': 8.0,
     'L0_conv_proj_w': 5.071,
     'L0_conv_proj_b': 10.509,
     'L0_conv_rel_pos_h': 8.0,
     'L0_conv_rel_pos_w': 8.0,
     'L0_conv_fc1_b': 32.664,
     'L0_conv_fc2_b': 9.83,
     'L1_conv_wq': 8.0,
     'L1_conv_wk': 8.0,
     'L1_conv_wv': 3.326,
     'L1_conv_rel_pos_0': 8.0,
     'L1_conv_rel_pos_1': 8.0}
    for name, (base, spread) in spreads.items():
        noise = np.random.default_rng([zlib.crc32(name.encode()), seed]).standard_normal(out[name].shape)
        drawn = base * np.exp(spread * noise) if base else spread * noise
        out[name] = jnp.asarray(drawn.astype(out[name].dtype))
    for name, factor in factors.items():
        out[name] = (out[name] * factor).astype(out[name].dtype)
    return out
```

```python
from contextlib import ExitStack

import numpy as np

import concourse.bass as bass
from concourse import mybir

F32 = mybir.dt.float32
ALU = mybir.AluOpType
ACT = mybir.ActivationFunctionType
AX = mybir.AxisListType

P = 128
B, H, W, C = 8, 16, 16, 192
T = H * W
NT = T // P
CH = C // 2
MLP = 4 * C
NM = MLP // P
EPS = 1e-5
HEADS = 12
WS = 14
D0 = C // HEADS
D1 = 48
GH0 = CH // D0
NPAIR = HEADS // 2
N0 = WS * WS
HT0 = N0 // 2
NREM = T - N0
EDGE = H - WS
RPAD = 64
K0ROWS = D0 + 2 * WS
KR0ROWS = K0ROWS + 3
K1REL = 64
K1ROWS = K1REL + 2 * H
NEG = -1.0e30
L0_UNITS = [("main", 4 * q + j) if s == 0 else ("rem", 2 * q + j)
            for q in range(3) for s, j in ((0, 0), (0, 1), (1, 0), (0, 2), (0, 3), (1, 1))]


class Img:

    def __init__(self, pair, par):
        self.pair, self.par = pair, par

    def at(self, per, k):
        return self.pair * (2 * per) + (self.par * per + k)

    def counts(self, per, k):
        value = self.at(per, k)
        return not isinstance(value, int) or value > 0

    @property
    def parity(self):
        return self.par % 2

    def next(self):
        return Img(self.pair, self.par + 1)

    def prev(self):
        return Img(self.pair, self.par - 1)


def image_loop(eng, step):
    step(Img(0, 0), False, True)
    step(Img(0, 1), True, True)
    with eng.Fori(1, B // 2 - 1) as pair:
        step(Img(pair, 0), True, True)
        step(Img(pair, 1), True, True)
    step(Img(B // 2 - 1, 0), True, True)
    step(Img(B // 2 - 1, 1), True, False)


def build(nc, a, out):
    with ExitStack() as ctx:
        def sb(name, shape, dt=F32):
            return ctx.enter_context(nc.sbuf_tensor(name, shape, dt))

        def sem(name):
            return ctx.enter_context(nc.semaphore(name))

        bank = [ctx.enter_context(nc.psum_tensor(f"bank{i}", [P, 512], F32)) for i in range(8)]
        S_BANK, PT_BANK, O_BANK, Y_BANK, G_BANK = bank[0:2], bank[2:4], bank[4], bank[5], bank[6:8]

        x_all = sb("x_all", [P, B * NT, C])
        x_view = a["x"].rearrange("b (t r) w c -> (r w) (b t) c", t=NT)
        out_view = out.rearrange("b (t r) w c -> (r w) (b t) c", t=NT)
        ident = sb("ident", [P, P])

        wqkv0 = sb("wqkv0", [CH, 2, 3 * C])
        wproj0 = sb("wproj0", [P, 3, C])
        fc1w = [sb(f"fc1w{l}", [CH, 2, MLP]) for l in range(2)]
        fc2w = [sb(f"fc2w{l}", [P, NM, C]) for l in range(2)]
        wq1 = sb("wq1", [CH, 2, HEADS * D1])
        wk1 = sb("wk1", [CH, 2, HEADS * D1])
        wv1 = sb("wv1", [CH, 2, HEADS * D1])
        wo1 = sb("wo1", [P, NPAIR, C])
        lnw = [sb(f"lnw{i}", [CH, 2]) for i in range(4)]
        lnb = [sb(f"lnb{i}", [CH, 2]) for i in range(4)]
        qb0 = sb("qb0", [CH, 2])
        kb0 = sb("kb0", [CH, 2])
        kpad0 = sb("kpad0", [D0, HEADS])
        qb1 = sb("qb1", [CH, NPAIR])
        kb1 = sb("kb1", [CH, NPAIR])
        fc1b = [sb(f"fc1b{l}", [P, NM]) for l in range(2)]
        vb0 = sb("vb0", [P, 3])
        vb1 = sb("vb1", [P, NPAIR])
        obias = [sb(f"obias{l}", [P, C]) for l in range(2)]
        fc2b = [sb(f"fc2b{l}", [P, C]) for l in range(2)]
        relnat = [sb("relnat_h0", [27, GH0, D0]), sb("relnat_w0", [27, GH0, D0]),
                  sb("relnat_h1", [31, 2, D1]), sb("relnat_w1", [31, 2, D1])]
        flip = sb("flip", [31, 31])
        flip27 = sb("flip27", [27, 27])
        reltab = [sb("reltab_h0", [CH, 27]), sb("reltab_w0", [CH, 27]),
                  sb("reltab_h1", [CH, 31]), sb("reltab_w1", [CH, 31])]
        blk0 = sb("blk0", [CH, GH0])
        blk1 = sb("blk1", [CH, 2])
        relw = [sb("relw_h0", [CH, WS, GH0, WS]), sb("relw_w0", [CH, WS, GH0, WS]),
                sb("relw_h1", [CH, H, 2, H]), sb("relw_w1", [CH, W, 2, W])]

        lnst = sb("lnst", [P, NT, 6])
        lnag = sb("lnag", [P, NT, 2])
        lnve = sb("lnve", [P, NT])
        lnrs = sb("lnrs", [P, NT])
        mhalf = sb("mhalf", [P, NT])
        xhat = sb("xhat", [P, NT, C])
        xnT = sb("xnT", [CH, 2, T])
        xbias = sb("xbias", [P, NT, C])

        Q1 = [sb(f"Q_{i}", [K1ROWS, HEADS, T]) for i in range(2)]
        K1 = [sb(f"K_{i}", [K1ROWS, HEADS, T]) for i in range(2)]
        Q0, K0 = Q1, K1
        dense = [sb("dense_q", [CH, NPAIR, T]), sb("dense_k", [CH, NPAIR, T])]
        rel_dense = sb("rel_dense", [P, 3, T])
        QR0 = [sb(f"QR0_{i}", [K1ROWS, HEADS, RPAD]) for i in range(2)]
        KR0 = [sb(f"KR0_{i}", [K1ROWS, HEADS, NREM]) for i in range(2)]
        KP0 = sb("KP0", [K1ROWS, HEADS, N0])
        xr0 = sb("xr0", [CH, 2, NREM])
        xm0 = rel_dense[0:CH].rearrange("p g t -> p (g t)")[:, 0:2 * N0].rearrange("p (c t) -> p c t", c=2)
        V0 = [sb(f"V0_{i}", [HT0, 2, HEADS, 32]) for i in range(2)]
        VR0 = [sb(f"VR0_{i}", [NREM, HEADS, 32]) for i in range(2)]
        area = sb("area", [P, 2 * NT * HEADS * 64 + (8 + NPAIR) * T])
        PTm0 = area[0:HT0, 0:HEADS * 2 * N0].rearrange("p (h k q) -> p h k q", h=HEADS, k=2)
        hT = [area[:, i * NM * T:(i + 1) * NM * T].rearrange("p (m t) -> p m t", m=NM) for i in range(2)]
        V1 = [area[:, i * 1536:(i + 1) * 1536].rearrange("p (t h d) -> p t h d", t=NT, h=HEADS) for i in range(2)]
        PT1 = area[:, 3072:3072 + 8 * T].rearrange("p (b k q) -> p b k q", b=4, k=2)
        AO1 = area[:, 3072 + 8 * T:3072 + (8 + NPAIR) * T].rearrange("p (q t) -> p q t", q=NPAIR)
        PTr0 = area[0:NREM, HEADS * 2 * N0:HEADS * 2 * N0 + NPAIR * P].rearrange("p (h q) -> p h q", h=NPAIR)
        AO0 = area[:, HEADS * 2 * N0 + NPAIR * P:HEADS * 2 * N0 + NPAIR * P + 3 * T].rearrange("p (q t) -> p q t", q=3)

        nmax = sb("nmax", [P, 2, 2])
        esum = sb("esum", [P, 2, 2])
        rsum = sb("rsum", [P, 2, 2])
        Pb = [sb(f"Pb{i}", [P, 2, T]) for i in range(2)]

        ld_x = sem("ld_x")
        ld_w = sem("ld_w")
        zeroed = sem("zeroed")
        ld_c = sem("ld_c")
        prep_pe = sem("prep_pe")
        prep_dve = sem("prep_dve")
        prep_pool = sem("prep_pool")
        out_done = sem("out_done")
        xdone = [sem(f"xdone{i}") for i in range(4)]

        loads = []

        def col(v, n, off=0, p=CH):
            return v[off:off + p * n].rearrange("(c p) -> p c", p=p)

        def bcast(v, n=P):
            return v.partition_broadcast(n)

        loads += [(ident[:], a["c_ident"]), (flip[:], a["c_flip31"]), (flip27[:], a["c_flip27"]),
                  (blk0[:], a["c_blk0"]), (blk1[:], a["c_blk1"])]
        loads += [(wqkv0[:], a["L0_conv_qkv_w"].rearrange("(c p) n -> p c n", p=CH)),
                  (fc1w[0][:], a["L0_conv_fc1_w"].rearrange("(c p) n -> p c n", p=CH)),
                  (fc2w[0][:], a["L0_conv_fc2_w"].rearrange("(m p) n -> p m n", p=P)),
                  (wq1[:], a["L1_conv_wq"].rearrange("(c p) n -> p c n", p=CH)),
                  (wk1[:], a["L1_conv_wk"].rearrange("(c p) n -> p c n", p=CH)),
                  (wv1[:], a["L1_conv_wv"].rearrange("(c p) n -> p c n", p=CH)),
                  (fc1w[1][:], a["L1_conv_w1"].rearrange("(c p) n -> p c n", p=CH)),
                  (fc2w[1][:], a["L1_conv_w2"].rearrange("(m p) n -> p m n", p=P))]
        for i, (w_, b_) in enumerate((("L0_conv_norm1_w", "L0_conv_norm1_b"), ("L0_conv_norm2_w", "L0_conv_norm2_b"),
                                      ("L1_conv_ln1_scale", "L1_conv_ln1_offset"), ("L1_conv_ln2_scale", "L1_conv_ln2_offset"))):
            loads += [(lnw[i][:], col(a[w_], 2)), (lnb[i][:], col(a[b_], 2))]
        qkvb = a["L0_conv_qkv_b"]
        loads += [(qb0[:], col(qkvb, 2)), (kb0[:], col(qkvb, 2, C)),
                  (kpad0[:], qkvb[C:2 * C].rearrange("(h d) -> d h", d=D0)),
                  (qb1[:], col(a["L1_conv_bq"], NPAIR)), (kb1[:], col(a["L1_conv_bk"], NPAIR)),
                  (fc1b[0][:], col(a["L0_conv_fc1_b"], NM, p=P)), (fc1b[1][:], col(a["L1_conv_b1"], NM, p=P)),
                  (obias[0][:], bcast(a["L0_conv_proj_b"])), (obias[1][:], bcast(a["L1_conv_bo"])),
                  (fc2b[0][:], bcast(a["L0_conv_fc2_b"])), (fc2b[1][:], bcast(a["L1_conv_b2"]))]
        for i, (name, n, rep, d) in enumerate((("L0_conv_rel_pos_h", 27, GH0, D0), ("L0_conv_rel_pos_w", 27, GH0, D0),
                                               ("L1_conv_rel_pos_0", 31, 2, D1), ("L1_conv_rel_pos_1", 31, 2, D1))):
            for r in range(rep):
                loads.append((relnat[i][:, r, :], a[name]))

        late = []
        for j in range(4):
            late.append((wproj0[32 * j:32 * j + D0, :, :],
                         a["L0_conv_proj_w"].rearrange("(q j d) n -> j d q n", j=4, d=D0)[j]))
            late.append((vb0[32 * j:32 * j + D0, :], qkvb[2 * C:].rearrange("(q j d) -> j d q", j=4, d=D0)[j]))
        for j in range(2):
            late.append((wo1[64 * j:64 * j + D1, :, :],
                         a["L1_conv_wo"].rearrange("(q j d) n -> j d q n", j=2, d=D1)[j]))
            late.append((vb1[64 * j:64 * j + D1, :], a["L1_conv_bv"].rearrange("(q j d) -> j d q", j=2, d=D1)[j]))
        def per_head(v):
            return v.unsqueeze(1).broadcast_to([v.shape[0], HEADS, v.shape[1]])

        late.append((KP0[D0:KR0ROWS], per_head(a["c_hotpad"])))
        for i in range(2):
            late.append((K1[i][D0:K0ROWS], per_head(a["c_hot0"])))
            late.append((K1[i][K1REL:K1ROWS], per_head(a["c_hot1"])))
            late.append((KR0[i][D0:KR0ROWS], per_head(a["c_hotrem"])))
            late.append((QR0[i][K0ROWS:KR0ROWS], per_head(a["c_qwin"])))

        landed = {e: sem(f"landed_{e}") for e in ("pe", "dve", "pool", "sp")}

        def land(eng, name):
            eng.sem_inc(landed[name], 1)

        class Norm:
            def __init__(self, l, x_before):
                self.l, self.x_before = l, x_before
                self.stats = sem(f"ln_stats{l}")
                self.eps = sem(f"ln_eps{l}")
                self.rstd = sem(f"ln_rstd{l}")
                self.xhat = sem(f"ln_xhat{l}")

            def dve_stats(self, eng, n):
                s, v = self.x_before(n)
                eng.wait_ge(s, v)
                for t in range(NT):
                    nc.vector.bn_stats(lnst[:, t, :], self.x(n, t)).then_inc(self.stats, 1)
                eng.wait_ge(self.stats, n.at(2 * NT, NT))
                land(eng, "dve")
                for t in range(NT):
                    nc.vector.bn_aggr(lnag[:, t, :], lnst[:, t, :]).then_inc(self.stats, 1)

            def x(self, n, t):
                return x_all[:, bass.ds(n.at(NT, t), 1), :].rearrange("p a c -> p (a c)")

            def pool_rstd(self, eng, n):
                eng.wait_ge(self.stats, n.at(2 * NT, 2 * NT))
                land(eng, "pool")
                nc.gpsimd.tensor_scalar(lnve[:], lnag[:, :, 1], EPS, None, ALU.add).then_inc(self.eps, 1)
                eng.wait_ge(self.eps, n.at(1, 1))
                nc.gpsimd.tensor_tensor(lnrs[:], lnve[:], mhalf[:], ALU.pow).then_inc(self.rstd, 1)

            def dve_xhat(self, eng, n, transposed, per, k):
                eng.wait_ge(self.rstd, n.at(1, 1))
                if n.counts(per, k):
                    eng.wait_ge(transposed, n.at(per, k))
                for t in range(NT):
                    nc.vector.tensor_scalar(xhat[:, t, :], self.x(n, t), lnag[:, t, 0:1], lnrs[:, t:t + 1],
                                            ALU.subtract, ALU.mult).then_inc(self.xhat, 1)

        class Mlp:
            def __init__(self, l, func, x_sem, done, last):
                self.l, self.func, self.done, self.last = l, func, done, last
                self.norm = Norm(2 * l + 1, lambda n: (x_sem, n.at(1, 1)))
                self.xt = [sem(f"m{l}_xt{c}") for c in range(2)]
                self.xn = [sem(f"m{l}_xn{c}") for c in range(2)]
                self.h = sem(f"m{l}_h")
                self.g = sem(f"m{l}_g")
                self.y = sem(f"m{l}_y")
                self.xb = sem(f"m{l}_xb")
                self.hbank = [S_BANK[0], S_BANK[1], PT_BANK[0], PT_BANK[1]]

            def pe_front(self, eng, n):
                for c in range(2):
                    if n.counts(1, 0):
                        eng.wait_ge(self.xn[c], n.at(1, 0))
                    for t in range(NT):
                        eng.wait_ge(self.norm.xhat, n.at(NT, t + 1))
                        mm = nc.tensor.transpose(G_BANK[c][0:CH, t * P:(t + 1) * P],
                                                 xhat[:, t, c * CH:(c + 1) * CH], ident[:])
                    mm.then_inc(self.xt[c], 1)
                for c in range(2):
                    eng.wait_ge(self.xn[c], n.at(1, 1))
                for m in range(NM):
                    if n.counts(NM, m - 3):
                        eng.wait_ge(self.g, n.at(NM, m - 3))
                    for c in range(2):
                        mm = nc.tensor.matmul(self.hbank[(n.parity * NM + m) % 4][:, 0:T],
                                              fc1w[self.l][:, c, m * P:(m + 1) * P], xnT[:, c, :],
                                              start=(c == 0), stop=(c == 1))
                    mm.then_inc(self.h, 1)

            def act_front(self, eng, n):
                eng.wait_ge(self.xt[0], n.at(1, 1))
                if n.counts(NM, 0):
                    eng.wait_ge(self.h, n.at(NM, 0))
                nc.scalar.activation(xnT[:, 0, :], G_BANK[0][0:CH, 0:T], ACT.Identity,
                                     scale=lnw[2 * self.l + 1][:, 0:1], bias=lnb[2 * self.l + 1][:, 0:1]).then_inc(self.xn[0], 1)
                for m in range(NM):
                    eng.wait_ge(self.h, n.at(NM, m + 1))
                    if n.counts(1, -1):
                        eng.wait_ge(self.y, n.at(1, -1))
                    nc.scalar.activation(hT[n.parity][:, m, :], self.hbank[(n.parity * NM + m) % 4][:, 0:T],
                                         self.func, bias=fc1b[self.l][:, m:m + 1]).then_inc(self.g, 1)

            def dve_front(self, eng, n):
                self.norm.dve_stats(eng, n)
                self.norm.dve_xhat(eng, n, self.xt[1], 1, 0)
                eng.wait_ge(self.xt[1], n.at(1, 1))
                if n.counts(NM, 0):
                    eng.wait_ge(self.h, n.at(NM, 0))
                nc.vector.tensor_scalar(xnT[:, 1, :], G_BANK[1][0:CH, 0:T], lnw[2 * self.l + 1][:, 1:2],
                                        lnb[2 * self.l + 1][:, 1:2], ALU.mult, ALU.add).then_inc(self.xn[1], 1)

            def pe_back(self, eng, n):
                ybank = (O_BANK, Y_BANK)[n.parity]
                eng.wait_ge(self.g, n.at(NM, NM))
                if n.counts(1, -1):
                    eng.wait_ge(self.done, n.at(1, -1))
                for t in range(NT):
                    for m in range(NM):
                        mm = nc.tensor.matmul(ybank[:, t * C:(t + 1) * C], hT[n.parity][:, m, t * P:(t + 1) * P],
                                              fc2w[self.l][:, m, :], start=(m == 0), stop=(m == NM - 1))
                mm.then_inc(self.y, 1)

            def pool_back(self, eng, n):
                s, v = self.norm.x_before(n)
                eng.wait_ge(s, v)
                if n.counts(1, 0):
                    eng.wait_ge(self.done, n.at(1, 0))
                nc.gpsimd.tensor_tensor(xbias[:], x_all[:, bass.ds(n.at(NT, 0), NT), :],
                                        fc2b[self.l][:].unsqueeze(1).broadcast_to([P, NT, C]),
                                        ALU.add).then_inc(self.xb, 1)

            def dve_back(self, eng, n):
                ybank = (O_BANK, Y_BANK)[n.parity]
                eng.wait_ge(self.y, n.at(1, 1))
                eng.wait_ge(self.xb, n.at(1, 1))
                nc.vector.tensor_tensor(x_all[:, bass.ds(n.at(NT, 0), NT), :],
                                        ybank[:, 0:NT * C].rearrange("p (t c) -> p t c", t=NT), xbias[:],
                                        ALU.add).then_inc(self.done, 1)

            def run(self, eng, which):
                front, back = {"pe": (self.pe_front, self.pe_back), "act": (self.act_front, None),
                               "dve": (self.dve_front, self.dve_back)}[which]
                front(eng, Img(0, 0))

                def step(n, has_prev, has_next):
                    if has_next:
                        front(eng, n.next())
                    if back:
                        back(eng, n)
                image_loop(eng, step)

            def run_pool(self, eng):
                self.norm.pool_rstd(eng, Img(0, 0))

                def step(n, has_prev, has_next):
                    if has_next:
                        self.norm.pool_rstd(eng, n.next())
                    self.pool_back(eng, n)
                image_loop(eng, step)

        class Attention:

            def __init__(self, l, x_before, done, units, pv_after):
                self.l, self.done, self.units = l, done, units
                self.norm = Norm(2 * l, x_before)
                self.NU = len(units)
                self.pv_after = pv_after
                tiles = [len(self.tiles(u)) for u in range(self.NU)]
                self.cum = [sum(tiles[:u]) for u in range(self.NU + 1)]
                self.NTL = self.cum[-1]
                s = f"a{l}_"
                self.s_rdy = sem(s + "scores")
                self.m_rdy = sem(s + "max")
                self.e_rdy = sem(s + "exp")
                self.r_rdy = sem(s + "rsum")
                self.p_rdy = sem(s + "probs")
                self.t_rdy = sem(s + "probsT")
                self.pt = [sem(s + "ptA"), sem(s + "ptB")]
                self.pv = sem(s + "values")
                self.ao = [sem(s + "aoA"), sem(s + "aoB")]
                self.y = sem(s + "proj")
                self.xb = sem(s + "xbias")
                self.g_rdy = [sem(s + "g0"), sem(s + "g1")]
                self.g_out = [sem(s + "g0out"), sem(s + "g1out")]
                self.scat = sem(s + "scatter")
                self.relscat = sem(s + "relscat")

            def pe_scores(self, eng, n, u):
                if n.counts(self.NTL, self.cum[u - 1] if u >= 1 else self.cum[self.NU - 1] - self.NTL):
                    eng.wait_ge(self.e_rdy, n.at(self.NTL, self.cum[u - 1] if u >= 1 else self.cum[self.NU - 1] - self.NTL))
                self.emit_scores(eng, n, u).then_inc(self.s_rdy, 1)

            def score_tiles(self, u):
                rows, cols, k = self.tiles(u)[0][0], self.tiles(u)[0][1], len(self.tiles(u))
                return S_BANK[u % 2][0:rows, 0:k * cols].rearrange("p (t c) -> p t c", t=k)

            def dve_max(self, eng, n, u):
                eng.wait_ge(self.s_rdy, n.at(self.NU, u + 1))
                sc = self.score_tiles(u)
                nc.vector.tensor_reduce(nmax[0:sc.shape[0], u % 2, 0:sc.shape[1]], sc, AX.X, ALU.max,
                                        negate=True).then_inc(self.m_rdy, 1)

            def act_exp(self, eng, n, u):
                eng.wait_ge(self.m_rdy, n.at(self.NU, u + 1))
                if n.counts(self.NU, u - 1):
                    eng.wait_ge(self.t_rdy, n.at(self.NU, u - 1))
                sc = self.score_tiles(u)
                rows, k, cols = sc.shape
                for t in range(k):
                    nc.scalar.activation(Pb[u % 2][0:rows, t, 0:cols], sc[:, t, :], ACT.Exp,
                                         bias=nmax[0:rows, u % 2, t:t + 1],
                                         accum_out=esum[0:rows, u % 2, t:t + 1]).then_inc(self.e_rdy, 1)

            def dve_norm(self, eng, n, u):
                rows, _, keep = self.tiles(u)[0]
                k = len(self.tiles(u))
                eng.wait_ge(self.e_rdy, n.at(self.NTL, self.cum[u + 1]))
                nc.vector.reciprocal(rsum[0:rows, u % 2, 0:k], esum[0:rows, u % 2, 0:k]).then_inc(self.r_rdy, 1)
                eng.wait_ge(self.r_rdy, n.at(self.NU, u + 1))
                for t in range(k):
                    nc.vector.tensor_scalar(Pb[u % 2][0:rows, t, 0:keep], Pb[u % 2][0:rows, t, 0:keep],
                                            rsum[0:rows, u % 2, t:t + 1], None, ALU.mult).then_inc(self.p_rdy, 1)

            def pe_probsT(self, eng, n, u):
                eng.wait_ge(self.p_rdy, n.at(self.NTL, self.cum[u + 1]))
                if n.counts(self.NU // 2, u // 2):
                    eng.wait_ge(self.pt[u % 2], n.at(self.NU // 2, u // 2))
                if len(self.tiles(u)) == 1:
                    land(eng, "pe")
                self.emit_probsT(eng, n, u).then_inc(self.t_rdy, 1)

            def pt_out(self, eng, n, u, copy):
                eng.wait_ge(self.t_rdy, n.at(self.NU, u + 1))
                per, k = self.pt_free(u)
                if n.counts(per, k):
                    eng.wait_ge(self.pv, n.at(per, k))
                copy(*self.pt_views(u)).then_inc(self.pt[u % 2], 1)

            def g_free(self, eng, n, b, outs_before):
                if n.counts(self.G_OUTS[b], outs_before):
                    eng.wait_ge(self.g_out[b], n.at(self.G_OUTS[b], outs_before))

            def pe_transpose_x(self, eng, n):
                for c in range(2):
                    self.g_free(eng, n, c, 0)
                    for t in range(NT):
                        eng.wait_ge(self.norm.xhat, n.at(NT, t + 1))
                        mm = nc.tensor.transpose(G_BANK[c][0:CH, t * P:(t + 1) * P],
                                                 xhat[:, t, c * CH:(c + 1) * CH], ident[:])
                    mm.then_inc(self.g_rdy[c], 1)

            def act_xn(self, eng, n):
                eng.wait_ge(self.g_rdy[0], n.at(self.G_USES[0], 1))
                for b in range(2):
                    if n.counts(self.G_USES[b], 0):
                        eng.wait_ge(self.g_rdy[b], n.at(self.G_USES[b], 0))
                nc.scalar.activation(xnT[:, 0, :], G_BANK[0][0:CH, 0:T], ACT.Identity,
                                     scale=lnw[2 * self.l][:, 0:1], bias=lnb[2 * self.l][:, 0:1]).then_inc(self.g_out[0], 1)

            def dve_xn(self, eng, n):
                eng.wait_ge(self.g_rdy[1], n.at(self.G_USES[1], 1))
                for b in range(2):
                    if n.counts(self.G_USES[b], 0):
                        eng.wait_ge(self.g_rdy[b], n.at(self.G_USES[b], 0))
                nc.vector.tensor_scalar(xnT[:, 1, :], G_BANK[1][0:CH, 0:T], lnw[2 * self.l][:, 1:2],
                                        lnb[2 * self.l][:, 1:2], ALU.mult, ALU.add).then_inc(self.g_out[1], 1)

            def xn_ready(self, eng, n):
                for b in range(2):
                    eng.wait_ge(self.g_out[b], n.at(self.G_OUTS[b], 1))

            def pool_xbias(self, eng, n):
                s, v = self.norm.x_before(n)
                eng.wait_ge(s, v)
                if n.counts(1, 0):
                    eng.wait_ge(self.done, n.at(1, 0))
                nc.gpsimd.tensor_tensor(xbias[:], x_all[:, bass.ds(n.at(NT, 0), NT), :],
                                        obias[self.l][:].unsqueeze(1).broadcast_to([P, NT, C]),
                                        ALU.add).then_inc(self.xb, 1)

            def dve_back(self, eng, n):
                eng.wait_ge(self.y, n.at(1, 1))
                eng.wait_ge(self.xb, n.at(1, 1))
                nc.vector.tensor_tensor(x_all[:, bass.ds(n.at(NT, 0), NT), :],
                                        Y_BANK[:, 0:NT * C].rearrange("p (t c) -> p t c", t=NT), xbias[:],
                                        ALU.add).then_inc(self.done, 1)

            def run(self, eng, which):
                fronts = {"pe": self.pe_fronts, "act": self.act_fronts, "dve": self.dve_fronts}[which]
                slot = {"pe": self.pe_slot, "act": self.act_slot, "dve": self.dve_slot}[which]
                for k in sorted(fronts):
                    for f in fronts[k]:
                        f(eng, Img(0, 0))
                if which == "pe":
                    self.pe_scores(eng, Img(0, 0), 0)
                    self.pe_scores(eng, Img(0, 0), 1)
                elif which == "act":
                    self.act_exp(eng, Img(0, 0), 0)
                else:
                    self.dve_max(eng, Img(0, 0), 0)
                    self.dve_max(eng, Img(0, 0), 1)
                    self.dve_norm(eng, Img(0, 0), 0)

                def step(n, has_prev, has_next):
                    def ahead(u, k):
                        if u + k < self.NU:
                            return n, u + k
                        return (n.next(), u + k - self.NU) if has_next else None
                    for u in range(self.NU):
                        slot(eng, n, u, has_prev, ahead(u, 1), ahead(u, 2))
                        if has_next:
                            for f in fronts.get(u, ()):
                                f(eng, n.next())
                    if not has_next:
                        last = len(self.pv_after) - 1
                        if which == "pe":
                            self.pe_values(eng, n, last)
                            self.pe_back(eng, n)
                        elif which == "act":
                            self.act_ao(eng, n, last)
                        else:
                            self.dve_ao(eng, n, last)
                            self.dve_back(eng, n)
                image_loop(eng, step)

            def groups_at(self, n, u, has_prev):
                if u == 0:
                    return [(n.prev(), len(self.pv_after) - 1)] if has_prev else []
                return [(n, g) for g in self.pv_after.get(u - 1, ())]

            def pe_slot(self, eng, n, u, has_prev, one, two):
                self.pe_probsT(eng, n, u)
                if two:
                    self.pe_scores(eng, *two)
                for m, g in self.groups_at(n, u, has_prev):
                    self.pe_values(eng, m, g)
                if u == 1 and has_prev:
                    self.pe_back(eng, n.prev())

            def act_slot(self, eng, n, u, has_prev, one, two):
                if one:
                    self.act_exp(eng, *one)
                if u % 2 == 0:
                    self.pt_out(eng, n, u, nc.scalar.copy)
                for m, g in self.groups_at(n, u, has_prev):
                    self.act_ao(eng, m, g)

            def dve_slot(self, eng, n, u, has_prev, one, two):
                if u % 2 == 1:
                    self.pt_out(eng, n, u, nc.vector.tensor_copy)
                if one:
                    self.dve_norm(eng, *one)
                if two:
                    self.dve_max(eng, *two)
                for m, g in self.groups_at(n, u, has_prev):
                    self.dve_ao(eng, m, g)
                if u == 1 and has_prev:
                    self.dve_back(eng, n.prev())

            def run_pool(self, eng):
                def front(n):
                    self.norm.pool_rstd(eng, n)
                    self.pool_front(eng, n)
                front(Img(0, 0))

                def step(n, has_prev, has_next):
                    if has_next:
                        front(n.next())
                    self.pool_xbias(eng, n)
                image_loop(eng, step)

        class Attention0(Attention):
            G_USES = (6, 5)
            G_OUTS = (6, 5)

            def tiles(self, u):
                return [(P, N0, N0)] * 2 if self.units[u][0] == "main" else [(P, NREM + N0, NREM)]

            def emit_scores(self, eng, n, u):
                kind, h = self.units[u]
                p = n.parity
                if u == 0:
                    eng.wait_ge(self.scat, n.at(16 * 2 * GH0, 16 * 2 * GH0))
                    eng.wait_ge(self.relscat, n.at(16 * 2 * GH0, 16 * 2 * GH0))
                if kind == "main":
                    k = K0[p][:, h, :].rearrange("k (r c) -> k r c", c=W)[:, 0:WS, 0:WS]
                    for t in range(2):
                        mm = nc.tensor.matmul(S_BANK[u % 2][:, t * N0:(t + 1) * N0],
                                              Q0[p][:, h, t * P:(t + 1) * P], k, start=True, stop=True)
                    return mm
                eng.wait_ge(self.gath, n.at(6, 6))
                land(eng, "pe")
                for j in range(2):
                    for keys, lo, hi in ((KR0[p], 0, NREM), (KP0, NREM, NREM + N0)):
                        mm = nc.tensor.matmul(S_BANK[u % 2][RPAD * j:RPAD * (j + 1), lo:hi],
                                              QR0[p][:, 2 * h + j, :], keys[:, 2 * h + j, :], start=True, stop=True)
                return mm

            def emit_probsT(self, eng, n, u):
                kind, h = self.units[u]
                pb, ptb = Pb[u % 2], PT_BANK[u % 2]
                if kind == "main":
                    for kc in range(2):
                        for t in range(2):
                            mm = nc.tensor.transpose(ptb[0:HT0, kc * T + t * P:kc * T + (t + 1) * P],
                                                     pb[:, t, kc * HT0:(kc + 1) * HT0], ident[:])
                    return mm
                return nc.tensor.transpose(ptb[0:NREM, 0:P], pb[:, 0, 0:NREM], ident[:])

            def pt_views(self, u):
                kind, h = self.units[u]
                if kind == "main":
                    return (PTm0[:, h, :, :].rearrange("p k (r c) -> p k r c", c=WS),
                            PT_BANK[u % 2][0:HT0, :].rearrange("p (k r c) -> p k r c", k=2, c=W)[:, :, 0:WS, 0:WS])
                return PTr0[:, h, :], PT_BANK[u % 2][0:NREM, 0:P]

            def pt_free(self, u):
                return 3, u // 6 - 2

            def pe_values(self, eng, n, q):
                p = n.parity
                for s in self.pt:
                    eng.wait_ge(s, n.at(self.NU // 2, 3 * q + 3))
                if n.counts(9, 3 * q):
                    eng.wait_ge(self.ao[0], n.at(9, 3 * q))
                if n.counts(3, q):
                    eng.wait_ge(self.ao[1], n.at(3, q))
                for kc in range(2):
                    for j in range(4):
                        nc.tensor.matmul(O_BANK[32 * j:32 * j + 32, 0:N0], V0[p][:, kc, 4 * q + j, :],
                                         PTm0[:, 4 * q + j, kc, :], start=(kc == 0), stop=(kc == 1))
                for j in range(4):
                    mm = nc.tensor.matmul(O_BANK[32 * j:32 * j + 32, N0:T], VR0[p][:, 4 * q + j, :],
                                          PTr0[:, 2 * q + j // 2, RPAD * (j % 2):RPAD * (j % 2) + NREM],
                                          start=True, stop=True)
                mm.then_inc(self.pv, 1)

            def ao_view(self, q):
                return AO0[:, q, :].rearrange("p (r c) -> p r c", c=W)

            def act_ao(self, eng, n, q):
                eng.wait_ge(self.pv, n.at(3, q + 1))
                if n.counts(1, 0):
                    eng.wait_ge(self.y, n.at(1, 0))
                ao = self.ao_view(q)
                e = EDGE * WS
                parts = ((ao[:, 0:WS, WS:W], N0, e), (ao[:, WS:H, 0:WS], N0 + e, e),
                         (ao[:, WS:H, WS:W], N0 + 2 * e, EDGE * EDGE))
                for dst, at, k in parts:
                    nc.scalar.copy(dst, O_BANK[:, at:at + k].rearrange("p (r c) -> p r c", c=dst.shape[2]))\
                      .then_inc(self.ao[0], 1)

            def dve_ao(self, eng, n, q):
                eng.wait_ge(self.pv, n.at(3, q + 1))
                eng.wait_ge(self.ao[0], n.at(9, 3 * q + 3))
                if n.counts(1, 0):
                    eng.wait_ge(self.y, n.at(1, 0))
                nc.vector.tensor_copy(self.ao_view(q)[:, 0:WS, 0:WS],
                                      O_BANK[:, 0:N0].rearrange("p (r c) -> p r c", c=WS)).then_inc(self.ao[1], 1)

            def pe_back(self, eng, n):
                eng.wait_ge(self.ao[0], n.at(9, 9))
                eng.wait_ge(self.ao[1], n.at(3, 3))
                if n.counts(1, 0):
                    eng.wait_ge(self.done, n.at(1, 0))
                for t in range(NT):
                    for q in range(3):
                        mm = nc.tensor.matmul(Y_BANK[:, t * C:(t + 1) * C], AO0[:, q, t * P:(t + 1) * P],
                                              wproj0[:, q, :], start=(q == 0), stop=(q == 2))
                mm.then_inc(self.y, 1)

            def xn_views(self, c):
                return (xm0[:, c, :].rearrange("p (r c) -> p r c", c=WS),
                        G_BANK[c][0:CH, 0:T].rearrange("p (r c) -> p r c", c=W)[:, 0:WS, 0:WS])

            def act_xn(self, eng, n):
                eng.wait_ge(self.g_rdy[0], n.at(6, 1))
                for b in range(2):
                    if n.counts(self.G_USES[b], 0):
                        eng.wait_ge(self.g_rdy[b], n.at(self.G_USES[b], 0))
                nc.scalar.activation(*self.xn_views(0), ACT.Identity, scale=lnw[0][:, 0:1],
                                     bias=lnb[0][:, 0:1]).then_inc(self.xmain[0], 1)
                super().act_xn(eng, n)

            def dve_xn(self, eng, n):
                eng.wait_ge(self.g_rdy[1], n.at(5, 1))
                for b in range(2):
                    if n.counts(self.G_USES[b], 0):
                        eng.wait_ge(self.g_rdy[b], n.at(self.G_USES[b], 0))
                nc.vector.tensor_scalar(*self.xn_views(1), lnw[0][:, 1:2], lnb[0][:, 1:2],
                                        ALU.mult, ALU.add).then_inc(self.xmain[1], 1)
                super().dve_xn(eng, n)

            def pe_qk(self, eng, n, g):
                self.xn_ready(eng, n)
                for b in range(2):
                    self.g_free(eng, n, b, 1 + g)
                    for c in range(2):
                        mm = nc.tensor.matmul(G_BANK[b][0:CH, 0:T], wqkv0[:, c, b * C + g * CH:b * C + (g + 1) * CH],
                                              xnT[:, c, :], start=(c == 0), stop=(c == 1))
                    mm.then_inc(self.g_rdy[b], 1)

            def act_q(self, eng, n, g):
                eng.wait_ge(self.g_rdy[0], n.at(6, 2 + g))
                if g == 0:
                    if n.counts(16 * 2 * GH0, 0):
                        eng.wait_ge(self.scat, n.at(16 * 2 * GH0, 0))
                    if n.counts(6, 0):
                        eng.wait_ge(self.g_rdy[0], n.at(6, 0))
                nc.scalar.activation(self.qd[:, g, :], G_BANK[0][0:CH, 0:T], ACT.Identity,
                                     bias=qb0[:, g:g + 1]).then_inc(self.g_out[0], 1)

            def dve_k(self, eng, n, g):
                eng.wait_ge(self.g_rdy[1], n.at(5, 2 + g))
                if g == 0:
                    if n.counts(16 * 2 * GH0, 0):
                        eng.wait_ge(self.scat, n.at(16 * 2 * GH0, 0))
                nc.vector.tensor_scalar(self.kd[:, g, :], G_BANK[1][0:CH, 0:T], kb0[:, g:g + 1], D0 ** -0.5,
                                        ALU.add, ALU.mult).then_inc(self.g_out[1], 1)

            def pe_v(self, eng, n):
                for t in range(2):
                    self.g_free(eng, n, t, 4)
                    for c in range(2):
                        eng.wait_ge(self.xmain[c], n.at(1, 1))
                        mm = nc.tensor.matmul(G_BANK[t][0:HT0, 0:C], xm0[:, c, t * HT0:(t + 1) * HT0],
                                              wqkv0[:, c, 2 * C:3 * C], start=(c == 0), stop=(c == 1))
                    mm.then_inc(self.g_rdy[t], 1)
                self.g_free(eng, n, 0, 5)
                eng.wait_ge(self.xgath, n.at(3, 3))
                for c in range(2):
                    mm = nc.tensor.matmul(G_BANK[0][0:NREM, 0:C], xr0[:, c, :], wqkv0[:, c, 2 * C:3 * C],
                                          start=(c == 0), stop=(c == 1))
                mm.then_inc(self.g_rdy[0], 1)

            def act_v(self, eng, n):
                eng.wait_ge(self.g_rdy[0], n.at(6, 5))
                if n.counts(3, -3):
                    eng.wait_ge(self.pv, n.at(3, -3))
                nc.scalar.copy(V0[n.parity][:, 0, :, 0:D0], G_BANK[0][0:HT0, 0:C].rearrange("p (h d) -> p h d", d=D0))\
                  .then_inc(self.g_out[0], 1)
                eng.wait_ge(self.g_rdy[0], n.at(6, 6))
                nc.scalar.copy(VR0[n.parity][:, :, 0:D0], G_BANK[0][0:NREM, 0:C].rearrange("p (h d) -> p h d", d=D0))\
                  .then_inc(self.g_out[0], 1)

            def dve_v(self, eng, n):
                eng.wait_ge(self.g_rdy[1], n.at(5, 5))
                if n.counts(3, -3):
                    eng.wait_ge(self.pv, n.at(3, -3))
                nc.vector.tensor_copy(V0[n.parity][:, 1, :, 0:D0],
                                      G_BANK[1][0:HT0, 0:C].rearrange("p (h d) -> p h d", d=D0))\
                  .then_inc(self.g_out[1], 1)

            def pe_rel(self, eng, n):
                eng.wait_ge(self.g_out[0], n.at(6, 3))
                m = GH0 * WS
                for b, (tab, line) in ((1, (relw[0], lambda v, i: v[:, :, i, :])), (0, (relw[1], lambda v, i: v[:, :, :, i]))):
                    self.g_free(eng, n, b, 3)
                    qv = self.qd[:, :, :].rearrange("k g (r c) -> k g r c", c=W)
                    for i in range(H):
                        mm = nc.tensor.matmul(G_BANK[b][0:m, 32 * i:32 * i + 32],
                                              tab[:, i % WS, :, :].rearrange("k h w -> k (h w)"), line(qv, i),
                                              start=True, stop=True)
                    mm.then_inc(self.g_rdy[b], 1)

            def dve_rel(self, eng, n):
                eng.wait_ge(self.g_rdy[1], n.at(5, 4))
                if n.counts(16 * 2 * GH0, 0):
                    eng.wait_ge(self.relscat, n.at(16 * 2 * GH0, 0))
                m = GH0 * WS
                nc.vector.tensor_copy(self.reld[0].rearrange("p g (r c) -> p g r c", c=W),
                                      G_BANK[1][0:m, :].rearrange("p (r g c) -> p g r c", g=2, c=W)).then_inc(self.g_out[1], 1)

            def act_rel(self, eng, n):
                eng.wait_ge(self.g_rdy[0], n.at(6, 4))
                if n.counts(16 * 2 * GH0, 0):
                    eng.wait_ge(self.relscat, n.at(16 * 2 * GH0, 0))
                m = GH0 * WS
                nc.scalar.copy(self.reld[1].rearrange("p g (r c) -> p g r c", c=W),
                               G_BANK[0][0:m, :].rearrange("p (c g r) -> p g r c", g=2, r=H)).then_inc(self.g_out[0], 1)

            def sp(self, eng):
                def image(n):
                    p = n.parity
                    eng.wait_ge(self.g_out[0], n.at(6, 3))
                    land(eng, "sp")
                    eng.wait_ge(self.g_out[1], n.at(5, 3))
                    land(eng, "sp")
                    if n.counts(self.NU, -self.NU):
                        eng.wait_ge(self.s_rdy, n.at(self.NU, -self.NU))
                    land(eng, "sp")
                    if n.counts(6, -6):
                        eng.wait_ge(self.gath, n.at(6, -6))
                    land(eng, "sp")
                    for h in range(GH0):
                        for src, dst in ((self.qd, Q0), (self.kd, K0)):
                            eng.dma_start(dst[p][0:D0, h:HEADS:GH0, :], src[h * D0:(h + 1) * D0, :, :]).then_inc(self.scat, 16)
                    eng.wait_ge(self.g_out[1], n.at(5, 4))
                    land(eng, "sp")
                    eng.wait_ge(self.g_out[0], n.at(6, 4))
                    land(eng, "sp")
                    for h in range(GH0):
                        for i in range(2):
                            eng.dma_start(Q0[p][D0 + i * WS:D0 + (i + 1) * WS, h:HEADS:GH0, :],
                                          self.reld[i][h * WS:(h + 1) * WS, :, :]).then_inc(self.relscat, 16)
                image(Img(0, 0))
                image(Img(0, 1))
                with eng.Fori(1, B // 2) as pair:
                    image(Img(pair, 0))
                    image(Img(pair, 1))

            def pool_front(self, eng, n):
                p, e = n.parity, EDGE * WS
                self.xn_ready(eng, n)
                if n.counts(6, 0):
                    eng.wait_ge(self.g_rdy[0], n.at(6, 0))
                land(eng, "pool")
                cuts = ((0, e, slice(0, WS), slice(WS, W)), (e, 2 * e, slice(WS, H), slice(0, WS)),
                        (2 * e, NREM, slice(WS, H), slice(WS, W)))

                def gather(dst, src, semaphore):
                    v = src.rearrange("p h (r c) -> p h r c", c=W)
                    for lo, hi, r, c in cuts:
                        nc.gpsimd.tensor_copy(dst[:, :, lo:hi].rearrange("p h (r c) -> p h r c", c=c.stop - c.start),
                                              v[:, :, r, c]).then_inc(semaphore, 1)
                gather(xr0[:, :, :], xnT[:, :, :], self.xgath)
                eng.wait_ge(self.scat, n.at(16 * 2 * GH0, 16 * 2 * GH0))
                if n.counts(self.NU, -self.NU):
                    eng.wait_ge(self.s_rdy, n.at(self.NU, -self.NU))
                land(eng, "pool")
                gather(KR0[p][0:D0], K0[p][0:D0], self.gath)
                eng.wait_ge(self.relscat, n.at(16 * 2 * GH0, 16 * 2 * GH0))
                land(eng, "pool")
                gather(QR0[p][0:K0ROWS], Q0[p][0:K0ROWS], self.gath)

            def setup(self):
                self.qd, self.kd = dense[0][:, 0:2, :], dense[1][:, 0:2, :]
                self.reld = [dense[i][0:GH0 * WS, 2:4, :] for i in range(2)]
                self.gath = sem("a0_gather")
                self.xmain = [sem("a0_xm0"), sem("a0_xm1")]
                self.xgath = sem("a0_xgather")
                ln = lambda e, n: self.norm.dve_stats(e, n)
                xh = lambda e, n: self.norm.dve_xhat(e, n, self.g_rdy[1], 5, -4)
                q = [lambda e, n, g=g: self.pe_qk(e, n, g) for g in range(2)]
                self.pe_fronts = {2: [self.pe_transpose_x], 4: [q[0]], 5: [q[1]], 6: [self.pe_rel], 9: [self.pe_v]}
                self.act_fronts = {2: [self.act_xn], 4: [lambda e, n: self.act_q(e, n, 0)],
                                   5: [lambda e, n: self.act_q(e, n, 1)], 7: [self.act_rel], 9: [self.act_v]}
                self.dve_fronts = {0: [ln], 1: [xh], 2: [self.dve_xn], 4: [lambda e, n: self.dve_k(e, n, 0)],
                                   5: [lambda e, n: self.dve_k(e, n, 1)], 7: [self.dve_rel], 9: [self.dve_v]}

        class Attention1(Attention):
            G_USES = (10, 10)
            G_OUTS = (11, 11)

            def tiles(self, u):
                return [(P, T, T)] * 2

            def emit_scores(self, eng, n, u):
                p = n.parity
                if u == 0:
                    eng.wait_ge(self.scat, n.at(64, 64))
                    eng.wait_ge(self.relscat, n.at(128, 128))
                for t in range(NT):
                    mm = nc.tensor.matmul(S_BANK[u % 2][:, t * T:(t + 1) * T], Q1[p][:, u, t * P:(t + 1) * P],
                                          K1[p][:, u, :], start=True, stop=True)
                return mm

            def emit_probsT(self, eng, n, u):
                for kc in range(2):
                    for t in range(NT):
                        mm = nc.tensor.transpose(PT_BANK[u % 2][:, kc * T + t * P:kc * T + (t + 1) * P],
                                                 Pb[u % 2][:, t, kc * P:(kc + 1) * P], ident[:])
                return mm

            def pt_views(self, u):
                return PT1[:, u % 4, :, :].rearrange("p k q -> p (k q)"), PT_BANK[u % 2][:, 0:2 * T]

            def pt_free(self, u):
                return NPAIR, u // 2 - 1

            def pe_values(self, eng, n, q):
                p = n.parity
                for s in self.pt:
                    eng.wait_ge(s, n.at(self.NU // 2, q + 1))
                if n.counts(NPAIR, q):
                    eng.wait_ge(self.ao[0], n.at(NPAIR, q))
                for kc in range(2):
                    for j in range(2):
                        mm = nc.tensor.matmul(O_BANK[64 * j:64 * j + 64, 0:T], V1[p][:, kc, 2 * q + j, :],
                                              PT1[:, (2 * q + j) % 4, kc, :], start=(kc == 0), stop=(kc == 1))
                mm.then_inc(self.pv, 1)

            def act_ao(self, eng, n, q):
                eng.wait_ge(self.pv, n.at(NPAIR, q + 1))
                if n.counts(1, 0):
                    eng.wait_ge(self.y, n.at(1, 0))
                nc.scalar.copy(AO1[:, q, :], O_BANK[:, 0:T]).then_inc(self.ao[0], 1)

            def dve_ao(self, eng, n, q):
                pass

            def pe_back(self, eng, n):
                eng.wait_ge(self.ao[0], n.at(NPAIR, NPAIR))
                if n.counts(1, 0):
                    eng.wait_ge(self.done, n.at(1, 0))
                for t in range(NT):
                    for q in range(NPAIR):
                        mm = nc.tensor.matmul(Y_BANK[:, t * C:(t + 1) * C], AO1[:, q, t * P:(t + 1) * P],
                                              wo1[:, q, :], start=(q == 0), stop=(q == NPAIR - 1))
                mm.then_inc(self.y, 1)

            def pe_qk(self, eng, n, g):
                self.xn_ready(eng, n)
                for b, w in enumerate((wq1, wk1)):
                    self.g_free(eng, n, b, 1 + g)
                    for c in range(2):
                        mm = nc.tensor.matmul(G_BANK[b][0:CH, 0:T], w[:, c, g * CH:(g + 1) * CH], xnT[:, c, :],
                                              start=(c == 0), stop=(c == 1))
                    mm.then_inc(self.g_rdy[b], 1)

            def act_q(self, eng, n, g):
                eng.wait_ge(self.g_rdy[0], n.at(10, 2 + g))
                if g == 0:
                    if n.counts(64, 0):
                        eng.wait_ge(self.scat, n.at(64, 0))
                    if n.counts(10, 0):
                        eng.wait_ge(self.g_rdy[1], n.at(10, 0))
                nc.scalar.activation(self.qd[:, g, :], G_BANK[0][0:CH, 0:T], ACT.Identity,
                                     bias=qb1[:, g:g + 1]).then_inc(self.g_out[0], 1)

            def dve_k(self, eng, n, g):
                eng.wait_ge(self.g_rdy[1], n.at(10, 2 + g))
                if g == 0:
                    if n.counts(64, 0):
                        eng.wait_ge(self.scat, n.at(64, 0))
                nc.vector.tensor_scalar(self.kd[:, g, :], G_BANK[1][0:CH, 0:T], kb1[:, g:g + 1], D1 ** -0.5,
                                        ALU.add, ALU.mult).then_inc(self.g_out[1], 1)

            def pe_v(self, eng, n, t):
                half = HEADS * D1 // 2
                for b in range(2):
                    self.g_free(eng, n, b, 9 + t)
                    for c in range(2):
                        mm = nc.tensor.matmul(G_BANK[b][:, 0:half], xnT[:, c, t * P:(t + 1) * P],
                                              wv1[:, c, b * half:(b + 1) * half], start=(c == 0), stop=(c == 1))
                    mm.then_inc(self.g_rdy[b], 1)

            def v_views(self, n, t, b):
                return (V1[n.parity][:, t, b * NPAIR:(b + 1) * NPAIR, 0:D1],
                        G_BANK[b][:, 0:HEADS * D1 // 2].rearrange("p (h d) -> p h d", d=D1))

            def act_v(self, eng, n, t):
                eng.wait_ge(self.g_rdy[0], n.at(10, 9 + t))
                if n.counts(NPAIR, -NPAIR):
                    eng.wait_ge(self.pv, n.at(NPAIR, -NPAIR))
                nc.scalar.copy(*self.v_views(n, t, 0)).then_inc(self.g_out[0], 1)

            def dve_v(self, eng, n, t):
                eng.wait_ge(self.g_rdy[1], n.at(10, 9 + t))
                if n.counts(NPAIR, -NPAIR):
                    eng.wait_ge(self.pv, n.at(NPAIR, -NPAIR))
                nc.vector.tensor_copy(*self.v_views(n, t, 1)).then_inc(self.g_out[1], 1)

            def pe_rel(self, eng, n):
                eng.wait_ge(self.g_out[0], n.at(11, 7))
                for b in range(2):
                    self.g_free(eng, n, b, 7)
                    for i in range(8):
                        for s in range(4):
                            v = self.qd[:, 3 * (s % 2):3 * (s % 2) + 3, :].rearrange("k g (r c) -> k g r c", c=W)
                            line = 8 * b + i
                            v = v[:, :, line, :] if s < 2 else v[:, :, :, line]
                            mm = nc.tensor.matmul(G_BANK[b][32 * s:32 * s + 32, 48 * i:48 * i + 48],
                                                  relw[2 + s // 2][:, line, :, :].rearrange("k a b -> k (a b)"), v,
                                                  start=True, stop=True)
                    mm.then_inc(self.g_rdy[b], 1)

            def rel_views(self, b, s):
                rows = slice(64 * s, 64 * s + 64)
                src = G_BANK[b][rows, 0:8 * 48]
                dst = self.reld[rows, :, :].rearrange("p g (r c) -> p g r c", c=W)
                if s == 0:
                    return dst[:, :, 8 * b:8 * b + 8, :], src.rearrange("p (r g c) -> p g r c", g=3, c=W)
                return dst[:, :, :, 8 * b:8 * b + 8], src.rearrange("p (c g r) -> p g r c", g=3, r=H)

            def act_rel(self, eng, n):
                eng.wait_ge(self.g_rdy[0], n.at(10, 8))
                if n.counts(128, 0):
                    eng.wait_ge(self.relscat, n.at(128, 0))
                for s in range(2):
                    nc.scalar.copy(*self.rel_views(0, s)).then_inc(self.g_out[0], 1)

            def dve_rel(self, eng, n):
                eng.wait_ge(self.g_rdy[1], n.at(10, 8))
                if n.counts(128, 0):
                    eng.wait_ge(self.relscat, n.at(128, 0))
                for s in range(2):
                    nc.vector.tensor_copy(*self.rel_views(1, s)).then_inc(self.g_out[1], 1)

            def sp(self, eng):
                def image(n):
                    p = n.parity
                    if n.counts(self.NU, -self.NU):
                        eng.wait_ge(self.s_rdy, n.at(self.NU, -self.NU))
                    land(eng, "sp")
                    eng.wait_ge(self.g_out[0], n.at(11, 7))
                    land(eng, "sp")
                    for j in range(2):
                        eng.dma_start(Q1[p][0:D1, j:HEADS:2, :], self.qd[D1 * j:D1 * (j + 1), :, :]).then_inc(self.scat, 16)
                    eng.wait_ge(self.g_out[1], n.at(11, 7))
                    land(eng, "sp")
                    for j in range(2):
                        eng.dma_start(K1[p][0:D1, j:HEADS:2, :], self.kd[D1 * j:D1 * (j + 1), :, :]).then_inc(self.scat, 16)
                    for b in range(2):
                        eng.wait_ge(self.g_out[b], n.at(11, 9))
                        land(eng, "sp")
                    for s in range(4):
                        for j in range(2):
                            at = K1REL + H * (s // 2)
                            first = 6 * (s % 2) + j
                            eng.dma_start(Q1[p][at:at + H, first:first + 5:2, :],
                                          self.reld[32 * s + H * j:32 * s + H * (j + 1), :, :]).then_inc(self.relscat, 16)
                image(Img(0, 0))
                image(Img(0, 1))
                with eng.Fori(1, B // 2) as pair:
                    image(Img(pair, 0))
                    image(Img(pair, 1))

            def pool_front(self, eng, n):
                pass

            def setup(self):
                self.qd, self.kd, self.reld = dense[0][:], dense[1][:], rel_dense[:]
                ln = lambda e, n: self.norm.dve_stats(e, n)
                xh = lambda e, n: self.norm.dve_xhat(e, n, self.g_rdy[1], 10, -9)

                def each(f, ks):
                    return [lambda e, n, k=k: f(e, n, k) for k in ks]
                self.pe_fronts = {2: [self.pe_transpose_x], 3: each(self.pe_qk, (0, 1)), 4: each(self.pe_qk, (2, 3)),
                                  5: each(self.pe_qk, (4, 5)), 6: [self.pe_rel], 8: each(self.pe_v, (0,)),
                                  9: each(self.pe_v, (1,))}
                self.act_fronts = {2: [self.act_xn], 3: each(self.act_q, (0, 1)), 4: each(self.act_q, (2, 3)),
                                   5: each(self.act_q, (4, 5)), 7: [self.act_rel], 8: each(self.act_v, (0,)),
                                   9: each(self.act_v, (1,))}
                self.dve_fronts = {0: [ln], 1: [xh], 2: [self.dve_xn], 3: each(self.dve_k, (0, 1)),
                                   4: each(self.dve_k, (2, 3)), 5: each(self.dve_k, (4, 5)), 7: [self.dve_rel],
                                   8: each(self.dve_v, (0,)), 9: each(self.dve_v, (1,))}

        a0 = Attention0(0, lambda n: (ld_x, 16), xdone[0], L0_UNITS, {6 * q + 5: [q] for q in range(3)})
        m0 = Mlp(0, ACT.Gelu, xdone[0], xdone[1], False)
        a1 = Attention1(1, lambda n: (xdone[1], n.at(1, 1)), xdone[2], [("main", h) for h in range(HEADS)],
                        {2 * q + 1: [q] for q in range(NPAIR)})
        m1 = Mlp(1, ACT.Gelu_apprx_tanh, xdone[2], xdone[3], True)
        a0.setup()
        a1.setup()
        stages = (a0, m0, a1, m1)

        def stage_start(eng, i):
            if i:
                eng.wait_ge(xdone[i - 1], B)

        ctx.enter_context(nc.allow_non_contiguous_dma(reason="bias vectors to columns, a few KB once"))
        block = ctx.enter_context(nc.Block())

        zero_dve = [Q1[0], K1[0], V0[0], V0[1], KP0]
        zero_pool = [wproj0, vb0, wo1, vb1, QR0[0], QR0[1], KR0[0], KR0[1], VR0[0], VR0[1], Q1[1], K1[1]]
        NZ = len(zero_dve) + len(zero_pool)
        vbc = [area[:, 0:3 * P].rearrange("p (q m) -> p q m", q=3),
               area[:, 3 * P:(3 + NPAIR) * P].rearrange("p (q m) -> p q m", q=NPAIR)]
        tab_bank = G_BANK[0]
        NPREP = 4 + 2 + 2 * WS + H + W + 1 + 2

        @block.sync
        def _(sp):
            sp.dma_start(x_all[:], x_view).then_inc(ld_x, 16)
            for dst, src in loads:
                sp.dma_start(dst, src).then_inc(ld_w, 16)
            sp.wait_ge(zeroed, NZ)
            for dst, src in late:
                sp.dma_start(dst, src).then_inc(ld_c, 16)
            a0.sp(sp)
            stage_start(sp, 2)
            a1.sp(sp)
            with sp.Fori(0, B) as n:
                sp.wait_ge(xdone[3], n + 1)
                sp.dma_start(out_view[:, bass.ds(n * NT, NT), :], x_all[:, bass.ds(n * NT, NT), :]).then_inc(out_done, 16)
            sp.wait_ge(out_done, 16 * B)

        @block.gpsimd
        def _(pool):
            for z in zero_pool:
                nc.gpsimd.memset(z[:], 0.0).then_inc(zeroed, 1)
            nc.gpsimd.memset(mhalf[:], -0.5).then_inc(prep_pool, 1)
            pool.wait_ge(prep_pool, 1)
            for i, s in enumerate(stages):
                stage_start(pool, i)
                if i == 2:
                    for v in V1:
                        nc.gpsimd.memset(v[:, :, :, D1:64], 0.0).then_inc(prep_pool, 1)
                s.run_pool(pool)

        @block.tensor
        def _(pe):
            pe.wait_ge(ld_w, 16 * len(loads))
            for i in range(4):
                n = 27 if i < 2 else 31
                nc.tensor.matmul(tab_bank[0:CH, 32 * i:32 * i + n], relnat[i][:].rearrange("r h d -> r (h d)"),
                                 (flip27 if i < 2 else flip)[:], start=True, stop=True).then_inc(prep_pe, 1)
            pe.wait_ge(prep_dve, 6)
            pe.wait_ge(ld_c, 16 * len(late))
            for l, (w, k) in enumerate(((wproj0, 3), (wo1, NPAIR))):
                for q in range(k):
                    mm = nc.tensor.matmul(G_BANK[1][:, l * C:(l + 1) * C], vbc[l][:, q, :], w[:, q, :],
                                          start=(q == 0), stop=(q == k - 1))
                mm.then_inc(prep_pe, 1)
            pe.wait_ge(prep_dve, NPREP - 2)
            for i, s in enumerate(stages):
                stage_start(pe, i)
                if i == 2:
                    pe.wait_ge(prep_pool, 3)
                s.run(pe, "pe")

        @block.scalar
        def _(act):
            act.wait_ge(ld_w, 16 * len(loads))
            for i, s in enumerate(stages):
                stage_start(act, i)
                s.run(act, "act")


        @block.vector
        def _(dve):
            for z in zero_dve:
                nc.vector.memset(z[:], 0.0).then_inc(zeroed, 1)
            dve.wait_ge(ld_w, 16 * len(loads))
            dve.wait_ge(prep_pe, 4)
            for i in range(4):
                n = 27 if i < 2 else 31
                nc.vector.tensor_copy(reltab[i][:], tab_bank[0:CH, 32 * i:32 * i + n]).then_inc(prep_dve, 1)
            dve.wait_ge(ld_c, 16 * len(late))
            for l, (v, k) in enumerate(((vb0, 3), (vb1, NPAIR))):
                nc.vector.tensor_copy(vbc[l], v[:].unsqueeze(2).broadcast_to([P, k, P])).then_inc(prep_dve, 1)
            dve.wait_ge(prep_dve, 4)
            for i, (win, heads, blk) in enumerate(((WS, GH0, blk0), (WS, GH0, blk0), (H, 2, blk1), (W, 2, blk1))):
                for line in range(win):
                    row = reltab[i][:, win - 1 - line:2 * win - 1 - line]
                    nc.vector.tensor_tensor(relw[i][:, line, :, :], row.unsqueeze(1).broadcast_to([CH, heads, win]),
                                            blk[:].unsqueeze(2).broadcast_to([CH, heads, win]), ALU.mult)\
                      .then_inc(prep_dve, 1)
            nc.vector.tensor_scalar(KP0[0:D0], kpad0[:].unsqueeze(2).broadcast_to([D0, HEADS, N0]), D0 ** -0.5, None,
                                    ALU.mult).then_inc(prep_dve, 1)
            dve.wait_ge(prep_pe, 6)
            for l in range(2):
                nc.vector.tensor_tensor(obias[l][:], G_BANK[1][:, l * C:(l + 1) * C], obias[l][:], ALU.add)\
                  .then_inc(prep_dve, 1)
            dve.wait_ge(prep_dve, NPREP)
            for i, s in enumerate(stages):
                stage_start(dve, i)
                s.run(dve, "dve")


def shape_constants():
    c = {"c_ident": np.eye(P), "c_flip31": np.eye(31)[::-1], "c_flip27": np.eye(27)[::-1]}
    ch = np.arange(CH)
    c["c_blk0"] = ch[:, None] // D0 == np.arange(GH0)
    c["c_blk1"] = ch[:, None] // D1 == np.arange(2)
    t = np.arange(T)
    c["c_hot0"] = np.concatenate([np.arange(WS)[:, None] == (t // W) % WS, np.arange(WS)[:, None] == (t % W) % WS])
    c["c_hot1"] = np.concatenate([np.arange(H)[:, None] == t // W, np.arange(W)[:, None] == t % W])
    grid = t.reshape(H, W)
    parts = [grid[:WS, WS:].ravel(), grid[WS:, :WS].ravel(), grid[WS:, WS:].ravel()]
    rem = np.concatenate(parts)
    window = np.repeat(np.arange(3), [len(p) for p in parts])
    mask = np.where(np.arange(3)[:, None] == window, 0.0, NEG)
    c["c_hotrem"] = np.concatenate([c["c_hot0"][:, rem], mask])
    c["c_qwin"] = np.concatenate([np.arange(3)[:, None] == window, np.zeros((3, RPAD - NREM))], axis=1)
    kh, kw = np.arange(N0) // WS, np.arange(N0) % WS
    pad = [kw >= EDGE, kh >= EDGE, (kh >= EDGE) | (kw >= EDGE)]
    c["c_hotpad"] = np.concatenate([np.arange(WS)[:, None] == kh, np.arange(WS)[:, None] == kw,
                                    np.where(np.stack(pad), 0.0, NEG)])
    return {k: np.ascontiguousarray(v, dtype=np.float32) for k, v in c.items()}


def kernel(**inputs):
    import concourse.bacc as bacc
    from concourse.bass_utils import run_bass_kernel_spmd

    nc = bacc.Bacc("TRN2", target_bir_lowering=False, num_devices=1)
    arrays = {k: np.ascontiguousarray(v) for k, v in inputs.items()}
    arrays.update(shape_constants())
    arrays = {f"in_{k}": v for k, v in arrays.items()}
    aps = {k[3:]: nc.dram_tensor(k, v.shape, mybir.dt.from_np(v.dtype), kind="ExternalInput").ap()
           for k, v in arrays.items()}
    out = nc.dram_tensor("out", (B, H, W, C), F32, kind="ExternalOutput").ap()
    build(nc, aps, out)
    r = run_bass_kernel_spmd(nc, [arrays], core_ids=[0])
    return r.results[0]["out"]
```

```python
from contextlib import ExitStack

import numpy as np

import concourse.bass as bass
from concourse import mybir

F32 = mybir.dt.float32
ALU = mybir.AluOpType
ACT = mybir.ActivationFunctionType
AX = mybir.AxisListType

P = 128
B, H, W, C = 8, 16, 16, 192
T = H * W
NT = T // P
CH = C // 2
MLP = 4 * C
NM = MLP // P
EPS = 1e-5
HEADS = 12
WS = 14
D0 = C // HEADS
D1 = 48
GH0 = CH // D0
NPAIR = HEADS // 2
N0 = WS * WS
HT0 = N0 // 2
NREM = T - N0
EDGE = H - WS
RPAD = 64
K0ROWS = D0 + 2 * WS
KR0ROWS = K0ROWS + 3
K1REL = 64
K1ROWS = K1REL + 2 * H
NEG = -1.0e30
L0_UNITS = [("main", 4 * q + j) if s == 0 else ("rem", 2 * q + j)
            for q in range(3) for s, j in ((0, 0), (0, 1), (1, 0), (0, 2), (0, 3), (1, 1))]


class Img:

    def __init__(self, pair, par):
        self.pair, self.par = pair, par

    def at(self, per, k):
        return self.pair * (2 * per) + (self.par * per + k)

    def counts(self, per, k):
        value = self.at(per, k)
        return not isinstance(value, int) or value > 0

    @property
    def parity(self):
        return self.par % 2

    def next(self):
        return Img(self.pair, self.par + 1)

    def prev(self):
        return Img(self.pair, self.par - 1)


def image_loop(eng, step):
    step(Img(0, 0), False, True)
    step(Img(0, 1), True, True)
    with eng.Fori(1, B // 2 - 1) as pair:
        step(Img(pair, 0), True, True)
        step(Img(pair, 1), True, True)
    step(Img(B // 2 - 1, 0), True, True)
    step(Img(B // 2 - 1, 1), True, False)


def mlp_loop(eng, step):
    step(Img(0, 0), True, True)
    step(Img(0, 1), True, True)
    with eng.Fori(1, B // 2 - 1) as pair:
        step(Img(pair, 0), True, True)
        step(Img(pair, 1), True, True)
    step(Img(B // 2 - 1, 0), True, False)
    step(Img(B // 2 - 1, 1), False, False)


def build(nc, a, out):
    with ExitStack() as ctx:
        def sb(name, shape, dt=F32):
            return ctx.enter_context(nc.sbuf_tensor(name, shape, dt))

        def sem(name):
            return ctx.enter_context(nc.semaphore(name))

        bank = [ctx.enter_context(nc.psum_tensor(f"bank{i}", [P, 512], F32)) for i in range(8)]
        S_BANK, PT_BANK, O_BANK, G_BANK = bank[0:3], bank[3:5], bank[5], bank[6:8]
        Y_BANK = O_BANK

        x_all = sb("x_all", [P, B * NT, C])
        x_view = a["x"].rearrange("b (t r) w c -> (r w) (b t) c", t=NT)
        out_view = out.rearrange("b (t r) w c -> (r w) (b t) c", t=NT)
        ident = sb("ident", [P, P])

        wqkv0 = sb("wqkv0", [CH, 2, 3 * C])
        wproj0 = sb("wproj0", [P, 3, C])
        fc1w = [sb(f"fc1w{l}", [CH, 2, MLP]) for l in range(2)]
        fc2w = [sb(f"fc2w{l}", [P, NM, C]) for l in range(2)]
        wq1 = sb("wq1", [CH, 2, HEADS * D1])
        wk1 = sb("wk1", [CH, 2, HEADS * D1])
        wv1 = sb("wv1", [CH, 2, HEADS * D1])
        wo1 = sb("wo1", [P, NPAIR, C])
        lnw = [sb(f"lnw{i}", [CH, 2]) for i in range(4)]
        lnb = [sb(f"lnb{i}", [CH, 2]) for i in range(4)]
        qb0 = sb("qb0", [CH, 2])
        kb0 = sb("kb0", [CH, 2])
        kpad0 = sb("kpad0", [D0, HEADS])
        qb1 = sb("qb1", [CH, NPAIR])
        kb1 = sb("kb1", [CH, NPAIR])
        fc1b = [sb(f"fc1b{l}", [P, NM]) for l in range(2)]
        vb0 = sb("vb0", [P, 3])
        vb1 = sb("vb1", [P, NPAIR])
        obias = [sb(f"obias{l}", [P, C]) for l in range(2)]
        fc2b = [sb(f"fc2b{l}", [P, C]) for l in range(2)]
        flip = sb("flip", [31, 31])
        flip27 = sb("flip27", [27, 27])
        reltab = [sb("reltab_h0", [CH, 27]), sb("reltab_w0", [CH, 27]),
                  sb("reltab_h1", [CH, 31]), sb("reltab_w1", [CH, 31])]
        blk0 = sb("blk0", [CH, GH0])
        blk1 = sb("blk1", [CH, 2])
        relw = [sb("relw_h0", [CH, WS, GH0, WS]), sb("relw_w0", [CH, WS, GH0, WS]),
                sb("relw_h1", [CH, H, 2, H]), sb("relw_w1", [CH, W, 2, W])]

        lnst = sb("lnst", [P, NT, 6])
        lnag = sb("lnag", [P, NT, 2])
        lnve = sb("lnve", [P, NT])
        lnrs = sb("lnrs", [P, NT])
        mhalf = sb("mhalf", [P, NT])
        xhat = sb("xhat", [P, NT, C])
        xnT = sb("xnT", [CH, 2, T])
        xbias = sb("xbias", [P, NT, C])

        Q1 = [sb(f"Q_{i}", [K1ROWS, HEADS, T]) for i in range(2)]
        K1 = [sb(f"K_{i}", [K1ROWS, HEADS, T]) for i in range(2)]
        Q0, K0 = Q1, K1
        dense = [sb("dense_q", [CH, NPAIR, T]), sb("dense_k", [CH, NPAIR, T])]
        rel_dense = sb("rel_dense", [P, 3, T])
        QR0 = [sb(f"QR0_{i}", [K1ROWS, HEADS, RPAD]) for i in range(2)]
        KR0 = [sb(f"KR0_{i}", [K1ROWS, HEADS, NREM]) for i in range(2)]
        KP0 = sb("KP0", [K1ROWS, HEADS, N0])
        xr0 = sb("xr0", [CH, 2, NREM])
        xm0 = rel_dense[0:CH].rearrange("p g t -> p (g t)")[:, 0:2 * N0].rearrange("p (c t) -> p c t", c=2)
        V0 = [sb(f"V0_{i}", [HT0, 2, HEADS, 32]) for i in range(2)]
        VR0 = [sb(f"VR0_{i}", [NREM, HEADS, 32]) for i in range(2)]
        area = sb("area", [P, 2 * NT * HEADS * 64 + (8 + NPAIR) * T])
        PTm0 = area[0:HT0, 0:HEADS * 2 * N0].rearrange("p (h k q) -> p h k q", h=HEADS, k=2)
        hT = [area[:, i * NM * T:(i + 1) * NM * T].rearrange("p (m t) -> p m t", m=NM) for i in range(2)]
        V1 = [area[:, i * 1536:(i + 1) * 1536].rearrange("p (t h d) -> p t h d", t=NT, h=HEADS) for i in range(2)]
        PT1 = area[:, 3072:3072 + 8 * T].rearrange("p (b k q) -> p b k q", b=4, k=2)
        AO1 = area[:, 3072 + 8 * T:3072 + (8 + NPAIR) * T].rearrange("p (q t) -> p q t", q=NPAIR)
        PTr0 = area[0:NREM, HEADS * 2 * N0:HEADS * 2 * N0 + NPAIR * P].rearrange("p (h q) -> p h q", h=NPAIR)
        AO0 = area[:, HEADS * 2 * N0 + NPAIR * P:HEADS * 2 * N0 + NPAIR * P + 3 * T].rearrange("p (q t) -> p q t", q=3)

        relnat = []
        for i, (n, rep, d) in enumerate(((27, GH0, D0), (27, GH0, D0), (31, 2, D1), (31, 2, D1))):
            relnat.append(area[0:n, (16 + i) * P:(16 + i) * P + rep * d].rearrange("r (h d) -> r h d", d=d))

        nmax = sb("nmax", [P, 3, 2])
        esum = sb("esum", [P, 3, 2])
        rsum = sb("rsum", [P, 3, 2])
        Pb = [sb(f"Pb{i}", [P, 2, T]) for i in range(3)]

        ld_x = sem("ld_x")
        ld_first = sem("ld_first")
        ld_w = sem("ld_w")
        relw_done = sem("relw_done")
        relw_h0_done = sem("relw_h0_done")
        relw_w0_done = sem("relw_w0_done")
        kpad_done = sem("kpad_done")
        obias_done = sem("obias_done")
        zeroed_more = sem("zeroed_more")
        zeroed = sem("zeroed")
        ld_c = sem("ld_c")
        prep_pe = sem("prep_pe")
        prep_dve = sem("prep_dve")
        prep_pool = sem("prep_pool")
        out_done = sem("out_done")
        xdone = [sem(f"xdone{i}") for i in range(4)]

        def col(v, n, off=0, p=CH):
            return v[off:off + p * n].rearrange("(c p) -> p c", p=p)

        def bcast(v, n=P):
            return v.partition_broadcast(n)

        def norm_loads(i, w_, b_):
            return [(lnw[i][:], col(a[w_], 2)), (lnb[i][:], col(a[b_], 2))]

        def table_loads(i, name):
            r_, rep, d = relnat[i].shape
            return [(relnat[i], a[name].unsqueeze(1).broadcast_to([r_, rep, d]))]

        qkvb = a["L0_conv_qkv_b"]
        first = [(ident[:], a["c_ident"]), (flip27[:], a["c_flip27"]), (blk0[:], a["c_blk0"])]
        first += table_loads(0, "L0_conv_rel_pos_h") + table_loads(1, "L0_conv_rel_pos_w")
        first += norm_loads(0, "L0_conv_norm1_w", "L0_conv_norm1_b")
        first += [(wqkv0[:], a["L0_conv_qkv_w"].rearrange("(c p) n -> p c n", p=CH)),
                  (qb0[:], col(qkvb, 2)), (kb0[:], col(qkvb, 2, C)),
                  (kpad0[:], qkvb[C:2 * C].rearrange("(h d) -> d h", d=D0))]
        rest = [(flip[:], a["c_flip31"]), (blk1[:], a["c_blk1"])]
        rest += table_loads(2, "L1_conv_rel_pos_0") + table_loads(3, "L1_conv_rel_pos_1")
        rest += [(obias[0][:], bcast(a["L0_conv_proj_b"])), (obias[1][:], bcast(a["L1_conv_bo"])),
                 (fc1w[0][:], a["L0_conv_fc1_w"].rearrange("(c p) n -> p c n", p=CH)),
                 (fc2w[0][:], a["L0_conv_fc2_w"].rearrange("(m p) n -> p m n", p=P)),
                 (wq1[:], a["L1_conv_wq"].rearrange("(c p) n -> p c n", p=CH)),
                 (wk1[:], a["L1_conv_wk"].rearrange("(c p) n -> p c n", p=CH)),
                 (wv1[:], a["L1_conv_wv"].rearrange("(c p) n -> p c n", p=CH)),
                 (fc1w[1][:], a["L1_conv_w1"].rearrange("(c p) n -> p c n", p=CH)),
                 (fc2w[1][:], a["L1_conv_w2"].rearrange("(m p) n -> p m n", p=P)),
                 (qb1[:], col(a["L1_conv_bq"], NPAIR)), (kb1[:], col(a["L1_conv_bk"], NPAIR)),
                 (fc1b[0][:], col(a["L0_conv_fc1_b"], NM, p=P)), (fc1b[1][:], col(a["L1_conv_b1"], NM, p=P)),
                 (fc2b[0][:], bcast(a["L0_conv_fc2_b"])), (fc2b[1][:], bcast(a["L1_conv_b2"]))]
        rest += norm_loads(1, "L0_conv_norm2_w", "L0_conv_norm2_b")
        rest += norm_loads(2, "L1_conv_ln1_scale", "L1_conv_ln1_offset")
        rest += norm_loads(3, "L1_conv_ln2_scale", "L1_conv_ln2_offset")

        late = []
        for j in range(4):
            late.append((wproj0[32 * j:32 * j + D0, :, :],
                         a["L0_conv_proj_w"].rearrange("(q j d) n -> j d q n", j=4, d=D0)[j]))
            late.append((vb0[32 * j:32 * j + D0, :], qkvb[2 * C:].rearrange("(q j d) -> j d q", j=4, d=D0)[j]))
        for j in range(2):
            late.append((wo1[64 * j:64 * j + D1, :, :],
                         a["L1_conv_wo"].rearrange("(q j d) n -> j d q n", j=2, d=D1)[j]))
            late.append((vb1[64 * j:64 * j + D1, :], a["L1_conv_bv"].rearrange("(q j d) -> j d q", j=2, d=D1)[j]))
        def per_head(v):
            return v.unsqueeze(1).broadcast_to([v.shape[0], HEADS, v.shape[1]])

        late.append((KP0[D0:KR0ROWS], per_head(a["c_hotpad"])))
        for i in range(2):
            late.append((K1[i][D0:K0ROWS], per_head(a["c_hot0"])))
            late.append((K1[i][K1REL:K1ROWS], per_head(a["c_hot1"])))
            late.append((KR0[i][D0:KR0ROWS], per_head(a["c_hotrem"])))
            late.append((QR0[i][K0ROWS:KR0ROWS], per_head(a["c_qwin"])))

        landed = {e: sem(f"landed_{e}") for e in ("pe", "dve", "pool", "sp")}

        def land(eng, name):
            eng.sem_inc(landed[name], 1)

        class Norm:
            def __init__(self, l, x_before):
                self.l, self.x_before = l, x_before
                self.stats = sem(f"ln_stats{l}")
                self.eps = sem(f"ln_eps{l}")
                self.rstd = sem(f"ln_rstd{l}")
                self.xhat = sem(f"ln_xhat{l}")

            def dve_stats(self, eng, n):
                s, v = self.x_before(n)
                eng.wait_ge(s, v)
                for t in range(NT):
                    nc.vector.bn_stats(lnst[:, t, :], self.x(n, t)).then_inc(self.stats, 1)
                eng.wait_ge(self.stats, n.at(2 * NT, NT))
                land(eng, "dve")
                for t in range(NT):
                    nc.vector.bn_aggr(lnag[:, t, :], lnst[:, t, :]).then_inc(self.stats, 1)

            def x(self, n, t):
                return x_all[:, bass.ds(n.at(NT, t), 1), :].rearrange("p a c -> p (a c)")

            def pool_rstd(self, eng, n):
                eng.wait_ge(self.stats, n.at(2 * NT, 2 * NT))
                land(eng, "pool")
                nc.gpsimd.tensor_scalar(lnve[:], lnag[:, :, 1], EPS, None, ALU.add).then_inc(self.eps, 1)
                eng.wait_ge(self.eps, n.at(1, 1))
                nc.gpsimd.tensor_tensor(lnrs[:], lnve[:], mhalf[:], ALU.pow).then_inc(self.rstd, 1)

            def dve_xhat(self, eng, n, transposed, per, k):
                eng.wait_ge(self.rstd, n.at(1, 1))
                if n.counts(per, k):
                    eng.wait_ge(transposed, n.at(per, k))
                for t in range(NT):
                    nc.vector.tensor_scalar(xhat[:, t, :], self.x(n, t), lnag[:, t, 0:1], lnrs[:, t:t + 1],
                                            ALU.subtract, ALU.mult).then_inc(self.xhat, 1)

        class Mlp:
            def __init__(self, l, func, x_sem, done, last):
                self.l, self.func, self.done, self.last = l, func, done, last
                self.norm = Norm(2 * l + 1, lambda n: (x_sem, n.at(1, 1)))
                self.xt = [sem(f"m{l}_xt{c}") for c in range(2)]
                self.xn = [sem(f"m{l}_xn{c}") for c in range(2)]
                self.h = sem(f"m{l}_h")
                self.g = sem(f"m{l}_g")
                self.y = sem(f"m{l}_y")
                self.xb = sem(f"m{l}_xb")
                self.hbank = [S_BANK[0], S_BANK[1], PT_BANK[0], PT_BANK[1]]

            def pe_norm(self, eng, n):
                for c in range(2):
                    if n.counts(1, 0):
                        eng.wait_ge(self.xn[c], n.at(1, 0))
                    for t in range(NT):
                        eng.wait_ge(self.norm.xhat, n.at(NT, t + 1))
                        mm = nc.tensor.transpose(G_BANK[c][0:CH, t * P:(t + 1) * P],
                                                 xhat[:, t, c * CH:(c + 1) * CH], ident[:])
                    mm.then_inc(self.xt[c], 1)

            def act_norm(self, eng, n):
                eng.wait_ge(self.xt[0], n.at(1, 1))
                if n.counts(NM, 0):
                    eng.wait_ge(self.h, n.at(NM, 0))
                nc.scalar.activation(xnT[:, 0, :], G_BANK[0][0:CH, 0:T], ACT.Identity,
                                     scale=lnw[2 * self.l + 1][:, 0:1], bias=lnb[2 * self.l + 1][:, 0:1]).then_inc(self.xn[0], 1)

            def dve_norm(self, eng, n):
                self.norm.dve_stats(eng, n)
                self.norm.dve_xhat(eng, n, self.xt[1], 1, 0)
                eng.wait_ge(self.xt[1], n.at(1, 1))
                if n.counts(NM, 0):
                    eng.wait_ge(self.h, n.at(NM, 0))
                nc.vector.tensor_scalar(xnT[:, 1, :], G_BANK[1][0:CH, 0:T], lnw[2 * self.l + 1][:, 1:2],
                                        lnb[2 * self.l + 1][:, 1:2], ALU.mult, ALU.add).then_inc(self.xn[1], 1)

            def pe_up(self, eng, n):
                for c in range(2):
                    eng.wait_ge(self.xn[c], n.at(1, 1))
                for m in range(NM):
                    if n.counts(NM, m - 3):
                        eng.wait_ge(self.g, n.at(NM, m - 3))
                    for c in range(2):
                        mm = nc.tensor.matmul(self.hbank[(n.parity * NM + m) % 4][:, 0:T],
                                              fc1w[self.l][:, c, m * P:(m + 1) * P], xnT[:, c, :],
                                              start=(c == 0), stop=(c == 1))
                    mm.then_inc(self.h, 1)

            def act_up(self, eng, n):
                for m in range(NM):
                    eng.wait_ge(self.h, n.at(NM, m + 1))
                    if n.counts(1, -1):
                        eng.wait_ge(self.y, n.at(1, -1))
                    nc.scalar.activation(hT[n.parity][:, m, :], self.hbank[(n.parity * NM + m) % 4][:, 0:T],
                                         self.func, bias=fc1b[self.l][:, m:m + 1]).then_inc(self.g, 1)

            def pe_down(self, eng, n):
                ybank = (O_BANK, S_BANK[2])[n.parity]
                eng.wait_ge(self.g, n.at(NM, NM))
                if n.counts(1, -1):
                    eng.wait_ge(self.done, n.at(1, -1))
                for t in range(NT):
                    for m in range(NM):
                        mm = nc.tensor.matmul(ybank[:, t * C:(t + 1) * C], hT[n.parity][:, m, t * P:(t + 1) * P],
                                              fc2w[self.l][:, m, :], start=(m == 0), stop=(m == NM - 1))
                mm.then_inc(self.y, 1)

            def pool_back(self, eng, n):
                s, v = self.norm.x_before(n)
                eng.wait_ge(s, v)
                if n.counts(1, 0):
                    eng.wait_ge(self.done, n.at(1, 0))
                nc.gpsimd.tensor_tensor(xbias[:], x_all[:, bass.ds(n.at(NT, 0), NT), :],
                                        fc2b[self.l][:].unsqueeze(1).broadcast_to([P, NT, C]),
                                        ALU.add).then_inc(self.xb, 1)

            def dve_down(self, eng, n):
                ybank = (O_BANK, S_BANK[2])[n.parity]
                eng.wait_ge(self.y, n.at(1, 1))
                eng.wait_ge(self.xb, n.at(1, 1))
                nc.vector.tensor_tensor(x_all[:, bass.ds(n.at(NT, 0), NT), :],
                                        ybank[:, 0:NT * C].rearrange("p (t c) -> p t c", t=NT), xbias[:],
                                        ALU.add).then_inc(self.done, 1)

            def run(self, eng, which, meanwhile=None):
                norm, up, down = {"pe": (self.pe_norm, self.pe_up, self.pe_down),
                                  "act": (self.act_norm, self.act_up, None),
                                  "dve": (self.dve_norm, None, self.dve_down)}[which]
                norm(eng, Img(0, 0))
                if up:
                    up(eng, Img(0, 0))
                norm(eng, Img(0, 1))
                if meanwhile:
                    meanwhile(eng)

                def step(n, has_next, has_second):
                    if has_next and up:
                        up(eng, n.next())
                    if has_second:
                        norm(eng, n.next().next())
                    if down:
                        down(eng, n)
                mlp_loop(eng, step)

            def run_pool(self, eng):
                self.norm.pool_rstd(eng, Img(0, 0))
                self.norm.pool_rstd(eng, Img(0, 1))

                def step(n, has_next, has_second):
                    if has_second:
                        self.norm.pool_rstd(eng, n.next().next())
                    self.pool_back(eng, n)
                mlp_loop(eng, step)

        class Attention:

            def __init__(self, l, x_before, done, units, pv_after):
                self.l, self.done, self.units = l, done, units
                self.norm = Norm(2 * l, x_before)
                self.NU = len(units)
                self.pv_after = pv_after
                tiles = [len(self.tiles(u)) for u in range(self.NU)]
                self.cum = [sum(tiles[:u]) for u in range(self.NU + 1)]
                self.NTL = self.cum[-1]
                self.pt_cum = [[sum(self.pt_engine(v) == e for v in range(u)) for u in range(self.NU + 1)]
                               for e in range(2)]
                s = f"a{l}_"
                self.s_rdy = sem(s + "scores")
                self.m_rdy = sem(s + "max")
                self.e_rdy = sem(s + "exp")
                self.r_rdy = sem(s + "rsum")
                self.p_rdy = sem(s + "probs")
                self.t_rdy = sem(s + "probsT")
                self.pt = [sem(s + "ptA"), sem(s + "ptB")]
                self.pv = sem(s + "values")
                self.ao = [sem(s + "aoA"), sem(s + "aoB")]
                self.y = sem(s + "proj")
                self.xb = sem(s + "xbias")
                self.g_rdy = [sem(s + "g0"), sem(s + "g1")]
                self.g_out = [sem(s + "g0out"), sem(s + "g1out")]
                self.scat = sem(s + "scatter")
                self.relscat = sem(s + "relscat")

            def pe_scores(self, eng, n, u):
                used = self.cum[u - 2] if u >= 2 else self.cum[self.NU + u - 2] - self.NTL
                if n.counts(self.NTL, used):
                    eng.wait_ge(self.e_rdy, n.at(self.NTL, used))
                self.emit_scores(eng, n, u).then_inc(self.s_rdy, 1)

            def score_tiles(self, u):
                rows, cols, k = self.tiles(u)[0][0], self.tiles(u)[0][1], len(self.tiles(u))
                return S_BANK[u % 3][0:rows, 0:k * cols].rearrange("p (t c) -> p t c", t=k)

            def dve_max(self, eng, n, u):
                eng.wait_ge(self.s_rdy, n.at(self.NU, u + 1))
                sc = self.score_tiles(u)
                nc.vector.tensor_reduce(nmax[0:sc.shape[0], u % 3, 0:sc.shape[1]], sc, AX.X, ALU.max,
                                        negate=True).then_inc(self.m_rdy, 1)

            def act_exp(self, eng, n, u):
                eng.wait_ge(self.m_rdy, n.at(self.NU, u + 1))
                if n.counts(self.NU, u - 2):
                    eng.wait_ge(self.t_rdy, n.at(self.NU, u - 2))
                sc = self.score_tiles(u)
                rows, k, cols = sc.shape
                for t in range(k):
                    nc.scalar.activation(Pb[u % 3][0:rows, t, 0:cols], sc[:, t, :], ACT.Exp,
                                         bias=nmax[0:rows, u % 3, t:t + 1],
                                         accum_out=esum[0:rows, u % 3, t:t + 1]).then_inc(self.e_rdy, 1)

            def dve_norm(self, eng, n, u):
                rows, _, keep = self.tiles(u)[0]
                k = len(self.tiles(u))
                eng.wait_ge(self.e_rdy, n.at(self.NTL, self.cum[u + 1]))
                nc.vector.reciprocal(rsum[0:rows, u % 3, 0:k], esum[0:rows, u % 3, 0:k]).then_inc(self.r_rdy, 1)
                eng.wait_ge(self.r_rdy, n.at(self.NU, u + 1))
                for t in range(k):
                    nc.vector.tensor_scalar(Pb[u % 3][0:rows, t, 0:keep], Pb[u % 3][0:rows, t, 0:keep],
                                            rsum[0:rows, u % 3, t:t + 1], None, ALU.mult).then_inc(self.p_rdy, 1)

            def pe_probsT(self, eng, n, u):
                eng.wait_ge(self.p_rdy, n.at(self.NTL, self.cum[u + 1]))
                m, v = (n, u - 2) if u >= 2 else (n.prev(), self.NU + u - 2)
                e = self.pt_engine(v)
                if m.counts(self.pt_cum[e][-1], self.pt_cum[e][v + 1]):
                    eng.wait_ge(self.pt[e], m.at(self.pt_cum[e][-1], self.pt_cum[e][v + 1]))
                if len(self.tiles(u)) == 1:
                    land(eng, "pe")
                self.emit_probsT(eng, n, u).then_inc(self.t_rdy, 1)

            def pt_out(self, eng, n, u, copy):
                eng.wait_ge(self.t_rdy, n.at(self.NU, u + 1))
                per, k = self.pt_free(u)
                if n.counts(per, k):
                    eng.wait_ge(self.pv, n.at(per, k))
                copy(*self.pt_views(u)).then_inc(self.pt[self.pt_engine(u)], 1)

            def g_free(self, eng, n, b, outs_before):
                if n.counts(self.G_OUTS[b], outs_before):
                    eng.wait_ge(self.g_out[b], n.at(self.G_OUTS[b], outs_before))

            def pe_transpose_x(self, eng, n):
                for c in range(2):
                    self.g_free(eng, n, c, 0)
                    for t in range(NT):
                        eng.wait_ge(self.norm.xhat, n.at(NT, t + 1))
                        mm = nc.tensor.transpose(G_BANK[c][0:CH, t * P:(t + 1) * P],
                                                 xhat[:, t, c * CH:(c + 1) * CH], ident[:])
                    mm.then_inc(self.g_rdy[c], 1)

            def act_xn(self, eng, n):
                eng.wait_ge(self.g_rdy[0], n.at(self.G_USES[0], 1))
                for b in range(2):
                    if n.counts(self.G_USES[b], 0):
                        eng.wait_ge(self.g_rdy[b], n.at(self.G_USES[b], 0))
                nc.scalar.activation(xnT[:, 0, :], G_BANK[0][0:CH, 0:T], ACT.Identity,
                                     scale=lnw[2 * self.l][:, 0:1], bias=lnb[2 * self.l][:, 0:1]).then_inc(self.g_out[0], 1)

            def dve_xn(self, eng, n):
                eng.wait_ge(self.g_rdy[1], n.at(self.G_USES[1], 1))
                for b in range(2):
                    if n.counts(self.G_USES[b], 0):
                        eng.wait_ge(self.g_rdy[b], n.at(self.G_USES[b], 0))
                nc.vector.tensor_scalar(xnT[:, 1, :], G_BANK[1][0:CH, 0:T], lnw[2 * self.l][:, 1:2],
                                        lnb[2 * self.l][:, 1:2], ALU.mult, ALU.add).then_inc(self.g_out[1], 1)

            def xn_ready(self, eng, n):
                for b in range(2):
                    eng.wait_ge(self.g_out[b], n.at(self.G_OUTS[b], 1))

            def pool_xbias(self, eng, n):
                s, v = self.norm.x_before(n)
                eng.wait_ge(s, v)
                if n.counts(1, 0):
                    eng.wait_ge(self.done, n.at(1, 0))
                if isinstance(n.pair, int) and n.pair == 0:
                    eng.wait_ge(obias_done, 2)
                nc.gpsimd.tensor_tensor(xbias[:], x_all[:, bass.ds(n.at(NT, 0), NT), :],
                                        obias[self.l][:].unsqueeze(1).broadcast_to([P, NT, C]),
                                        ALU.add).then_inc(self.xb, 1)

            def dve_back(self, eng, n):
                eng.wait_ge(self.y, n.at(1, 1))
                eng.wait_ge(self.xb, n.at(1, 1))
                nc.vector.tensor_tensor(x_all[:, bass.ds(n.at(NT, 0), NT), :],
                                        Y_BANK[:, 0:NT * C].rearrange("p (t c) -> p t c", t=NT), xbias[:],
                                        ALU.add).then_inc(self.done, 1)

            def run(self, eng, which, meanwhile=None):
                fronts = {"pe": self.pe_fronts, "act": self.act_fronts, "dve": self.dve_fronts}[which]
                slot = {"pe": self.pe_slot, "act": self.act_slot, "dve": self.dve_slot}[which]
                for k in sorted(fronts):
                    for f in fronts[k]:
                        f(eng, Img(0, 0))
                if meanwhile:
                    meanwhile(eng)
                if which == "pe":
                    for u in range(3):
                        self.pe_scores(eng, Img(0, 0), u)
                elif which == "act":
                    for u in range(2):
                        self.act_exp(eng, Img(0, 0), u)
                else:
                    for u in range(3):
                        self.dve_max(eng, Img(0, 0), u)
                    self.dve_norm(eng, Img(0, 0), 0)

                def step(n, has_prev, has_next):
                    def ahead(u, k):
                        if u + k < self.NU:
                            return n, u + k
                        return (n.next(), u + k - self.NU) if has_next else None
                    for u in range(self.NU):
                        slot(eng, n, u, has_prev, ahead)
                        if has_next:
                            for f in fronts.get(u, ()):
                                f(eng, n.next())
                    if not has_next:
                        last = len(self.pv_after) - 1
                        if which == "pe":
                            self.pe_values(eng, n, last)
                            self.pe_back(eng, n)
                        elif which == "act":
                            self.act_ao(eng, n, last)
                        else:
                            self.dve_ao(eng, n, last)
                            self.dve_back(eng, n)
                image_loop(eng, step)

            def groups_at(self, n, u, has_prev):
                if u == 0:
                    return [(n.prev(), len(self.pv_after) - 1)] if has_prev else []
                return [(n, g) for g in self.pv_after.get(u - 1, ())]

            def pe_slot(self, eng, n, u, has_prev, ahead):
                self.pe_probsT(eng, n, u)
                if ahead(u, 3):
                    self.pe_scores(eng, *ahead(u, 3))
                for m, g in self.groups_at(n, u, has_prev):
                    self.pe_values(eng, m, g)
                if u == 1 and has_prev:
                    self.pe_back(eng, n.prev())

            def act_slot(self, eng, n, u, has_prev, ahead):
                if ahead(u, 2):
                    self.act_exp(eng, *ahead(u, 2))
                if self.pt_engine(u) == 0:
                    self.pt_out(eng, n, u, nc.scalar.copy)
                for m, g in self.groups_at(n, u, has_prev):
                    self.act_ao(eng, m, g)

            def dve_slot(self, eng, n, u, has_prev, ahead):
                if ahead(u, 1):
                    self.dve_norm(eng, *ahead(u, 1))
                if self.pt_engine(u) == 1:
                    self.pt_out(eng, n, u, nc.vector.tensor_copy)
                if ahead(u, 3):
                    self.dve_max(eng, *ahead(u, 3))
                for m, g in self.groups_at(n, u, has_prev):
                    self.dve_ao(eng, m, g)
                if u == 1 and has_prev:
                    self.dve_back(eng, n.prev())

            def run_pool(self, eng):
                def front(n):
                    self.norm.pool_rstd(eng, n)
                    self.pool_front(eng, n)
                front(Img(0, 0))

                def step(n, has_prev, has_next):
                    if has_next:
                        front(n.next())
                    self.pool_xbias(eng, n)
                image_loop(eng, step)

        class Attention0(Attention):
            G_USES = (6, 5)
            G_OUTS = (6, 5)

            def pt_engine(self, u):
                return 0 if self.units[u][0] == "main" else 1

            def tiles(self, u):
                return [(P, N0, N0)] * 2 if self.units[u][0] == "main" else [(P, NREM + N0, NREM)]

            def emit_scores(self, eng, n, u):
                kind, h = self.units[u]
                p = n.parity
                if u == 0:
                    eng.wait_ge(self.scat, n.at(16 * 2 * GH0, 16 * 2 * GH0))
                    eng.wait_ge(self.relscat, n.at(16 * 2 * GH0, 16 * 2 * GH0))
                if kind == "main":
                    k = K0[p][:, h, :].rearrange("k (r c) -> k r c", c=W)[:, 0:WS, 0:WS]
                    for t in range(2):
                        mm = nc.tensor.matmul(S_BANK[u % 3][:, t * N0:(t + 1) * N0],
                                              Q0[p][:, h, t * P:(t + 1) * P], k, start=True, stop=True)
                    return mm
                eng.wait_ge(self.gath, n.at(6, 6))
                land(eng, "pe")
                for j in range(2):
                    for keys, lo, hi in ((KR0[p], 0, NREM), (KP0, NREM, NREM + N0)):
                        mm = nc.tensor.matmul(S_BANK[u % 3][RPAD * j:RPAD * (j + 1), lo:hi],
                                              QR0[p][:, 2 * h + j, :], keys[:, 2 * h + j, :], start=True, stop=True)
                return mm

            def emit_probsT(self, eng, n, u):
                kind, h = self.units[u]
                pb, ptb = Pb[u % 3], PT_BANK[u % 2]
                if kind == "main":
                    for kc in range(2):
                        for t in range(2):
                            mm = nc.tensor.transpose(ptb[0:HT0, kc * T + t * P:kc * T + (t + 1) * P],
                                                     pb[:, t, kc * HT0:(kc + 1) * HT0], ident[:])
                    return mm
                return nc.tensor.transpose(ptb[0:NREM, 0:P], pb[:, 0, 0:NREM], ident[:])

            def pt_views(self, u):
                kind, h = self.units[u]
                if kind == "main":
                    return (PTm0[:, h, :, :].rearrange("p k (r c) -> p k r c", c=WS),
                            PT_BANK[u % 2][0:HT0, :].rearrange("p (k r c) -> p k r c", k=2, c=W)[:, :, 0:WS, 0:WS])
                return PTr0[:, h, :], PT_BANK[u % 2][0:NREM, 0:P]

            def pt_free(self, u):
                return 3, u // 6 - 2

            def pe_values(self, eng, n, q):
                p = n.parity
                for e in range(2):
                    eng.wait_ge(self.pt[e], n.at(self.pt_cum[e][-1], self.pt_cum[e][6 * q + 6]))
                if q == 0 and n.counts(1, 0):
                    eng.wait_ge(self.done, n.at(1, 0))
                if n.counts(9, 3 * q):
                    eng.wait_ge(self.ao[0], n.at(9, 3 * q))
                if n.counts(3, q):
                    eng.wait_ge(self.ao[1], n.at(3, q))
                for kc in range(2):
                    for j in range(4):
                        nc.tensor.matmul(O_BANK[32 * j:32 * j + 32, 0:N0], V0[p][:, kc, 4 * q + j, :],
                                         PTm0[:, 4 * q + j, kc, :], start=(kc == 0), stop=(kc == 1))
                for j in range(4):
                    mm = nc.tensor.matmul(O_BANK[32 * j:32 * j + 32, N0:T], VR0[p][:, 4 * q + j, :],
                                          PTr0[:, 2 * q + j // 2, RPAD * (j % 2):RPAD * (j % 2) + NREM],
                                          start=True, stop=True)
                mm.then_inc(self.pv, 1)

            def ao_view(self, q):
                return AO0[:, q, :].rearrange("p (r c) -> p r c", c=W)

            def act_ao(self, eng, n, q):
                eng.wait_ge(self.pv, n.at(3, q + 1))
                if n.counts(1, 0):
                    eng.wait_ge(self.y, n.at(1, 0))
                ao = self.ao_view(q)
                e = EDGE * WS
                parts = ((ao[:, 0:WS, WS:W], N0, e), (ao[:, WS:H, 0:WS], N0 + e, e),
                         (ao[:, WS:H, WS:W], N0 + 2 * e, EDGE * EDGE))
                for dst, at, k in parts:
                    nc.scalar.copy(dst, O_BANK[:, at:at + k].rearrange("p (r c) -> p r c", c=dst.shape[2]))\
                      .then_inc(self.ao[0], 1)

            def dve_ao(self, eng, n, q):
                eng.wait_ge(self.pv, n.at(3, q + 1))
                eng.wait_ge(self.ao[0], n.at(9, 3 * q + 3))
                if n.counts(1, 0):
                    eng.wait_ge(self.y, n.at(1, 0))
                nc.vector.tensor_copy(self.ao_view(q)[:, 0:WS, 0:WS],
                                      O_BANK[:, 0:N0].rearrange("p (r c) -> p r c", c=WS)).then_inc(self.ao[1], 1)

            def pe_back(self, eng, n):
                eng.wait_ge(self.ao[0], n.at(9, 9))
                eng.wait_ge(self.ao[1], n.at(3, 3))
                if n.counts(1, 0):
                    eng.wait_ge(self.done, n.at(1, 0))
                for t in range(NT):
                    for q in range(3):
                        mm = nc.tensor.matmul(Y_BANK[:, t * C:(t + 1) * C], AO0[:, q, t * P:(t + 1) * P],
                                              wproj0[:, q, :], start=(q == 0), stop=(q == 2))
                mm.then_inc(self.y, 1)

            def xn_views(self, c):
                return (xm0[:, c, :].rearrange("p (r c) -> p r c", c=WS),
                        G_BANK[c][0:CH, 0:T].rearrange("p (r c) -> p r c", c=W)[:, 0:WS, 0:WS])

            def act_xn(self, eng, n):
                eng.wait_ge(self.g_rdy[0], n.at(6, 1))
                for b in range(2):
                    if n.counts(self.G_USES[b], 0):
                        eng.wait_ge(self.g_rdy[b], n.at(self.G_USES[b], 0))
                nc.scalar.activation(*self.xn_views(0), ACT.Identity, scale=lnw[0][:, 0:1],
                                     bias=lnb[0][:, 0:1]).then_inc(self.xmain[0], 1)
                super().act_xn(eng, n)

            def dve_xn(self, eng, n):
                eng.wait_ge(self.g_rdy[1], n.at(5, 1))
                for b in range(2):
                    if n.counts(self.G_USES[b], 0):
                        eng.wait_ge(self.g_rdy[b], n.at(self.G_USES[b], 0))
                nc.vector.tensor_scalar(*self.xn_views(1), lnw[0][:, 1:2], lnb[0][:, 1:2],
                                        ALU.mult, ALU.add).then_inc(self.xmain[1], 1)
                super().dve_xn(eng, n)

            def pe_qk(self, eng, n, g):
                self.xn_ready(eng, n)
                for b in range(2):
                    self.g_free(eng, n, b, 1 + g)
                    for c in range(2):
                        mm = nc.tensor.matmul(G_BANK[b][0:CH, 0:T], wqkv0[:, c, b * C + g * CH:b * C + (g + 1) * CH],
                                              xnT[:, c, :], start=(c == 0), stop=(c == 1))
                    mm.then_inc(self.g_rdy[b], 1)

            def act_q(self, eng, n, g):
                eng.wait_ge(self.g_rdy[0], n.at(6, 2 + g))
                if g == 0:
                    if n.counts(16 * 2 * GH0, 0):
                        eng.wait_ge(self.scat, n.at(16 * 2 * GH0, 0))
                    if n.counts(6, 0):
                        eng.wait_ge(self.g_rdy[0], n.at(6, 0))
                nc.scalar.activation(self.qd[:, g, :], G_BANK[0][0:CH, 0:T], ACT.Identity,
                                     bias=qb0[:, g:g + 1]).then_inc(self.g_out[0], 1)

            def dve_k(self, eng, n, g):
                eng.wait_ge(self.g_rdy[1], n.at(5, 2 + g))
                if g == 0:
                    if n.counts(16 * 2 * GH0, 0):
                        eng.wait_ge(self.scat, n.at(16 * 2 * GH0, 0))
                nc.vector.tensor_scalar(self.kd[:, g, :], G_BANK[1][0:CH, 0:T], kb0[:, g:g + 1], D0 ** -0.5,
                                        ALU.add, ALU.mult).then_inc(self.g_out[1], 1)

            def pe_v(self, eng, n):
                for t in range(2):
                    self.g_free(eng, n, t, 4)
                    for c in range(2):
                        eng.wait_ge(self.xmain[c], n.at(1, 1))
                        mm = nc.tensor.matmul(G_BANK[t][0:HT0, 0:C], xm0[:, c, t * HT0:(t + 1) * HT0],
                                              wqkv0[:, c, 2 * C:3 * C], start=(c == 0), stop=(c == 1))
                    mm.then_inc(self.g_rdy[t], 1)
                self.g_free(eng, n, 0, 5)
                eng.wait_ge(self.xgath, n.at(3, 3))
                for c in range(2):
                    mm = nc.tensor.matmul(G_BANK[0][0:NREM, 0:C], xr0[:, c, :], wqkv0[:, c, 2 * C:3 * C],
                                          start=(c == 0), stop=(c == 1))
                mm.then_inc(self.g_rdy[0], 1)

            def act_v(self, eng, n):
                eng.wait_ge(self.g_rdy[0], n.at(6, 5))
                if n.counts(3, -3):
                    eng.wait_ge(self.pv, n.at(3, -3))
                nc.scalar.copy(V0[n.parity][:, 0, :, 0:D0], G_BANK[0][0:HT0, 0:C].rearrange("p (h d) -> p h d", d=D0))\
                  .then_inc(self.g_out[0], 1)
                eng.wait_ge(self.g_rdy[0], n.at(6, 6))
                nc.scalar.copy(VR0[n.parity][:, :, 0:D0], G_BANK[0][0:NREM, 0:C].rearrange("p (h d) -> p h d", d=D0))\
                  .then_inc(self.g_out[0], 1)

            def dve_v(self, eng, n):
                eng.wait_ge(self.g_rdy[1], n.at(5, 5))
                if n.counts(3, -3):
                    eng.wait_ge(self.pv, n.at(3, -3))
                nc.vector.tensor_copy(V0[n.parity][:, 1, :, 0:D0],
                                      G_BANK[1][0:HT0, 0:C].rearrange("p (h d) -> p h d", d=D0))\
                  .then_inc(self.g_out[1], 1)

            def pe_rel(self, eng, n, b):
                eng.wait_ge(self.g_out[0], n.at(6, 3))
                if isinstance(n.pair, int) and n.pair == 0:
                    eng.wait_ge(relw_h0_done, WS)
                    eng.wait_ge(relw_w0_done, WS)
                self.g_free(eng, n, b, 3)
                for i in range(H):
                    qv = self.qd[:, :, :].rearrange("k g (r c) -> k g r c", c=W)
                    qv = qv[:, :, i, :] if b else qv[:, :, :, i]
                    mm = nc.tensor.matmul(G_BANK[b][0:GH0 * WS, 32 * i:32 * i + 32],
                                          relw[1 - b][:, i % WS, :, :].rearrange("k h w -> k (h w)"), qv,
                                          start=True, stop=True)
                mm.then_inc(self.g_rdy[b], 1)

            def dve_rel(self, eng, n):
                eng.wait_ge(self.g_rdy[1], n.at(5, 4))
                if n.counts(16 * 2 * GH0, 0):
                    eng.wait_ge(self.relscat, n.at(16 * 2 * GH0, 0))
                m = GH0 * WS
                nc.vector.tensor_copy(self.reld[0].rearrange("p g (r c) -> p g r c", c=W),
                                      G_BANK[1][0:m, :].rearrange("p (r g c) -> p g r c", g=2, c=W)).then_inc(self.g_out[1], 1)

            def act_rel(self, eng, n):
                eng.wait_ge(self.g_rdy[0], n.at(6, 4))
                if n.counts(16 * 2 * GH0, 0):
                    eng.wait_ge(self.relscat, n.at(16 * 2 * GH0, 0))
                m = GH0 * WS
                nc.scalar.copy(self.reld[1].rearrange("p g (r c) -> p g r c", c=W),
                               G_BANK[0][0:m, :].rearrange("p (c g r) -> p g r c", g=2, r=H)).then_inc(self.g_out[0], 1)

            def sp(self, eng):
                def image(n):
                    p = n.parity
                    eng.wait_ge(self.g_out[0], n.at(6, 3))
                    land(eng, "sp")
                    eng.wait_ge(self.g_out[1], n.at(5, 3))
                    land(eng, "sp")
                    if n.counts(self.NU, -self.NU):
                        eng.wait_ge(self.s_rdy, n.at(self.NU, -self.NU))
                    land(eng, "sp")
                    if n.counts(6, -6):
                        eng.wait_ge(self.gath, n.at(6, -6))
                    land(eng, "sp")
                    for h in range(GH0):
                        for src, dst in ((self.qd, Q0), (self.kd, K0)):
                            eng.dma_start(dst[p][0:D0, h:HEADS:GH0, :], src[h * D0:(h + 1) * D0, :, :]).then_inc(self.scat, 16)
                    eng.wait_ge(self.g_out[1], n.at(5, 4))
                    land(eng, "sp")
                    eng.wait_ge(self.g_out[0], n.at(6, 4))
                    land(eng, "sp")
                    for h in range(GH0):
                        for i in range(2):
                            eng.dma_start(Q0[p][D0 + i * WS:D0 + (i + 1) * WS, h:HEADS:GH0, :],
                                          self.reld[i][h * WS:(h + 1) * WS, :, :]).then_inc(self.relscat, 16)
                image(Img(0, 0))
                image(Img(0, 1))
                with eng.Fori(1, B // 2) as pair:
                    image(Img(pair, 0))
                    image(Img(pair, 1))

            def pool_front(self, eng, n):
                p, e = n.parity, EDGE * WS
                self.xn_ready(eng, n)
                if n.counts(6, 0):
                    eng.wait_ge(self.g_rdy[0], n.at(6, 0))
                land(eng, "pool")
                cuts = ((0, e, slice(0, WS), slice(WS, W)), (e, 2 * e, slice(WS, H), slice(0, WS)),
                        (2 * e, NREM, slice(WS, H), slice(WS, W)))

                def gather(dst, src, semaphore):
                    v = src.rearrange("p h (r c) -> p h r c", c=W)
                    for lo, hi, r, c in cuts:
                        nc.gpsimd.tensor_copy(dst[:, :, lo:hi].rearrange("p h (r c) -> p h r c", c=c.stop - c.start),
                                              v[:, :, r, c]).then_inc(semaphore, 1)
                gather(xr0[:, :, :], xnT[:, :, :], self.xgath)
                eng.wait_ge(self.scat, n.at(16 * 2 * GH0, 16 * 2 * GH0))
                if n.counts(self.NU, -self.NU):
                    eng.wait_ge(self.s_rdy, n.at(self.NU, -self.NU))
                land(eng, "pool")
                gather(KR0[p][0:D0], K0[p][0:D0], self.gath)
                eng.wait_ge(self.relscat, n.at(16 * 2 * GH0, 16 * 2 * GH0))
                land(eng, "pool")
                gather(QR0[p][0:K0ROWS], Q0[p][0:K0ROWS], self.gath)

            def setup(self):
                self.qd, self.kd = dense[0][:, 0:2, :], dense[1][:, 0:2, :]
                self.reld = [dense[i][0:GH0 * WS, 2:4, :] for i in range(2)]
                self.gath = sem("a0_gather")
                self.xmain = [sem("a0_xm0"), sem("a0_xm1")]
                self.xgath = sem("a0_xgather")
                ln = lambda e, n: self.norm.dve_stats(e, n)
                xh = lambda e, n: self.norm.dve_xhat(e, n, self.g_rdy[1], 5, -4)
                q = [lambda e, n, g=g: self.pe_qk(e, n, g) for g in range(2)]
                self.pe_fronts = {2: [self.pe_transpose_x], 3: [q[0]], 5: [q[1]], 7: [lambda e, n: self.pe_rel(e, n, 1)],
                                  8: [lambda e, n: self.pe_rel(e, n, 0)], 11: [self.pe_v]}
                self.act_fronts = {2: [self.act_xn], 3: [lambda e, n: self.act_q(e, n, 0)],
                                   5: [lambda e, n: self.act_q(e, n, 1)], 8: [self.act_rel], 11: [self.act_v]}
                self.dve_fronts = {0: [ln], 1: [xh], 2: [self.dve_xn], 3: [lambda e, n: self.dve_k(e, n, 0)],
                                   5: [lambda e, n: self.dve_k(e, n, 1)], 7: [self.dve_rel], 11: [self.dve_v]}

        class Attention1(Attention):
            G_USES = (10, 10)
            G_OUTS = (11, 11)

            def pt_engine(self, u):
                return u % 4 == 3

            def tiles(self, u):
                return [(P, T, T)] * 2

            def emit_scores(self, eng, n, u):
                p = n.parity
                if u == 0:
                    eng.wait_ge(self.scat, n.at(64, 64))
                    eng.wait_ge(self.relscat, n.at(128, 128))
                for t in range(NT):
                    mm = nc.tensor.matmul(S_BANK[u % 3][:, t * T:(t + 1) * T], Q1[p][:, u, t * P:(t + 1) * P],
                                          K1[p][:, u, :], start=True, stop=True)
                return mm

            def emit_probsT(self, eng, n, u):
                for kc in range(2):
                    for t in range(NT):
                        mm = nc.tensor.transpose(PT_BANK[u % 2][:, kc * T + t * P:kc * T + (t + 1) * P],
                                                 Pb[u % 3][:, t, kc * P:(kc + 1) * P], ident[:])
                return mm

            def pt_views(self, u):
                return PT1[:, u % 4, :, :].rearrange("p k q -> p (k q)"), PT_BANK[u % 2][:, 0:2 * T]

            def pt_free(self, u):
                return NPAIR, u // 2 - 1

            def pe_values(self, eng, n, q):
                p = n.parity
                for e in range(2):
                    eng.wait_ge(self.pt[e], n.at(self.pt_cum[e][-1], self.pt_cum[e][2 * q + 2]))
                if q == 0 and n.counts(1, 0):
                    eng.wait_ge(self.done, n.at(1, 0))
                if n.counts(NPAIR, q):
                    eng.wait_ge(self.ao[0], n.at(NPAIR, q))
                for kc in range(2):
                    for j in range(2):
                        mm = nc.tensor.matmul(O_BANK[64 * j:64 * j + 64, 0:T], V1[p][:, kc, 2 * q + j, :],
                                              PT1[:, (2 * q + j) % 4, kc, :], start=(kc == 0), stop=(kc == 1))
                mm.then_inc(self.pv, 1)

            def act_ao(self, eng, n, q):
                eng.wait_ge(self.pv, n.at(NPAIR, q + 1))
                if n.counts(1, 0):
                    eng.wait_ge(self.y, n.at(1, 0))
                nc.scalar.copy(AO1[:, q, :], O_BANK[:, 0:T]).then_inc(self.ao[0], 1)

            def dve_ao(self, eng, n, q):
                pass

            def pe_back(self, eng, n):
                eng.wait_ge(self.ao[0], n.at(NPAIR, NPAIR))
                if n.counts(1, 0):
                    eng.wait_ge(self.done, n.at(1, 0))
                for t in range(NT):
                    for q in range(NPAIR):
                        mm = nc.tensor.matmul(Y_BANK[:, t * C:(t + 1) * C], AO1[:, q, t * P:(t + 1) * P],
                                              wo1[:, q, :], start=(q == 0), stop=(q == NPAIR - 1))
                mm.then_inc(self.y, 1)

            def pe_qk(self, eng, n, g):
                self.xn_ready(eng, n)
                for b, w in enumerate((wq1, wk1)):
                    self.g_free(eng, n, b, 1 + g)
                    for c in range(2):
                        mm = nc.tensor.matmul(G_BANK[b][0:CH, 0:T], w[:, c, g * CH:(g + 1) * CH], xnT[:, c, :],
                                              start=(c == 0), stop=(c == 1))
                    mm.then_inc(self.g_rdy[b], 1)

            def act_q(self, eng, n, g):
                eng.wait_ge(self.g_rdy[0], n.at(10, 2 + g))
                if g == 0:
                    if n.counts(64, 0):
                        eng.wait_ge(self.scat, n.at(64, 0))
                    if n.counts(10, 0):
                        eng.wait_ge(self.g_rdy[1], n.at(10, 0))
                nc.scalar.activation(self.qd[:, g, :], G_BANK[0][0:CH, 0:T], ACT.Identity,
                                     bias=qb1[:, g:g + 1]).then_inc(self.g_out[0], 1)

            def dve_k(self, eng, n, g):
                eng.wait_ge(self.g_rdy[1], n.at(10, 2 + g))
                if g == 0:
                    if n.counts(64, 0):
                        eng.wait_ge(self.scat, n.at(64, 0))
                nc.vector.tensor_scalar(self.kd[:, g, :], G_BANK[1][0:CH, 0:T], kb1[:, g:g + 1], D1 ** -0.5,
                                        ALU.add, ALU.mult).then_inc(self.g_out[1], 1)

            def pe_v(self, eng, n, t):
                half = HEADS * D1 // 2
                for b in range(2):
                    self.g_free(eng, n, b, 9 + t)
                    for c in range(2):
                        mm = nc.tensor.matmul(G_BANK[b][:, 0:half], xnT[:, c, t * P:(t + 1) * P],
                                              wv1[:, c, b * half:(b + 1) * half], start=(c == 0), stop=(c == 1))
                    mm.then_inc(self.g_rdy[b], 1)

            def v_views(self, n, t, b):
                return (V1[n.parity][:, t, b * NPAIR:(b + 1) * NPAIR, 0:D1],
                        G_BANK[b][:, 0:HEADS * D1 // 2].rearrange("p (h d) -> p h d", d=D1))

            def act_v(self, eng, n, t):
                eng.wait_ge(self.g_rdy[0], n.at(10, 9 + t))
                if n.counts(NPAIR, -NPAIR):
                    eng.wait_ge(self.pv, n.at(NPAIR, -NPAIR))
                nc.scalar.copy(*self.v_views(n, t, 0)).then_inc(self.g_out[0], 1)

            def dve_v(self, eng, n, t):
                eng.wait_ge(self.g_rdy[1], n.at(10, 9 + t))
                if n.counts(NPAIR, -NPAIR):
                    eng.wait_ge(self.pv, n.at(NPAIR, -NPAIR))
                nc.vector.tensor_copy(*self.v_views(n, t, 1)).then_inc(self.g_out[1], 1)

            def pe_rel(self, eng, n):
                eng.wait_ge(self.g_out[0], n.at(11, 7))
                for b in range(2):
                    self.g_free(eng, n, b, 7)
                    for i in range(8):
                        for s in range(4):
                            v = self.qd[:, 3 * (s % 2):3 * (s % 2) + 3, :].rearrange("k g (r c) -> k g r c", c=W)
                            line = 8 * b + i
                            v = v[:, :, line, :] if s < 2 else v[:, :, :, line]
                            mm = nc.tensor.matmul(G_BANK[b][32 * s:32 * s + 32, 48 * i:48 * i + 48],
                                                  relw[2 + s // 2][:, line, :, :].rearrange("k a b -> k (a b)"), v,
                                                  start=True, stop=True)
                    mm.then_inc(self.g_rdy[b], 1)

            def rel_views(self, b, s):
                rows = slice(64 * s, 64 * s + 64)
                src = G_BANK[b][rows, 0:8 * 48]
                dst = self.reld[rows, :, :].rearrange("p g (r c) -> p g r c", c=W)
                if s == 0:
                    return dst[:, :, 8 * b:8 * b + 8, :], src.rearrange("p (r g c) -> p g r c", g=3, c=W)
                return dst[:, :, :, 8 * b:8 * b + 8], src.rearrange("p (c g r) -> p g r c", g=3, r=H)

            def act_rel(self, eng, n):
                eng.wait_ge(self.g_rdy[0], n.at(10, 8))
                if n.counts(128, 0):
                    eng.wait_ge(self.relscat, n.at(128, 0))
                for s in range(2):
                    nc.scalar.copy(*self.rel_views(0, s)).then_inc(self.g_out[0], 1)

            def dve_rel(self, eng, n):
                eng.wait_ge(self.g_rdy[1], n.at(10, 8))
                if n.counts(128, 0):
                    eng.wait_ge(self.relscat, n.at(128, 0))
                for s in range(2):
                    nc.vector.tensor_copy(*self.rel_views(1, s)).then_inc(self.g_out[1], 1)

            def sp(self, eng):
                def image(n):
                    p = n.parity
                    if n.counts(self.NU, -self.NU):
                        eng.wait_ge(self.s_rdy, n.at(self.NU, -self.NU))
                    land(eng, "sp")
                    eng.wait_ge(self.g_out[0], n.at(11, 7))
                    land(eng, "sp")
                    for j in range(2):
                        eng.dma_start(Q1[p][0:D1, j:HEADS:2, :], self.qd[D1 * j:D1 * (j + 1), :, :]).then_inc(self.scat, 16)
                    eng.wait_ge(self.g_out[1], n.at(11, 7))
                    land(eng, "sp")
                    for j in range(2):
                        eng.dma_start(K1[p][0:D1, j:HEADS:2, :], self.kd[D1 * j:D1 * (j + 1), :, :]).then_inc(self.scat, 16)
                    for b in range(2):
                        eng.wait_ge(self.g_out[b], n.at(11, 9))
                        land(eng, "sp")
                    for s in range(4):
                        for j in range(2):
                            at = K1REL + H * (s // 2)
                            first = 6 * (s % 2) + j
                            eng.dma_start(Q1[p][at:at + H, first:first + 5:2, :],
                                          self.reld[32 * s + H * j:32 * s + H * (j + 1), :, :]).then_inc(self.relscat, 16)
                image(Img(0, 0))
                image(Img(0, 1))
                with eng.Fori(1, B // 2) as pair:
                    image(Img(pair, 0))
                    image(Img(pair, 1))

            def pool_front(self, eng, n):
                pass

            def setup(self):
                self.qd, self.kd, self.reld = dense[0][:], dense[1][:], rel_dense[:]
                ln = lambda e, n: self.norm.dve_stats(e, n)
                xh = lambda e, n: self.norm.dve_xhat(e, n, self.g_rdy[1], 10, -9)

                def each(f, ks):
                    return [lambda e, n, k=k: f(e, n, k) for k in ks]
                self.pe_fronts = {2: [self.pe_transpose_x], 3: each(self.pe_qk, (0, 1, 2)), 4: each(self.pe_qk, (3, 4)),
                                  5: each(self.pe_qk, (5,)) + [self.pe_rel], 8: each(self.pe_v, (0,)),
                                  9: each(self.pe_v, (1,))}
                self.act_fronts = {2: [self.act_xn], 3: each(self.act_q, (0, 1, 2)), 4: each(self.act_q, (3, 4)),
                                   5: each(self.act_q, (5,)), 6: [self.act_rel], 8: each(self.act_v, (0,)),
                                   9: each(self.act_v, (1,))}
                self.dve_fronts = {0: [ln], 1: [xh], 2: [self.dve_xn], 3: each(self.dve_k, (0, 1, 2)),
                                   4: each(self.dve_k, (3, 4)), 5: each(self.dve_k, (5,)), 6: [self.dve_rel],
                                   8: each(self.dve_v, (0,)), 9: each(self.dve_v, (1,))}

        a0 = Attention0(0, lambda n: (ld_x, 16), xdone[0], L0_UNITS, {6 * q + 5: [q] for q in range(3)})
        m0 = Mlp(0, ACT.Gelu, xdone[0], xdone[1], False)
        a1 = Attention1(1, lambda n: (xdone[1], n.at(1, 1)), xdone[2], [("main", h) for h in range(HEADS)],
                        {2 * q + 1: [q] for q in range(NPAIR)})
        m1 = Mlp(1, ACT.Gelu_apprx_tanh, xdone[2], xdone[3], True)
        a0.setup()
        a1.setup()
        stages = (a0, m0, a1, m1)

        def stage_start(eng, i):
            if i:
                eng.wait_ge(xdone[i - 1], B)

        ctx.enter_context(nc.allow_non_contiguous_dma(reason="bias vectors to columns, a few KB once"))
        block = ctx.enter_context(nc.Block())

        zero_dve = [K1[0], KP0, V0[0], V0[1]]
        zero_pool = [vb0, vb1, wproj0, wo1, KR0[0], KR0[1], QR0[0], QR0[1], K1[1]]
        zero_more = [VR0[0], VR0[1], Q1[0], Q1[1]]
        NZ = len(zero_dve) + len(zero_pool)
        vbc = [area[:, 0:3 * P].rearrange("p (q m) -> p q m", q=3),
               area[:, 3 * P:(3 + NPAIR) * P].rearrange("p (q m) -> p q m", q=NPAIR)]
        tab_bank = O_BANK
        relw_spec = ((WS, GH0, blk0), (WS, GH0, blk0), (H, 2, blk1), (W, 2, blk1))

        def spread(engine, i):
            win, heads, blk = relw_spec[i]
            for line in range(win):
                row = reltab[i][:, win - 1 - line:2 * win - 1 - line]
                yield engine.tensor_tensor(relw[i][:, line, :, :], row.unsqueeze(1).broadcast_to([CH, heads, win]),
                                           blk[:].unsqueeze(2).broadcast_to([CH, heads, win]), ALU.mult)

        def table_products(layer):
            for i in (2 * layer, 2 * layer + 1):
                n = reltab[i].shape[1]
                nc.tensor.matmul(tab_bank[0:CH, 32 * i:32 * i + n], relnat[i].rearrange("r h d -> r (h d)"),
                                 (flip, flip27)[layer == 0][:], start=True, stop=True).then_inc(prep_pe, 1)

        def pe_meanwhile(pe):
            pe.wait_ge(ld_w, 16 * len(rest))
            table_products(1)
            pe.wait_ge(prep_dve, 4)
            pe.wait_ge(prep_dve, 6)
            for l, (w, k) in enumerate(((wproj0, 3), (wo1, NPAIR))):
                for q in range(k):
                    mm = nc.tensor.matmul(O_BANK[:, l * C:(l + 1) * C], vbc[l][:, q, :], w[:, q, :],
                                          start=(q == 0), stop=(q == k - 1))
                mm.then_inc(prep_pe, 1)
            pe.wait_ge(obias_done, 2)
            pe.wait_ge(kpad_done, 1)

        def dve_meanwhile(dve):
            dve.wait_ge(prep_pe, 4)
            for i in (2, 3):
                nc.vector.tensor_copy(reltab[i][:], tab_bank[0:CH, 32 * i:32 * i + 31]).then_inc(prep_dve, 1)
            dve.wait_ge(ld_c, 16 * len(late))
            for l, (v, k) in enumerate(((vb0, 3), (vb1, NPAIR))):
                nc.vector.tensor_copy(vbc[l], v[:].unsqueeze(2).broadcast_to([P, k, P])).then_inc(prep_dve, 1)
            nc.vector.tensor_scalar(KP0[0:D0], kpad0[:].unsqueeze(2).broadcast_to([D0, HEADS, N0]), D0 ** -0.5, None,
                                    ALU.mult).then_inc(kpad_done, 1)
            dve.wait_ge(prep_pe, 6)
            dve.wait_ge(ld_w, 16 * len(rest))
            for l in range(2):
                nc.vector.tensor_tensor(obias[l][:], O_BANK[:, l * C:(l + 1) * C], obias[l][:], ALU.add)\
                  .then_inc(obias_done, 1)

        def dve_tables1(dve):
            dve.wait_ge(prep_dve, 4)
            for i in (2, 3):
                for instruction in spread(nc.vector, i):
                    instruction.then_inc(relw_done, 1)

        @block.sync
        def _(sp):
            sp.dma_start(x_all[:], x_view).then_inc(ld_x, 16)
            for dst, src in first:
                sp.dma_start(dst, src).then_inc(ld_first, 16)
            sp.wait_ge(zeroed, NZ)
            for dst, src in late:
                sp.dma_start(dst, src).then_inc(ld_c, 16)
            for dst, src in rest:
                sp.dma_start(dst, src).then_inc(ld_w, 16)
            sp.wait_ge(zeroed_more, len(zero_more))
            a0.sp(sp)
            stage_start(sp, 2)
            a1.sp(sp)
            with sp.Fori(0, B) as n:
                sp.wait_ge(xdone[3], n + 1)
                sp.dma_start(out_view[:, bass.ds(n * NT, NT), :], x_all[:, bass.ds(n * NT, NT), :]).then_inc(out_done, 16)
            sp.wait_ge(out_done, 16 * B)

        @block.gpsimd
        def _(pool):
            nc.gpsimd.memset(mhalf[:], -0.5).then_inc(prep_pool, 1)
            for z in zero_pool:
                nc.gpsimd.memset(z[:], 0.0).then_inc(zeroed, 1)
            pool.wait_ge(prep_dve, 2)
            pool.wait_ge(ld_first, 16 * len(first))
            for instruction in spread(nc.gpsimd, 1):
                instruction.then_inc(relw_w0_done, 1)
            for z in zero_more:
                nc.gpsimd.memset(z[:], 0.0).then_inc(zeroed_more, 1)
            pool.wait_ge(prep_pool, 1)
            pool.wait_ge(ld_c, 16 * len(late))
            for i, s in enumerate(stages):
                stage_start(pool, i)
                if i == 2:
                    for v in V1:
                        nc.gpsimd.memset(v[:, :, :, D1:64], 0.0).then_inc(prep_pool, 1)
                s.run_pool(pool)

        @block.tensor
        def _(pe):
            pe.wait_ge(ld_first, 16 * len(first))
            table_products(0)
            a0.run(pe, "pe", pe_meanwhile)
            stage_start(pe, 1)
            m0.run(pe, "pe")
            stage_start(pe, 2)
            pe.wait_ge(prep_pool, 3)
            pe.wait_ge(relw_done, H + W)
            a1.run(pe, "pe")
            stage_start(pe, 3)
            m1.run(pe, "pe")

        @block.scalar
        def _(act):
            act.wait_ge(ld_first, 16 * len(first))
            act.wait_ge(zeroed, NZ)
            act.wait_ge(zeroed_more, len(zero_more))
            for i, s in enumerate(stages):
                stage_start(act, i)
                if i == 1:
                    act.wait_ge(ld_w, 16 * len(rest))
                s.run(act, "act")

        @block.vector
        def _(dve):
            for z in zero_dve:
                nc.vector.memset(z[:], 0.0).then_inc(zeroed, 1)
            dve.wait_ge(zeroed, NZ)
            dve.wait_ge(ld_first, 16 * len(first))
            dve.wait_ge(prep_pe, 2)
            for i in (0, 1):
                nc.vector.tensor_copy(reltab[i][:], tab_bank[0:CH, 32 * i:32 * i + 27]).then_inc(prep_dve, 1)
            dve.wait_ge(prep_dve, 2)
            for instruction in spread(nc.vector, 0):
                instruction.then_inc(relw_h0_done, 1)
            a0.run(dve, "dve", dve_meanwhile)
            stage_start(dve, 1)
            m0.run(dve, "dve", dve_tables1)
            stage_start(dve, 2)
            a1.run(dve, "dve")
            stage_start(dve, 3)
            m1.run(dve, "dve")


def shape_constants():
    c = {"c_ident": np.eye(P), "c_flip31": np.eye(31)[::-1], "c_flip27": np.eye(27)[::-1]}
    ch = np.arange(CH)
    c["c_blk0"] = ch[:, None] // D0 == np.arange(GH0)
    c["c_blk1"] = ch[:, None] // D1 == np.arange(2)
    t = np.arange(T)
    c["c_hot0"] = np.concatenate([np.arange(WS)[:, None] == (t // W) % WS, np.arange(WS)[:, None] == (t % W) % WS])
    c["c_hot1"] = np.concatenate([np.arange(H)[:, None] == t // W, np.arange(W)[:, None] == t % W])
    grid = t.reshape(H, W)
    parts = [grid[:WS, WS:].ravel(), grid[WS:, :WS].ravel(), grid[WS:, WS:].ravel()]
    rem = np.concatenate(parts)
    window = np.repeat(np.arange(3), [len(p) for p in parts])
    mask = np.where(np.arange(3)[:, None] == window, 0.0, NEG)
    c["c_hotrem"] = np.concatenate([c["c_hot0"][:, rem], mask])
    c["c_qwin"] = np.concatenate([np.arange(3)[:, None] == window, np.zeros((3, RPAD - NREM))], axis=1)
    kh, kw = np.arange(N0) // WS, np.arange(N0) % WS
    pad = [kw >= EDGE, kh >= EDGE, (kh >= EDGE) | (kw >= EDGE)]
    c["c_hotpad"] = np.concatenate([np.arange(WS)[:, None] == kh, np.arange(WS)[:, None] == kw,
                                    np.where(np.stack(pad), 0.0, NEG)])
    return {k: np.ascontiguousarray(v, dtype=np.float32) for k, v in c.items()}


def kernel(**inputs):
    import concourse.bacc as bacc
    from concourse.bass_utils import run_bass_kernel_spmd

    nc = bacc.Bacc("TRN2", target_bir_lowering=False, num_devices=1)
    arrays = {k: np.ascontiguousarray(v) for k, v in inputs.items()}
    arrays.update(shape_constants())
    arrays = {f"in_{k}": v for k, v in arrays.items()}
    aps = {k[3:]: nc.dram_tensor(k, v.shape, mybir.dt.from_np(v.dtype), kind="ExternalInput").ap()
           for k, v in arrays.items()}
    out = nc.dram_tensor("out", (B, H, W, C), F32, kind="ExternalOutput").ap()
    build(nc, aps, out)
    r = run_bass_kernel_spmd(nc, [arrays], core_ids=[0])
    return r.results[0]["out"]
```

```python
from contextlib import ExitStack

import numpy as np

import concourse.bass as bass
from concourse import mybir

F32 = mybir.dt.float32
F32R = mybir.dt.float32r
ALU = mybir.AluOpType
ACT = mybir.ActivationFunctionType
AX = mybir.AxisListType

P = 128
B, H, W, C = 8, 16, 16, 192
T = H * W
NT = T // P
CH = C // 2
MLP = 4 * C
NM = MLP // P
EPS = 1e-5
HEADS = 12
WS = 14
D0 = C // HEADS
D1 = 48
GH0 = CH // D0
NPAIR = HEADS // 2
N0 = WS * WS
HT0 = N0 // 2
NREM = T - N0
EDGE = H - WS
RPAD = 64
K0ROWS = D0 + 2 * WS
KR0ROWS = K0ROWS + 3
K1REL = 64
K1ROWS = K1REL + 2 * H
NEG = -1.0e30
L0_UNITS = [("main", 4 * q + j) if s == 0 else ("rem", 2 * q + j)
            for q in range(3) for s, j in ((0, 0), (0, 1), (1, 0), (0, 2), (0, 3), (1, 1))]


class Img:

    def __init__(self, pair, par):
        self.pair, self.par = pair, par

    def at(self, per, k):
        return self.pair * (2 * per) + (self.par * per + k)

    def counts(self, per, k):
        value = self.at(per, k)
        return not isinstance(value, int) or value > 0

    def index0(self):
        return isinstance(self.pair, int) and self.pair == 0 and self.par == 0

    @property
    def parity(self):
        return self.par % 2

    def next(self):
        return Img(self.pair, self.par + 1)

    def prev(self):
        return Img(self.pair, self.par - 1)


def image_loop(eng, step):
    step(Img(0, 0), False, True)
    step(Img(0, 1), True, True)
    with eng.Fori(1, B // 2 - 1) as pair:
        step(Img(pair, 0), True, True)
        step(Img(pair, 1), True, True)
    step(Img(B // 2 - 1, 0), True, True)
    step(Img(B // 2 - 1, 1), True, False)


def each(step, indices):
    return [lambda eng, n, k=k: step(eng, n, k) for k in indices]


def mlp_loop(eng, step):
    step(Img(0, 0), True, True)
    step(Img(0, 1), True, True)
    with eng.Fori(1, B // 2 - 1) as pair:
        step(Img(pair, 0), True, True)
        step(Img(pair, 1), True, True)
    step(Img(B // 2 - 1, 0), True, False)
    step(Img(B // 2 - 1, 1), False, False)


def build(nc, a, out):
    with ExitStack() as ctx:
        def sb(name, shape, dt=F32):
            return ctx.enter_context(nc.sbuf_tensor(name, shape, dt))

        def lent(name, shape):
            with nc.sbuf_tensor(name, shape, F32) as buffer:
                return buffer

        def whole_and_low(name, shape):
            return lent(name, shape), sb(name + "_low", shape, F32R)

        def sem(name):
            return ctx.enter_context(nc.semaphore(name))

        bank = [ctx.enter_context(nc.psum_tensor(f"bank{i}", [P, 512], F32)) for i in range(8)]
        S_BANK, PT_BANK, O_BANK, G_BANK = bank[0:3], bank[3:5], bank[5], bank[6:8]
        Y_BANK = O_BANK

        x_all = sb("x_all", [P, B * NT, C])
        x_view = a["x"].rearrange("b (t r) w c -> (r w) (b t) c", t=NT)
        out_view = out.rearrange("b (t r) w c -> (r w) (b t) c", t=NT)
        ident = sb("ident", [P, P])

        early_sizes = {"KP0": HEADS * N0, "QR0_0": HEADS * RPAD, "QR0_1": HEADS * RPAD, "KR0_0": HEADS * NREM,
                       "KR0_1": HEADS * NREM, "V0_0": 2 * HEADS * 32, "V0_1": 2 * HEADS * 32,
                       "VR0_0": HEADS * 32, "VR0_1": HEADS * 32,
                       "relw_h0": WS * GH0 * WS, "relw_w0": WS * GH0 * WS}
        early = lent("early", [P, sum(early_sizes.values())])
        late_shapes = {"fc1_0": (CH, 2, MLP), "fc1_1": (CH, 2, MLP),
                       "wq1": (CH, 2, HEADS * D1), "wk1": (CH, 2, HEADS * D1), "wv1": (CH, 2, HEADS * D1)}
        high = {name: sb(f"{name}_high", list(shape), F32R) for name, shape in late_shapes.items()}
        relw1 = [sb("relw_h1", [CH, H, 2, H]), sb("relw_w1", [CH, W, 2, W])]
        sb("early_rest", [P, sum(early_sizes.values()) - sum(s_[1] * s_[2] for s_ in late_shapes.values()) - 2 * H * 2 * H])

        def carve(rows, name, *shape):
            at = sum(list(early_sizes.values())[:list(early_sizes).index(name)])
            view = early[0:rows, at:at + early_sizes[name]]
            letters = "abc"[:len(shape)]
            return view.rearrange(f"p ({' '.join(letters)}) -> p {' '.join(letters)}", **dict(zip(letters, shape)))

        wqkv0 = sb("wqkv0", [CH, 2, 3 * C])
        wproj0 = sb("wproj0", [P, 3, C])
        fc1w, fc1_low = zip(*(whole_and_low(f"fc1w{l}", [CH, 2, MLP]) for l in range(2)))
        fc2w = [sb(f"fc2w{l}", [P, NM, C]) for l in range(2)]
        wq1, wq1_low = whole_and_low("wq1", [CH, 2, HEADS * D1])
        wk1, wk1_low = whole_and_low("wk1", [CH, 2, HEADS * D1])
        wv1, wv1_low = whole_and_low("wv1", [CH, 2, HEADS * D1])
        wo1 = sb("wo1", [P, NPAIR, C])
        lnw = [sb(f"lnw{i}", [CH, 2]) for i in range(4)]
        lnb = [sb(f"lnb{i}", [CH, 2]) for i in range(4)]
        qb0 = sb("qb0", [CH, 2])
        kb0 = sb("kb0", [CH, 2])
        kpad0 = sb("kpad0", [D0, HEADS])
        qb1 = sb("qb1", [CH, NPAIR])
        kb1 = sb("kb1", [CH, NPAIR])
        fc1b = [sb(f"fc1b{l}", [P, NM]) for l in range(2)]
        vb0 = sb("vb0", [P, 3])
        vb1 = sb("vb1", [P, NPAIR])
        obias = [sb(f"obias{l}", [P, C]) for l in range(2)]
        fc2b = [sb(f"fc2b{l}", [P, C]) for l in range(2)]
        flip = sb("flip", [31, 31])
        flip27 = sb("flip27", [27, 27])
        reltab = [sb("reltab_h0", [CH, 27]), sb("reltab_w0", [CH, 27]),
                  sb("reltab_h1", [CH, 31]), sb("reltab_w1", [CH, 31])]
        blk0 = sb("blk0", [CH, GH0])
        blk1 = sb("blk1", [CH, 2])
        relw = [carve(CH, "relw_h0", WS, GH0, WS), carve(CH, "relw_w0", WS, GH0, WS)] + relw1
        fc1s = [(fc1w[l][:], high[f"fc1_{l}"][:], fc1_low[l][:]) for l in range(2)]
        wq1s = (wq1[:], high["wq1"][:], wq1_low[:])
        wk1s = (wk1[:], high["wk1"][:], wk1_low[:])
        wv1s = (wv1[:], high["wv1"][:], wv1_low[:])

        def three(a_parts, b_parts):
            return (a_parts[1], b_parts[1]), (a_parts[1], b_parts[2]), (a_parts[2], b_parts[1])

        lnst = sb("lnst", [P, NT, 6])
        lnag = sb("lnag", [P, NT, 2])
        lnve = sb("lnve", [P, NT])
        lnrs = sb("lnrs", [P, NT])
        mhalf = sb("mhalf", [P, NT])
        xhat = sb("xhat", [P, NT, C])
        xnT, xnL = whole_and_low("xnT", [CH, 2, T])
        xnH = sb("xnH", [CH, 2, T], F32R)
        xns = (xnT[:], xnH[:], xnL[:])
        xbias = sb("xbias", [P, NT, C])

        Q1 = [sb(f"Q_{i}", [K1ROWS, HEADS, T]) for i in range(2)]
        K1 = [sb(f"K_{i}", [K1ROWS, HEADS, T]) for i in range(2)]
        Q0, K0 = Q1, K1
        dense = [sb("dense_q", [CH, NPAIR, T]), sb("dense_k", [CH, NPAIR, T])]
        rel_dense = sb("rel_dense", [P, 3, T])
        QR0 = [carve(K1ROWS, f"QR0_{i}", HEADS, RPAD) for i in range(2)]
        KR0 = [carve(K1ROWS, f"KR0_{i}", HEADS, NREM) for i in range(2)]
        KP0 = carve(K1ROWS, "KP0", HEADS, N0)
        xr0 = sb("xr0", [CH, 2, NREM])
        xm0 = rel_dense[0:CH].rearrange("p g t -> p (g t)")[:, 0:2 * N0].rearrange("p (c t) -> p c t", c=2)
        V0 = [carve(HT0, f"V0_{i}", 2, HEADS, 32) for i in range(2)]
        VR0 = [carve(NREM, f"VR0_{i}", HEADS, 32) for i in range(2)]
        area = sb("area", [P, 2 * NT * HEADS * 64 + (8 + NPAIR) * T])
        PTm0 = area[0:HT0, 0:HEADS * 2 * N0].rearrange("p (h k q) -> p h k q", h=HEADS, k=2)
        hT = [area[:, i * NM * T:(i + 1) * NM * T].rearrange("p (m t) -> p m t", m=NM) for i in range(2)]
        V1 = [area[:, i * 1536:(i + 1) * 1536].rearrange("p (t h d) -> p t h d", t=NT, h=HEADS) for i in range(2)]
        PT1 = area[:, 3072:3072 + 8 * T].rearrange("p (b k q) -> p b k q", b=4, k=2)
        AO1 = area[:, 3072 + 8 * T:3072 + (8 + NPAIR) * T].rearrange("p (q t) -> p q t", q=NPAIR)
        PTr0 = area[0:NREM, HEADS * 2 * N0:HEADS * 2 * N0 + NPAIR * P].rearrange("p (h q) -> p h q", h=NPAIR)
        AO0 = area[:, HEADS * 2 * N0 + NPAIR * P:HEADS * 2 * N0 + NPAIR * P + 3 * T].rearrange("p (q t) -> p q t", q=3)

        relnat = []
        for i, (n, rep, d) in enumerate(((27, GH0, D0), (27, GH0, D0), (31, 2, D1), (31, 2, D1))):
            relnat.append(area[0:n, (16 + i) * P:(16 + i) * P + rep * d].rearrange("r (h d) -> r h d", d=d))

        nmax = sb("nmax", [P, 3, 2])
        esum = sb("esum", [P, 3, 2])
        rsum = sb("rsum", [P, 3, 2])
        Pb = [sb(f"Pb{i}", [P, 2, T]) for i in range(3)]

        ld_x0 = sem("ld_x0")
        ld_x = sem("ld_x")
        ld_norm = sem("ld_norm")
        ld_first = sem("ld_first")
        ld_w = sem("ld_w")
        ld_later = sem("ld_later")
        ld_zeroed = sem("ld_zeroed")
        ld_odd = sem("ld_odd")
        zeroed = sem("zeroed")
        zeroed_more = sem("zeroed_more")
        prep_pe = sem("prep_pe")
        prep_dve = sem("prep_dve")
        prep_pool = sem("prep_pool")
        relw_h0_done = sem("relw_h0_done")
        relw_w0_done = sem("relw_w0_done")
        relw_done = sem("relw_done")
        kpad_done = sem("kpad_done")
        obias_done = sem("obias_done")
        w1_high = sem("w1_high")
        w1_low = sem("w1_low")
        out_done = sem("out_done")
        xdone = [sem(f"xdone{i}") for i in range(4)]

        def col(v, n, off=0, p=CH):
            return v[off:off + p * n].rearrange("(c p) -> p c", p=p)

        def bcast(v, n=P):
            return v.partition_broadcast(n)

        def norm_loads(i, w_, b_):
            return [(lnw[i][:], col(a[w_], 2)), (lnb[i][:], col(a[b_], 2))]

        def table_loads(i, name):
            r_, rep, d = relnat[i].shape
            return [(relnat[i], a[name].unsqueeze(1).broadcast_to([r_, rep, d]))]

        qkvb = a["L0_conv_qkv_b"]
        for_norm = [(ident[:], a["c_ident"])] + norm_loads(0, "L0_conv_norm1_w", "L0_conv_norm1_b")
        first = [(flip27[:], a["c_flip27"]), (blk0[:], a["c_blk0"])]
        first += table_loads(0, "L0_conv_rel_pos_h") + table_loads(1, "L0_conv_rel_pos_w")
        first += [(wqkv0[:], a["L0_conv_qkv_w"].rearrange("(c p) n -> p c n", p=CH)),
                  (qb0[:], col(qkvb, 2)), (kb0[:], col(qkvb, 2, C)),
                  (kpad0[:], qkvb[C:2 * C].rearrange("(h d) -> d h", d=D0))]
        rest = [(flip[:], a["c_flip31"]), (blk1[:], a["c_blk1"])]
        rest += table_loads(2, "L1_conv_rel_pos_0") + table_loads(3, "L1_conv_rel_pos_1")
        rest += [(obias[0][:], bcast(a["L0_conv_proj_b"])), (obias[1][:], bcast(a["L1_conv_bo"]))]
        later = [(fc1w[0][:], a["L0_conv_fc1_w"].rearrange("(c p) n -> p c n", p=CH)),
                 (fc2w[0][:], a["L0_conv_fc2_w"].rearrange("(m p) n -> p m n", p=P)),
                 (wq1[:], a["L1_conv_wq"].rearrange("(c p) n -> p c n", p=CH)),
                 (wk1[:], a["L1_conv_wk"].rearrange("(c p) n -> p c n", p=CH)),
                 (wv1[:], a["L1_conv_wv"].rearrange("(c p) n -> p c n", p=CH)),
                 (fc1w[1][:], a["L1_conv_w1"].rearrange("(c p) n -> p c n", p=CH)),
                 (fc2w[1][:], a["L1_conv_w2"].rearrange("(m p) n -> p m n", p=P)),
                 (qb1[:], col(a["L1_conv_bq"], NPAIR)), (kb1[:], col(a["L1_conv_bk"], NPAIR)),
                 (fc1b[0][:], col(a["L0_conv_fc1_b"], NM, p=P)), (fc1b[1][:], col(a["L1_conv_b1"], NM, p=P)),
                 (fc2b[0][:], bcast(a["L0_conv_fc2_b"])), (fc2b[1][:], bcast(a["L1_conv_b2"]))]
        later += norm_loads(1, "L0_conv_norm2_w", "L0_conv_norm2_b")
        later += norm_loads(2, "L1_conv_ln1_scale", "L1_conv_ln1_offset")
        later += norm_loads(3, "L1_conv_ln2_scale", "L1_conv_ln2_offset")

        late = []
        for j in range(4):
            late.append((wproj0[32 * j:32 * j + D0, :, :],
                         a["L0_conv_proj_w"].rearrange("(q j d) n -> j d q n", j=4, d=D0)[j]))
            late.append((vb0[32 * j:32 * j + D0, :], qkvb[2 * C:].rearrange("(q j d) -> j d q", j=4, d=D0)[j]))
        for j in range(2):
            late.append((wo1[64 * j:64 * j + D1, :, :],
                         a["L1_conv_wo"].rearrange("(q j d) n -> j d q n", j=2, d=D1)[j]))
            late.append((vb1[64 * j:64 * j + D1, :], a["L1_conv_bv"].rearrange("(q j d) -> j d q", j=2, d=D1)[j]))

        def per_head(v):
            return v.unsqueeze(1).broadcast_to([v.shape[0], HEADS, v.shape[1]])

        late.append((KP0[D0:KR0ROWS], per_head(a["c_hotpad"])))

        def constant_rows(i):
            return [(K1[i][D0:K0ROWS], per_head(a["c_hot0"])), (K1[i][K1REL:K1ROWS], per_head(a["c_hot1"])),
                    (KR0[i][D0:KR0ROWS], per_head(a["c_hotrem"])), (QR0[i][K0ROWS:KR0ROWS], per_head(a["c_qwin"]))]
        late += constant_rows(0)
        late_odd = constant_rows(1)

        landed = {e: sem(f"landed_{e}") for e in ("pe", "dve", "pool", "sp")}

        def land(eng, name):
            eng.sem_inc(landed[name], 1)

        class Norm:
            def __init__(self, l, x_before):
                self.l, self.x_before = l, x_before
                self.stats = sem(f"ln_stats{l}")
                self.eps = sem(f"ln_eps{l}")
                self.rstd = sem(f"ln_rstd{l}")
                self.xhat = sem(f"ln_xhat{l}")

            def dve_stats(self, eng, n):
                s, v = self.x_before(n)
                eng.wait_ge(s, v)
                for t in range(NT):
                    nc.vector.bn_stats(lnst[:, t, :], self.x(n, t)).then_inc(self.stats, 1)
                eng.wait_ge(self.stats, n.at(2 * NT, NT))
                land(eng, "dve")
                for t in range(NT):
                    nc.vector.bn_aggr(lnag[:, t, :], lnst[:, t, :]).then_inc(self.stats, 1)

            def x(self, n, t):
                return x_all[:, bass.ds(n.at(NT, t), 1), :].rearrange("p a c -> p (a c)")

            def pool_rstd(self, eng, n):
                eng.wait_ge(self.stats, n.at(2 * NT, 2 * NT))
                land(eng, "pool")
                nc.gpsimd.tensor_scalar(lnve[:], lnag[:, :, 1], EPS, None, ALU.add).then_inc(self.eps, 1)
                eng.wait_ge(self.eps, n.at(1, 1))
                nc.gpsimd.tensor_tensor(lnrs[:], lnve[:], mhalf[:], ALU.pow).then_inc(self.rstd, 1)

            def dve_xhat(self, eng, n, transposed, per, k):
                eng.wait_ge(self.rstd, n.at(1, 1))
                if n.counts(per, k):
                    eng.wait_ge(transposed, n.at(per, k))
                for t in range(NT):
                    nc.vector.tensor_scalar(xhat[:, t, :], self.x(n, t), lnag[:, t, 0:1], lnrs[:, t:t + 1],
                                            ALU.subtract, ALU.mult).then_inc(self.xhat, 1)

        class Mlp:
            def __init__(self, l, func, x_sem, done, last):
                self.l, self.func, self.done, self.last = l, func, done, last
                self.norm = Norm(2 * l + 1, lambda n: (x_sem, n.at(1, 1)))
                self.xt = [sem(f"m{l}_xt{c}") for c in range(2)]
                self.xn = [sem(f"m{l}_xn{c}") for c in range(2)]
                self.xl = sem(f"m{l}_xl")
                self.whi = sem(f"m{l}_whi")
                self.wlo = sem(f"m{l}_wlo")
                self.h = sem(f"m{l}_h")
                self.g = sem(f"m{l}_g")
                self.y = sem(f"m{l}_y")
                self.xb = sem(f"m{l}_xb")
                self.hbank = [S_BANK[0], S_BANK[1], PT_BANK[0], PT_BANK[1]]

            def act_weights(self, eng):
                whole, high, _ = fc1s[self.l]
                for half in (slice(0, MLP // 2), slice(MLP // 2, MLP)):
                    nc.scalar.copy(high[:, :, half], whole[:, :, half]).then_inc(self.whi, 1)

            def low_weights(self, eng, engine):
                whole, high, low = fc1s[self.l]
                for i, half in enumerate((slice(0, MLP // 2), slice(MLP // 2, MLP))):
                    eng.wait_ge(self.whi, i + 1)
                    engine.tensor_tensor(low[:, :, half], whole[:, :, half], high[:, :, half].bitcast(F32),
                                         ALU.subtract).then_inc(self.wlo, 1)

            def pe_norm(self, eng, n):
                for c in range(2):
                    if n.counts(2, 0):
                        eng.wait_ge(self.xn[c], n.at(2, 0))
                    for t in range(NT):
                        eng.wait_ge(self.norm.xhat, n.at(NT, t + 1))
                        mm = nc.tensor.transpose(G_BANK[c][0:CH, t * P:(t + 1) * P],
                                                 xhat[:, t, c * CH:(c + 1) * CH], ident[:])
                    mm.then_inc(self.xt[c], 1)

            def act_norm(self, eng, n):
                eng.wait_ge(self.xt[0], n.at(1, 1))
                if n.counts(NM, 0):
                    eng.wait_ge(self.h, n.at(NM, 0))
                for dst in (xnT, xnH):
                    nc.scalar.activation(dst[:, 0, :], G_BANK[0][0:CH, 0:T], ACT.Identity,
                                         scale=lnw[2 * self.l + 1][:, 0:1], bias=lnb[2 * self.l + 1][:, 0:1])\
                      .then_inc(self.xn[0], 1)

            def dve_norm(self, eng, n):
                eng.wait_ge(self.xt[1], n.at(1, 1))
                if n.counts(NM, 0):
                    eng.wait_ge(self.h, n.at(NM, 0))
                for dst in (xnT, xnH):
                    nc.vector.tensor_scalar(dst[:, 1, :], G_BANK[1][0:CH, 0:T], lnw[2 * self.l + 1][:, 1:2],
                                            lnb[2 * self.l + 1][:, 1:2], ALU.mult, ALU.add).then_inc(self.xn[1], 1)
                for c in range(2):
                    eng.wait_ge(self.xn[c], n.at(2, 2))
                nc.vector.tensor_tensor(xns[2], xns[0], xns[1].bitcast(F32), ALU.subtract).then_inc(self.xl, 1)

            def pe_up(self, eng, n):
                eng.wait_ge(self.xl, n.at(1, 1))
                for m in range(NM):
                    if isinstance(n.pair, int) and n.pair == 0 and m % (NM // 2) == 0:
                        eng.wait_ge(self.wlo, 1 + m // (NM // 2))
                    if n.counts(NM, m - 3):
                        eng.wait_ge(self.g, n.at(NM, m - 3))
                    for c in range(2):
                        for i, (w, x) in enumerate(three(fc1s[self.l], xns)):
                            mm = nc.tensor.matmul(self.hbank[(n.parity * NM + m) % 4][:, 0:T],
                                                  w[:, c, m * P:(m + 1) * P], x[:, c, :],
                                                  start=(c == 0 and i == 0), stop=(c == 1 and i == 2))
                    mm.then_inc(self.h, 1)

            def act_up(self, eng, n):
                for m in range(NM):
                    eng.wait_ge(self.h, n.at(NM, m + 1))
                    if n.counts(1, -1):
                        eng.wait_ge(self.y, n.at(1, -1))
                    nc.scalar.activation(hT[n.parity][:, m, :], self.hbank[(n.parity * NM + m) % 4][:, 0:T],
                                         self.func, bias=fc1b[self.l][:, m:m + 1]).then_inc(self.g, 1)

            def pe_down(self, eng, n):
                ybank = (O_BANK, S_BANK[2])[n.parity]
                eng.wait_ge(self.g, n.at(NM, NM))
                if n.counts(1, -1):
                    eng.wait_ge(self.done, n.at(1, -1))
                for t in range(NT):
                    for m in range(NM):
                        mm = nc.tensor.matmul(ybank[:, t * C:(t + 1) * C], hT[n.parity][:, m, t * P:(t + 1) * P],
                                              fc2w[self.l][:, m, :], start=(m == 0), stop=(m == NM - 1))
                mm.then_inc(self.y, 1)

            def pool_back(self, eng, n):
                s, v = self.norm.x_before(n)
                eng.wait_ge(s, v)
                if n.counts(1, 0):
                    eng.wait_ge(self.done, n.at(1, 0))
                nc.gpsimd.tensor_tensor(xbias[:], x_all[:, bass.ds(n.at(NT, 0), NT), :],
                                        fc2b[self.l][:].unsqueeze(1).broadcast_to([P, NT, C]),
                                        ALU.add).then_inc(self.xb, 1)

            def dve_down(self, eng, n):
                ybank = (O_BANK, S_BANK[2])[n.parity]
                eng.wait_ge(self.y, n.at(1, 1))
                eng.wait_ge(self.xb, n.at(1, 1))
                nc.vector.tensor_tensor(x_all[:, bass.ds(n.at(NT, 0), NT), :],
                                        ybank[:, 0:NT * C].rearrange("p (t c) -> p t c", t=NT), xbias[:],
                                        ALU.add).then_inc(self.done, 1)

            def start(self, eng, which, attention, part):
                if which == "pe":
                    for b in range(2):
                        eng.wait_ge(attention.g_out[b], B * attention.G_OUTS[b])
                    self.pe_norm(eng, Img(0, 0))
                    return
                if part == "stats":
                    self.norm.dve_stats(eng, Img(0, 0))
                    return
                for b in range(2):
                    eng.wait_ge(attention.g_rdy[b], B * attention.G_USES[b])
                if which == "act":
                    self.act_norm(eng, Img(0, 0))
                elif part == "xhat":
                    self.norm.dve_xhat(eng, Img(0, 0), self.xt[1], 1, 0)
                else:
                    self.dve_norm(eng, Img(0, 0))

            def run(self, eng, which, between=None, following=None):
                if which == "act" and self.l == 0:
                    self.act_weights(eng)
                if which == "dve":
                    if self.l == 0:
                        self.low_weights(eng, nc.vector)
                    self.norm.dve_stats(eng, Img(0, 1))
                    self.norm.dve_xhat(eng, Img(0, 1), self.xt[1], 1, 0)
                    self.dve_norm(eng, Img(0, 1))
                elif which == "act":
                    self.act_up(eng, Img(0, 0))
                    self.act_norm(eng, Img(0, 1))
                else:
                    self.pe_up(eng, Img(0, 0))
                    self.pe_norm(eng, Img(0, 1))

                def pe_step(n, has_next, has_second):
                    if has_next:
                        self.pe_up(eng, n.next())
                    if has_second:
                        self.pe_norm(eng, n.next().next())
                    elif has_next and following:
                        following(eng, "transpose")
                    self.pe_down(eng, n)

                def act_step(n, has_next, has_second):
                    if has_next:
                        self.act_up(eng, n.next())
                    if has_second:
                        self.act_norm(eng, n.next().next())
                    elif has_next and following:
                        following(eng, "xn")

                def dve_step(n, has_next, has_second):
                    second = n.next().next()
                    last = has_next and not has_second and following
                    if has_second:
                        self.norm.dve_stats(eng, second)
                    elif last:
                        following(eng, "stats")
                    if has_second:
                        self.norm.dve_xhat(eng, second, self.xt[1], 1, 0)
                    elif last:
                        following(eng, "xhat")
                    if has_second:
                        self.dve_norm(eng, second)
                    elif last:
                        following(eng, "xn")
                    self.dve_down(eng, n)

                def step(n, has_next, has_second):
                    {"pe": pe_step, "act": act_step, "dve": dve_step}[which](n, has_next, has_second)
                    if between and isinstance(n.pair, int):
                        between(eng, n)
                mlp_loop(eng, step)

            def run_pool(self, eng, between=None, following=None):
                self.norm.pool_rstd(eng, Img(0, 1))

                def step(n, has_next, has_second):
                    if has_second:
                        self.norm.pool_rstd(eng, n.next().next())
                    elif has_next and following:
                        following(eng)
                    self.pool_back(eng, n)
                    if between and isinstance(n.pair, int):
                        between(eng, n)
                mlp_loop(eng, step)

        class Attention:

            def __init__(self, l, x_before, done, units, pv_after):
                self.l, self.done, self.units = l, done, units
                self.norm = Norm(2 * l, x_before)
                self.NU = len(units)
                self.pv_after = pv_after
                tiles = [len(self.tiles(u)) for u in range(self.NU)]
                self.cum = [sum(tiles[:u]) for u in range(self.NU + 1)]
                self.NTL = self.cum[-1]
                self.pt_cum = [[sum(self.pt_engine(v) == e for v in range(u)) for u in range(self.NU + 1)]
                               for e in range(2)]
                s = f"a{l}_"
                self.s_rdy = sem(s + "scores")
                self.m_rdy = sem(s + "max")
                self.e_rdy = sem(s + "exp")
                self.r_rdy = sem(s + "rsum")
                self.p_rdy = sem(s + "probs")
                self.t_rdy = sem(s + "probsT")
                self.pt = [sem(s + "ptA"), sem(s + "ptB")]
                self.pv = sem(s + "values")
                self.ao = [sem(s + "aoA"), sem(s + "aoB")]
                self.y = sem(s + "proj")
                self.xb = sem(s + "xbias")
                self.g_rdy = [sem(s + "g0"), sem(s + "g1")]
                self.g_out = [sem(s + "g0out"), sem(s + "g1out")]
                self.scat = sem(s + "scatter")
                self.relscat = sem(s + "relscat")

            def pe_scores(self, eng, n, u):
                used = self.cum[u - 2] if u >= 2 else self.cum[self.NU + u - 2] - self.NTL
                if n.counts(self.NTL, used):
                    eng.wait_ge(self.e_rdy, n.at(self.NTL, used))
                self.emit_scores(eng, n, u).then_inc(self.s_rdy, 1)

            def score_tiles(self, u):
                rows, cols, k = self.tiles(u)[0][0], self.tiles(u)[0][1], len(self.tiles(u))
                return S_BANK[u % 3][0:rows, 0:k * cols].rearrange("p (t c) -> p t c", t=k)

            def dve_max(self, eng, n, u):
                eng.wait_ge(self.s_rdy, n.at(self.NU, u + 1))
                sc = self.score_tiles(u)
                nc.vector.tensor_reduce(nmax[0:sc.shape[0], u % 3, 0:sc.shape[1]], sc, AX.X, ALU.max,
                                        negate=True).then_inc(self.m_rdy, 1)

            def act_exp(self, eng, n, u):
                eng.wait_ge(self.m_rdy, n.at(self.NU, u + 1))
                if n.counts(self.NU, u - 2):
                    eng.wait_ge(self.t_rdy, n.at(self.NU, u - 2))
                sc = self.score_tiles(u)
                rows, k, cols = sc.shape
                for t in range(k):
                    nc.scalar.activation(Pb[u % 3][0:rows, t, 0:cols], sc[:, t, :], ACT.Exp,
                                         bias=nmax[0:rows, u % 3, t:t + 1],
                                         accum_out=esum[0:rows, u % 3, t:t + 1]).then_inc(self.e_rdy, 1)

            def dve_norm(self, eng, n, u):
                rows, _, keep = self.tiles(u)[0]
                k = len(self.tiles(u))
                eng.wait_ge(self.e_rdy, n.at(self.NTL, self.cum[u + 1]))
                nc.vector.reciprocal(rsum[0:rows, u % 3, 0:k], esum[0:rows, u % 3, 0:k]).then_inc(self.r_rdy, 1)
                eng.wait_ge(self.r_rdy, n.at(self.NU, u + 1))
                for t in range(k):
                    nc.vector.tensor_scalar(Pb[u % 3][0:rows, t, 0:keep], Pb[u % 3][0:rows, t, 0:keep],
                                            rsum[0:rows, u % 3, t:t + 1], None, ALU.mult).then_inc(self.p_rdy, 1)

            def pe_probsT(self, eng, n, u):
                eng.wait_ge(self.p_rdy, n.at(self.NTL, self.cum[u + 1]))
                m, v = (n, u - 2) if u >= 2 else (n.prev(), self.NU + u - 2)
                e = self.pt_engine(v)
                if m.counts(self.pt_cum[e][-1], self.pt_cum[e][v + 1]):
                    eng.wait_ge(self.pt[e], m.at(self.pt_cum[e][-1], self.pt_cum[e][v + 1]))
                if len(self.tiles(u)) == 1:
                    land(eng, "pe")
                self.emit_probsT(eng, n, u).then_inc(self.t_rdy, 1)

            def pt_out(self, eng, n, u, copy):
                eng.wait_ge(self.t_rdy, n.at(self.NU, u + 1))
                per, k = self.pt_free(u)
                if n.counts(per, k):
                    eng.wait_ge(self.pv, n.at(per, k))
                copy(*self.pt_views(u)).then_inc(self.pt[self.pt_engine(u)], 1)

            def g_free(self, eng, n, b, outs_before):
                if n.counts(self.G_OUTS[b], outs_before):
                    eng.wait_ge(self.g_out[b], n.at(self.G_OUTS[b], outs_before))

            def pe_transpose_x(self, eng, n):
                for c in range(2):
                    self.g_free(eng, n, c, 0)
                    for t in range(NT):
                        eng.wait_ge(self.norm.xhat, n.at(NT, t + 1))
                        mm = nc.tensor.transpose(G_BANK[c][0:CH, t * P:(t + 1) * P],
                                                 xhat[:, t, c * CH:(c + 1) * CH], ident[:])
                    mm.then_inc(self.g_rdy[c], 1)

            def act_xn(self, eng, n):
                eng.wait_ge(self.g_rdy[0], n.at(self.G_USES[0], 1))
                for b in range(2):
                    if n.counts(self.G_USES[b], 0):
                        eng.wait_ge(self.g_rdy[b], n.at(self.G_USES[b], 0))
                nc.scalar.activation(xnT[:, 0, :], G_BANK[0][0:CH, 0:T], ACT.Identity,
                                     scale=lnw[2 * self.l][:, 0:1], bias=lnb[2 * self.l][:, 0:1]).then_inc(self.g_out[0], 1)

            def dve_xn(self, eng, n):
                eng.wait_ge(self.g_rdy[1], n.at(self.G_USES[1], 1))
                for b in range(2):
                    if n.counts(self.G_USES[b], 0):
                        eng.wait_ge(self.g_rdy[b], n.at(self.G_USES[b], 0))
                nc.vector.tensor_scalar(xnT[:, 1, :], G_BANK[1][0:CH, 0:T], lnw[2 * self.l][:, 1:2],
                                        lnb[2 * self.l][:, 1:2], ALU.mult, ALU.add).then_inc(self.g_out[1], 1)

            def xn_ready(self, eng, n):
                for b in range(2):
                    eng.wait_ge(self.g_out[b], n.at(self.G_OUTS[b], 1))

            def dve_stats(self, eng, n):
                self.norm.dve_stats(eng, n)

            def dve_xhat(self, eng, n):
                self.norm.dve_xhat(eng, n, self.g_rdy[1], self.G_USES[1], 1 - self.G_USES[1])

            def pool_xbias(self, eng, n):
                s, v = self.norm.x_before(n)
                eng.wait_ge(s, v)
                if n.counts(1, 0):
                    eng.wait_ge(self.done, n.at(1, 0))
                if isinstance(n.pair, int) and n.pair == 0:
                    eng.wait_ge(obias_done, 2)
                nc.gpsimd.tensor_tensor(xbias[:], x_all[:, bass.ds(n.at(NT, 0), NT), :],
                                        obias[self.l][:].unsqueeze(1).broadcast_to([P, NT, C]),
                                        ALU.add).then_inc(self.xb, 1)

            def dve_back(self, eng, n):
                eng.wait_ge(self.y, n.at(1, 1))
                eng.wait_ge(self.xb, n.at(1, 1))
                nc.vector.tensor_tensor(x_all[:, bass.ds(n.at(NT, 0), NT), :],
                                        Y_BANK[:, 0:NT * C].rearrange("p (t c) -> p t c", t=NT), xbias[:],
                                        ALU.add).then_inc(self.done, 1)

            def run(self, eng, which, meanwhile=None, between={}, started=False, before_v=None, following=None):
                fronts = {"pe": self.pe_fronts, "act": self.act_fronts, "dve": self.dve_fronts}[which]
                slot = {"pe": self.pe_slot, "act": self.act_slot, "dve": self.dve_slot}[which]
                for k in sorted(fronts):
                    if started and k <= 2:
                        continue
                    if before_v and k == self.V_SLOT:
                        before_v(eng)
                    for f in fronts[k]:
                        f(eng, Img(0, 0))
                    if k in between:
                        between[k](eng)
                if meanwhile:
                    meanwhile(eng)
                if which == "pe":
                    for u in range(3):
                        self.pe_scores(eng, Img(0, 0), u)
                elif which == "act":
                    for u in range(2):
                        self.act_exp(eng, Img(0, 0), u)
                else:
                    for u in range(3):
                        self.dve_max(eng, Img(0, 0), u)
                    self.dve_norm(eng, Img(0, 0), 0)

                def step(n, has_prev, has_next):
                    def ahead(u, k):
                        if u + k < self.NU:
                            return n, u + k
                        return (n.next(), u + k - self.NU) if has_next else None
                    for u in range(self.NU):
                        slot(eng, n, u, has_prev, ahead)
                        if not has_next:
                            for part in {"pe": {5: ("transpose",)}, "act": {6: ("xn",)},
                                         "dve": {3: ("stats",), 4: ("xhat",), 6: ("xn",)}}[which].get(u, ()):
                                following(eng, part)
                        if has_next:
                            for f in fronts.get(u, ()):
                                if f not in (self.pe_transpose_x, self.dve_xhat, self.act_xn):
                                    f(eng, n.next())
                    if not has_next:
                        last = len(self.pv_after) - 1
                        if which == "pe":
                            self.pe_values(eng, n, last)
                            self.pe_back(eng, n)
                        elif which == "act":
                            self.act_ao(eng, n, last)
                        else:
                            self.dve_ao(eng, n, last)
                            self.dve_back(eng, n)
                image_loop(eng, step)

            def groups_at(self, n, u, has_prev):
                behind = u - self.VALUES_BEHIND
                if behind < 0:
                    return [(n.prev(), g) for g in self.pv_after.get(self.NU + behind, ())] if has_prev else []
                return [(n, g) for g in self.pv_after.get(behind, ())]

            def pe_slot(self, eng, n, u, has_prev, ahead):
                if ahead(u, 3):
                    self.pe_scores(eng, *ahead(u, 3))
                self.pe_probsT(eng, n, u)
                if u == 2 and ahead(self.NU - 1, 1):
                    self.pe_transpose_x(eng, n.next())
                for m, g in self.groups_at(n, u, has_prev):
                    self.pe_values(eng, m, g)
                if u == self.VALUES_BEHIND and has_prev:
                    self.pe_back(eng, n.prev())

            def act_slot(self, eng, n, u, has_prev, ahead):
                if ahead(u, 2):
                    self.act_exp(eng, *ahead(u, 2))
                if self.pt_engine(u) == 0:
                    self.pt_out(eng, n, u, nc.scalar.copy)
                if u == 2 and ahead(self.NU - 1, 1):
                    self.act_xn(eng, n.next())
                for m, g in self.groups_at(n, u, has_prev):
                    self.act_ao(eng, m, g)

            def dve_slot(self, eng, n, u, has_prev, ahead):
                if ahead(u, 1):
                    self.dve_norm(eng, *ahead(u, 1))
                if self.pt_engine(u) == 1:
                    self.pt_out(eng, n, u, nc.vector.tensor_copy)
                if ahead(u, 3):
                    self.dve_max(eng, *ahead(u, 3))
                for m, g in self.groups_at(n, u, has_prev):
                    self.dve_ao(eng, m, g)
                if u == 1 and ahead(self.NU - 1, 1):
                    self.dve_xhat(eng, n.next())
                if u == self.VALUES_BEHIND and has_prev:
                    self.dve_back(eng, n.prev())

            def run_pool(self, eng, following, started=False, before_front=None, after_front=None):
                def front(n):
                    self.norm.pool_rstd(eng, n)
                    self.pool_front(eng, n)
                if not started:
                    self.norm.pool_rstd(eng, Img(0, 0))
                if before_front:
                    before_front(eng)
                self.pool_front(eng, Img(0, 0))
                if after_front:
                    after_front(eng)

                def step(n, has_prev, has_next):
                    if has_next:
                        front(n.next())
                    else:
                        following(eng)
                    self.pool_xbias(eng, n)
                image_loop(eng, step)

        class Attention0(Attention):
            G_USES = (6, 5)
            G_OUTS = (6, 5)
            V_SLOT = 10
            VALUES_BEHIND = 1

            def pt_engine(self, u):
                return int(self.units[u][0] == "rem" or u % 6 == 3)

            def tiles(self, u):
                return [(P, N0, N0)] * 2 if self.units[u][0] == "main" else [(P, NREM + N0, NREM)]

            def emit_scores(self, eng, n, u):
                kind, h = self.units[u]
                p = n.parity
                if u == 0:
                    eng.wait_ge(self.scat, n.at(16 * 2 * GH0, 16 * 2 * GH0))
                    eng.wait_ge(self.relscat, n.at(16 * 2 * GH0, 16 * 2 * GH0))
                if kind == "main":
                    k = K0[p][:, h, :].rearrange("k (r c) -> k r c", c=W)[:, 0:WS, 0:WS]
                    for t in range(2):
                        mm = nc.tensor.matmul(S_BANK[u % 3][:, t * N0:(t + 1) * N0],
                                              Q0[p][:, h, t * P:(t + 1) * P], k, start=True, stop=True)
                    return mm
                eng.wait_ge(self.gath, n.at(6, 6))
                land(eng, "pe")
                for j in range(2):
                    for keys, lo, hi in ((KR0[p], 0, NREM), (KP0, NREM, NREM + N0)):
                        mm = nc.tensor.matmul(S_BANK[u % 3][RPAD * j:RPAD * (j + 1), lo:hi],
                                              QR0[p][:, 2 * h + j, :], keys[:, 2 * h + j, :], start=True, stop=True)
                return mm

            def emit_probsT(self, eng, n, u):
                kind, h = self.units[u]
                pb, ptb = Pb[u % 3], PT_BANK[u % 2]
                if kind == "main":
                    for kc in range(2):
                        for t in range(2):
                            mm = nc.tensor.transpose(ptb[0:HT0, kc * T + t * P:kc * T + (t + 1) * P],
                                                     pb[:, t, kc * HT0:(kc + 1) * HT0], ident[:])
                    return mm
                return nc.tensor.transpose(ptb[0:NREM, 0:P], pb[:, 0, 0:NREM], ident[:])

            def pt_views(self, u):
                kind, h = self.units[u]
                if kind == "main":
                    return (PTm0[:, h, :, :].rearrange("p k (r c) -> p k r c", c=WS),
                            PT_BANK[u % 2][0:HT0, :].rearrange("p (k r c) -> p k r c", k=2, c=W)[:, :, 0:WS, 0:WS])
                return PTr0[:, h, :], PT_BANK[u % 2][0:NREM, 0:P]

            def pt_free(self, u):
                return 3, u // 6 - 2

            def pe_values(self, eng, n, q):
                p = n.parity
                for e in range(2):
                    eng.wait_ge(self.pt[e], n.at(self.pt_cum[e][-1], self.pt_cum[e][6 * q + 6]))
                if q == 0 and n.counts(1, 0):
                    eng.wait_ge(self.done, n.at(1, 0))
                if n.counts(9, 3 * q):
                    eng.wait_ge(self.ao[0], n.at(9, 3 * q))
                if n.counts(3, q):
                    eng.wait_ge(self.ao[1], n.at(3, q))
                for kc in range(2):
                    for j in range(4):
                        nc.tensor.matmul(O_BANK[32 * j:32 * j + 32, 0:N0], V0[p][:, kc, 4 * q + j, :],
                                         PTm0[:, 4 * q + j, kc, :], start=(kc == 0), stop=(kc == 1))
                for j in range(4):
                    mm = nc.tensor.matmul(O_BANK[32 * j:32 * j + 32, N0:T], VR0[p][:, 4 * q + j, :],
                                          PTr0[:, 2 * q + j // 2, RPAD * (j % 2):RPAD * (j % 2) + NREM],
                                          start=True, stop=True)
                mm.then_inc(self.pv, 1)

            def ao_view(self, q):
                return AO0[:, q, :].rearrange("p (r c) -> p r c", c=W)

            def act_ao(self, eng, n, q):
                eng.wait_ge(self.pv, n.at(3, q + 1))
                if n.counts(1, 0):
                    eng.wait_ge(self.y, n.at(1, 0))
                ao = self.ao_view(q)
                e = EDGE * WS
                parts = ((ao[:, 0:WS, WS:W], N0, e), (ao[:, WS:H, 0:WS], N0 + e, e),
                         (ao[:, WS:H, WS:W], N0 + 2 * e, EDGE * EDGE))
                for dst, at, k in parts:
                    nc.scalar.copy(dst, O_BANK[:, at:at + k].rearrange("p (r c) -> p r c", c=dst.shape[2]))\
                      .then_inc(self.ao[0], 1)

            def dve_ao(self, eng, n, q):
                eng.wait_ge(self.pv, n.at(3, q + 1))
                eng.wait_ge(self.ao[0], n.at(9, 3 * q + 3))
                if n.counts(1, 0):
                    eng.wait_ge(self.y, n.at(1, 0))
                nc.vector.tensor_copy(self.ao_view(q)[:, 0:WS, 0:WS],
                                      O_BANK[:, 0:N0].rearrange("p (r c) -> p r c", c=WS)).then_inc(self.ao[1], 1)

            def pe_back(self, eng, n):
                eng.wait_ge(self.ao[0], n.at(9, 9))
                eng.wait_ge(self.ao[1], n.at(3, 3))
                if n.counts(1, 0):
                    eng.wait_ge(self.done, n.at(1, 0))
                for t in range(NT):
                    for q in range(3):
                        mm = nc.tensor.matmul(Y_BANK[:, t * C:(t + 1) * C], AO0[:, q, t * P:(t + 1) * P],
                                              wproj0[:, q, :], start=(q == 0), stop=(q == 2))
                mm.then_inc(self.y, 1)

            def xn_views(self, c):
                return (xm0[:, c, :].rearrange("p (r c) -> p r c", c=WS),
                        G_BANK[c][0:CH, 0:T].rearrange("p (r c) -> p r c", c=W)[:, 0:WS, 0:WS])

            def act_xn(self, eng, n):
                eng.wait_ge(self.g_rdy[0], n.at(6, 1))
                for b in range(2):
                    if n.counts(self.G_USES[b], 0):
                        eng.wait_ge(self.g_rdy[b], n.at(self.G_USES[b], 0))
                nc.scalar.activation(*self.xn_views(0), ACT.Identity, scale=lnw[0][:, 0:1],
                                     bias=lnb[0][:, 0:1]).then_inc(self.xmain[0], 1)
                super().act_xn(eng, n)

            def dve_xn(self, eng, n):
                eng.wait_ge(self.g_rdy[1], n.at(5, 1))
                for b in range(2):
                    if n.counts(self.G_USES[b], 0):
                        eng.wait_ge(self.g_rdy[b], n.at(self.G_USES[b], 0))
                nc.vector.tensor_scalar(*self.xn_views(1), lnw[0][:, 1:2], lnb[0][:, 1:2],
                                        ALU.mult, ALU.add).then_inc(self.xmain[1], 1)
                super().dve_xn(eng, n)

            def pe_qk(self, eng, n, g):
                self.xn_ready(eng, n)
                for b in range(2):
                    self.g_free(eng, n, b, 1 + g)
                    for c in range(2):
                        mm = nc.tensor.matmul(G_BANK[b][0:CH, 0:T], wqkv0[:, c, b * C + g * CH:b * C + (g + 1) * CH],
                                              xnT[:, c, :], start=(c == 0), stop=(c == 1))
                    mm.then_inc(self.g_rdy[b], 1)

            def act_q(self, eng, n, g):
                eng.wait_ge(self.g_rdy[0], n.at(6, 2 + g))
                if g == 0:
                    if n.counts(16 * 2 * GH0, 0):
                        eng.wait_ge(self.scat, n.at(16 * 2 * GH0, 0))
                    if n.counts(6, 0):
                        eng.wait_ge(self.g_rdy[0], n.at(6, 0))
                nc.scalar.activation(self.qd[:, g, :], G_BANK[0][0:CH, 0:T], ACT.Identity,
                                     bias=qb0[:, g:g + 1]).then_inc(self.g_out[0], 1)

            def dve_k(self, eng, n, g):
                eng.wait_ge(self.g_rdy[1], n.at(5, 2 + g))
                if g == 0:
                    if n.counts(16 * 2 * GH0, 0):
                        eng.wait_ge(self.scat, n.at(16 * 2 * GH0, 0))
                nc.vector.tensor_scalar(self.kd[:, g, :], G_BANK[1][0:CH, 0:T], kb0[:, g:g + 1], D0 ** -0.5,
                                        ALU.add, ALU.mult).then_inc(self.g_out[1], 1)

            def pe_v(self, eng, n):
                for t in range(2):
                    self.g_free(eng, n, t, 4)
                    for c in range(2):
                        eng.wait_ge(self.xmain[c], n.at(1, 1))
                        mm = nc.tensor.matmul(G_BANK[t][0:HT0, 0:C], xm0[:, c, t * HT0:(t + 1) * HT0],
                                              wqkv0[:, c, 2 * C:3 * C], start=(c == 0), stop=(c == 1))
                    mm.then_inc(self.g_rdy[t], 1)
                self.g_free(eng, n, 0, 5)
                eng.wait_ge(self.xgath, n.at(3, 3))
                for c in range(2):
                    mm = nc.tensor.matmul(G_BANK[0][0:NREM, 0:C], xr0[:, c, :], wqkv0[:, c, 2 * C:3 * C],
                                          start=(c == 0), stop=(c == 1))
                mm.then_inc(self.g_rdy[0], 1)

            def act_v(self, eng, n):
                eng.wait_ge(self.g_rdy[0], n.at(6, 5))
                if n.counts(3, -3):
                    eng.wait_ge(self.pv, n.at(3, -3))
                nc.scalar.copy(V0[n.parity][:, 0, :, 0:D0], G_BANK[0][0:HT0, 0:C].rearrange("p (h d) -> p h d", d=D0))\
                  .then_inc(self.g_out[0], 1)
                eng.wait_ge(self.g_rdy[0], n.at(6, 6))
                nc.scalar.copy(VR0[n.parity][:, :, 0:D0], G_BANK[0][0:NREM, 0:C].rearrange("p (h d) -> p h d", d=D0))\
                  .then_inc(self.g_out[0], 1)

            def dve_v(self, eng, n):
                eng.wait_ge(self.g_rdy[1], n.at(5, 5))
                if n.counts(3, -3):
                    eng.wait_ge(self.pv, n.at(3, -3))
                nc.vector.tensor_copy(V0[n.parity][:, 1, :, 0:D0],
                                      G_BANK[1][0:HT0, 0:C].rearrange("p (h d) -> p h d", d=D0))\
                  .then_inc(self.g_out[1], 1)

            def pe_rel(self, eng, n, b):
                eng.wait_ge(self.g_out[0], n.at(6, 3))
                if isinstance(n.pair, int) and n.pair == 0:
                    eng.wait_ge(relw_h0_done, WS)
                    eng.wait_ge(relw_w0_done, WS)
                self.g_free(eng, n, b, 3)
                lines = G_BANK[b][0:GH0 * WS, :].rearrange("p (i x) -> p i x", i=H)
                qv = self.qd[:, :, :].rearrange("k g (r c) -> k r g c" if b else "k g (r c) -> k c g r", c=W)
                for i in range(WS):
                    mm = nc.tensor.matmul(lines[:, i:H:WS, :], relw[1 - b][:, i, :, :].rearrange("k h w -> k (h w)"),
                                          qv[:, i:H:WS, :, :], start=True, stop=True)
                mm.then_inc(self.g_rdy[b], 1)

            def dve_rel(self, eng, n):
                eng.wait_ge(self.g_rdy[1], n.at(5, 4))
                if n.counts(16 * 2 * GH0, 0):
                    eng.wait_ge(self.relscat, n.at(16 * 2 * GH0, 0))
                m = GH0 * WS
                nc.vector.tensor_copy(self.reld[0].rearrange("p g (r c) -> p g r c", c=W),
                                      G_BANK[1][0:m, :].rearrange("p (r g c) -> p g r c", g=2, c=W)).then_inc(self.g_out[1], 1)

            def act_rel(self, eng, n):
                eng.wait_ge(self.g_rdy[0], n.at(6, 4))
                if n.counts(16 * 2 * GH0, 0):
                    eng.wait_ge(self.relscat, n.at(16 * 2 * GH0, 0))
                m = GH0 * WS
                nc.scalar.copy(self.reld[1].rearrange("p g (r c) -> p g r c", c=W),
                               G_BANK[0][0:m, :].rearrange("p (c g r) -> p g r c", g=2, r=H)).then_inc(self.g_out[0], 1)

            def sp(self, eng, after_first):
                def image(n):
                    p = n.parity
                    eng.wait_ge(self.g_out[0], n.at(6, 3))
                    land(eng, "sp")
                    eng.wait_ge(self.g_out[1], n.at(5, 3))
                    land(eng, "sp")
                    if n.counts(self.NU, -self.NU):
                        eng.wait_ge(self.s_rdy, n.at(self.NU, -self.NU))
                    land(eng, "sp")
                    if n.counts(6, -6):
                        eng.wait_ge(self.gath, n.at(6, -6))
                    land(eng, "sp")
                    for h in range(GH0):
                        for src, dst in ((self.qd, Q0), (self.kd, K0)):
                            eng.dma_start(dst[p][0:D0, h:HEADS:GH0, :], src[h * D0:(h + 1) * D0, :, :]).then_inc(self.scat, 16)
                    eng.wait_ge(self.g_out[1], n.at(5, 4))
                    land(eng, "sp")
                    eng.wait_ge(self.g_out[0], n.at(6, 4))
                    land(eng, "sp")
                    for h in range(GH0):
                        for i in range(2):
                            eng.dma_start(Q0[p][D0 + i * WS:D0 + (i + 1) * WS, h:HEADS:GH0, :],
                                          self.reld[i][h * WS:(h + 1) * WS, :, :]).then_inc(self.relscat, 16)
                image(Img(0, 0))
                after_first()
                image(Img(0, 1))
                with eng.Fori(1, B // 2) as pair:
                    image(Img(pair, 0))
                    image(Img(pair, 1))

            def pool_front(self, eng, n):
                p, e = n.parity, EDGE * WS
                self.xn_ready(eng, n)
                if n.counts(6, 0):
                    eng.wait_ge(self.g_rdy[0], n.at(6, 0))
                land(eng, "pool")
                cuts = ((0, e, slice(0, WS), slice(WS, W)), (e, 2 * e, slice(WS, H), slice(0, WS)),
                        (2 * e, NREM, slice(WS, H), slice(WS, W)))

                def gather(dst, src, semaphore):
                    v = src.rearrange("p h (r c) -> p h r c", c=W)
                    for lo, hi, r, c in cuts:
                        nc.gpsimd.tensor_copy(dst[:, :, lo:hi].rearrange("p h (r c) -> p h r c", c=c.stop - c.start),
                                              v[:, :, r, c]).then_inc(semaphore, 1)
                gather(xr0[:, :, :], xnT[:, :, :], self.xgath)
                eng.wait_ge(self.scat, n.at(16 * 2 * GH0, 16 * 2 * GH0))
                if n.counts(self.NU, -self.NU):
                    eng.wait_ge(self.s_rdy, n.at(self.NU, -self.NU))
                land(eng, "pool")
                gather(KR0[p][0:D0], K0[p][0:D0], self.gath)
                eng.wait_ge(self.relscat, n.at(16 * 2 * GH0, 16 * 2 * GH0))
                land(eng, "pool")
                gather(QR0[p][0:K0ROWS], Q0[p][0:K0ROWS], self.gath)

            def setup(self):
                self.qd, self.kd = dense[0][:, 0:2, :], dense[1][:, 0:2, :]
                self.reld = [dense[i][0:GH0 * WS, 2:4, :] for i in range(2)]
                self.gath = sem("a0_gather")
                self.xmain = [sem("a0_xm0"), sem("a0_xm1")]
                self.xgath = sem("a0_xgather")
                self.pe_fronts = {2: [self.pe_transpose_x], 3: each(self.pe_qk, (0,)), 4: each(self.pe_qk, (1,)),
                                  6: each(self.pe_rel, (1,)), 7: each(self.pe_rel, (0,)), 10: [self.pe_v]}
                self.act_fronts = {2: [self.act_xn], 3: each(self.act_q, (0,)), 4: each(self.act_q, (1,)),
                                   7: [self.act_rel], 10: [self.act_v]}
                self.dve_fronts = {0: [self.dve_stats], 1: [self.dve_xhat], 2: [self.dve_xn], 3: each(self.dve_k, (0,)),
                                   4: each(self.dve_k, (1,)), 6: [self.dve_rel], 10: [self.dve_v]}

        class Attention1(Attention):
            G_USES = (10, 10)
            G_OUTS = (11, 11)
            V_SLOT = 7
            VALUES_BEHIND = 1

            def pt_engine(self, u):
                return u % 4 == 3

            def tiles(self, u):
                return [(P, T, T)] * 2

            def emit_scores(self, eng, n, u):
                p = n.parity
                if u == 0:
                    eng.wait_ge(self.scat, n.at(64, 64))
                    eng.wait_ge(self.relscat, n.at(64, 64))
                    eng.wait_ge(self.relscat_w, n.at(64, 64))
                for t in range(NT):
                    mm = nc.tensor.matmul(S_BANK[u % 3][:, t * T:(t + 1) * T], Q1[p][:, u, t * P:(t + 1) * P],
                                          K1[p][:, u, :], start=True, stop=True)
                return mm

            def emit_probsT(self, eng, n, u):
                for kc in range(2):
                    for t in range(NT):
                        mm = nc.tensor.transpose(PT_BANK[u % 2][:, kc * T + t * P:kc * T + (t + 1) * P],
                                                 Pb[u % 3][:, t, kc * P:(kc + 1) * P], ident[:])
                return mm

            def pt_views(self, u):
                return PT1[:, u % 4, :, :].rearrange("p k q -> p (k q)"), PT_BANK[u % 2][:, 0:2 * T]

            def pt_free(self, u):
                return NPAIR, u // 2 - 1

            def pe_values(self, eng, n, q):
                p = n.parity
                for e in range(2):
                    eng.wait_ge(self.pt[e], n.at(self.pt_cum[e][-1], self.pt_cum[e][2 * q + 2]))
                if q == 0 and n.counts(1, 0):
                    eng.wait_ge(self.done, n.at(1, 0))
                if n.counts(NPAIR, q):
                    eng.wait_ge(self.ao[0], n.at(NPAIR, q))
                for kc in range(2):
                    for j in range(2):
                        mm = nc.tensor.matmul(O_BANK[64 * j:64 * j + 64, 0:T], V1[p][:, kc, 2 * q + j, :],
                                              PT1[:, (2 * q + j) % 4, kc, :], start=(kc == 0), stop=(kc == 1))
                mm.then_inc(self.pv, 1)

            def act_ao(self, eng, n, q):
                eng.wait_ge(self.pv, n.at(NPAIR, q + 1))
                if n.counts(1, 0):
                    eng.wait_ge(self.y, n.at(1, 0))
                nc.scalar.copy(AO1[:, q, :], O_BANK[:, 0:T]).then_inc(self.ao[0], 1)

            def dve_ao(self, eng, n, q):
                pass

            def pe_back(self, eng, n):
                eng.wait_ge(self.ao[0], n.at(NPAIR, NPAIR))
                if n.counts(1, 0):
                    eng.wait_ge(self.done, n.at(1, 0))
                for t in range(NT):
                    for q in range(NPAIR):
                        mm = nc.tensor.matmul(Y_BANK[:, t * C:(t + 1) * C], AO1[:, q, t * P:(t + 1) * P],
                                              wo1[:, q, :], start=(q == 0), stop=(q == NPAIR - 1))
                mm.then_inc(self.y, 1)

            def act_xn(self, eng, n):
                eng.wait_ge(self.g_rdy[0], n.at(10, 1))
                for b in range(2):
                    if n.counts(10, 0):
                        eng.wait_ge(self.g_rdy[b], n.at(10, 0))
                for dst, done in ((xnT, self.x_whole[0]), (xnH, self.g_out[0])):
                    nc.scalar.activation(dst[:, 0, :], G_BANK[0][0:CH, 0:T], ACT.Identity,
                                         scale=lnw[2][:, 0:1], bias=lnb[2][:, 0:1]).then_inc(done, 1)

            def dve_xn(self, eng, n):
                eng.wait_ge(self.g_rdy[1], n.at(10, 1))
                for b in range(2):
                    if n.counts(10, 0):
                        eng.wait_ge(self.g_rdy[b], n.at(10, 0))
                for dst, done in ((xnT, self.x_whole[1]), (xnH, self.g_out[1])):
                    nc.vector.tensor_scalar(dst[:, 1, :], G_BANK[1][0:CH, 0:T], lnw[2][:, 1:2], lnb[2][:, 1:2],
                                            ALU.mult, ALU.add).then_inc(done, 1)
                for c in range(2):
                    eng.wait_ge(self.x_whole[c], n.at(1, 1))
                    eng.wait_ge(self.g_out[c], n.at(11, 1))
                nc.vector.tensor_tensor(xns[2], xns[0], xns[1].bitcast(F32), ALU.subtract).then_inc(self.xl, 1)

            def pe_qk(self, eng, n, g):
                eng.wait_ge(self.xl, n.at(1, 1))
                for b, w_parts in enumerate((wq1s, wk1s)):
                    self.g_free(eng, n, b, 1 + g)
                    for c in range(2):
                        for i, (w, x) in enumerate(three(w_parts, xns)):
                            mm = nc.tensor.matmul(G_BANK[b][0:CH, 0:T], w[:, c, g * CH:(g + 1) * CH], x[:, c, :],
                                                  start=(c == 0 and i == 0), stop=(c == 1 and i == 2))
                    mm.then_inc(self.g_rdy[b], 1)

            def act_q(self, eng, n, g):
                eng.wait_ge(self.g_rdy[0], n.at(10, 2 + g))
                if g == 0:
                    if n.counts(64, 0):
                        eng.wait_ge(self.scat, n.at(64, 0))
                    if n.counts(10, 0):
                        eng.wait_ge(self.g_rdy[1], n.at(10, 0))
                nc.scalar.activation(self.qd[:, g, :], G_BANK[0][0:CH, 0:T], ACT.Identity,
                                     bias=qb1[:, g:g + 1]).then_inc(self.g_out[0], 1)

            def dve_k(self, eng, n, g):
                eng.wait_ge(self.g_rdy[1], n.at(10, 2 + g))
                if g == 0:
                    if n.counts(64, 0):
                        eng.wait_ge(self.scat, n.at(64, 0))
                nc.vector.tensor_scalar(self.kd[:, g, :], G_BANK[1][0:CH, 0:T], kb1[:, g:g + 1], D1 ** -0.5,
                                        ALU.add, ALU.mult).then_inc(self.g_out[1], 1)

            def pe_v(self, eng, n, t):
                half = HEADS * D1 // 2
                for b in range(2):
                    self.g_free(eng, n, b, 9 + t)
                    for c in range(2):
                        for i, (x, w) in enumerate(three(xns, wv1s)):
                            mm = nc.tensor.matmul(G_BANK[b][:, 0:half], x[:, c, t * P:(t + 1) * P],
                                                  w[:, c, b * half:(b + 1) * half],
                                                  start=(c == 0 and i == 0), stop=(c == 1 and i == 2))
                    mm.then_inc(self.g_rdy[b], 1)

            def v_views(self, n, t, b):
                return (V1[n.parity][:, t, b * NPAIR:(b + 1) * NPAIR, 0:D1],
                        G_BANK[b][:, 0:HEADS * D1 // 2].rearrange("p (h d) -> p h d", d=D1))

            def act_v(self, eng, n, t):
                eng.wait_ge(self.g_rdy[0], n.at(10, 9 + t))
                if n.counts(NPAIR, -NPAIR):
                    eng.wait_ge(self.pv, n.at(NPAIR, -NPAIR))
                nc.scalar.copy(*self.v_views(n, t, 0)).then_inc(self.g_out[0], 1)

            def dve_v(self, eng, n, t):
                eng.wait_ge(self.g_rdy[1], n.at(10, 9 + t))
                if n.counts(NPAIR, -NPAIR):
                    eng.wait_ge(self.pv, n.at(NPAIR, -NPAIR))
                nc.vector.tensor_copy(*self.v_views(n, t, 1)).then_inc(self.g_out[1], 1)

            def pe_rel(self, eng, n):
                eng.wait_ge(self.g_out[0], n.at(11, 7))
                for b in range(2):
                    self.g_free(eng, n, b, 7)
                    for i in range(8):
                        for s in range(4):
                            v = self.qd[:, 3 * (s % 2):3 * (s % 2) + 3, :].rearrange("k g (r c) -> k g r c", c=W)
                            line = 8 * b + i
                            v = v[:, :, line, :] if s < 2 else v[:, :, :, line]
                            mm = nc.tensor.matmul(G_BANK[b][32 * s:32 * s + 32, 48 * i:48 * i + 48],
                                                  relw[2 + s // 2][:, line, :, :].rearrange("k a b -> k (a b)"), v,
                                                  start=True, stop=True)
                    mm.then_inc(self.g_rdy[b], 1)

            def rel_views(self, b, s):
                rows = slice(64 * s, 64 * s + 64)
                src = G_BANK[b][rows, 0:8 * 48]
                dst = self.reld[rows, :, :].rearrange("p g (r c) -> p g r c", c=W)
                if s == 0:
                    return dst[:, :, 8 * b:8 * b + 8, :], src.rearrange("p (r g c) -> p g r c", g=3, c=W)
                return dst[:, :, :, 8 * b:8 * b + 8], src.rearrange("p (c g r) -> p g r c", g=3, r=H)

            def act_rel(self, eng, n):
                eng.wait_ge(self.g_rdy[0], n.at(10, 8))
                if n.counts(64, 0):
                    eng.wait_ge(self.relscat, n.at(64, 0))
                    eng.wait_ge(self.relscat_w, n.at(64, 0))
                for s in range(2):
                    nc.scalar.copy(*self.rel_views(0, s)).then_inc(self.g_out[0], 1)

            def dve_rel(self, eng, n):
                eng.wait_ge(self.g_rdy[1], n.at(10, 8))
                if n.counts(64, 0):
                    eng.wait_ge(self.relscat, n.at(64, 0))
                    eng.wait_ge(self.relscat_w, n.at(64, 0))
                for s in range(2):
                    nc.vector.tensor_copy(*self.rel_views(1, s)).then_inc(self.g_out[1], 1)

            def sp(self, eng):
                def image(n):
                    p = n.parity
                    if n.counts(self.NU, -self.NU):
                        eng.wait_ge(self.s_rdy, n.at(self.NU, -self.NU))
                    land(eng, "sp")
                    eng.wait_ge(self.g_out[0], n.at(11, 7))
                    land(eng, "sp")
                    for j in range(2):
                        eng.dma_start(Q1[p][0:D1, j:HEADS:2, :], self.qd[D1 * j:D1 * (j + 1), :, :]).then_inc(self.scat, 16)
                    eng.wait_ge(self.g_out[1], n.at(11, 7))
                    land(eng, "sp")
                    for j in range(2):
                        eng.dma_start(K1[p][0:D1, j:HEADS:2, :], self.kd[D1 * j:D1 * (j + 1), :, :]).then_inc(self.scat, 16)
                    for b in range(2):
                        eng.wait_ge(self.g_out[b], n.at(11, 9))
                        land(eng, "sp")
                    self.scatter_rel(eng, n, (0, 1))
                image(Img(0, 0))
                image(Img(0, 1))
                with eng.Fori(1, B // 2) as pair:
                    image(Img(pair, 0))
                    image(Img(pair, 1))

            def scatter_rel(self, eng, n, halves):
                for s in halves:
                    for j in range(2):
                        at = K1REL + H * (s // 2)
                        first = 6 * (s % 2) + j
                        eng.dma_start(Q1[n.parity][at:at + H, first:first + 5:2, :],
                                      self.reld[32 * s + H * j:32 * s + H * (j + 1), :, :])\
                           .then_inc((self.relscat, self.relscat_w)[s // 2], 16)

            def pool_front(self, eng, n):
                if n.counts(self.NU, -self.NU):
                    eng.wait_ge(self.s_rdy, n.at(self.NU, -self.NU))
                for b in range(2):
                    eng.wait_ge(self.g_out[b], n.at(11, 9))
                land(eng, "pool")
                self.scatter_rel(eng, n, (2, 3))

            def start(self, eng, which, mlp, part):
                n = Img(0, 0)
                if which == "pe":
                    for c in range(2):
                        eng.wait_ge(mlp.xn[c], 2 * B)
                    self.pe_transpose_x(eng, n)
                elif part == "stats":
                    self.norm.dve_stats(eng, n)
                elif part == "xhat":
                    eng.wait_ge(mlp.xt[1], B)
                    self.norm.dve_xhat(eng, n, self.g_rdy[1], 10, -9)
                else:
                    eng.wait_ge(mlp.h, NM * B)
                    (self.act_xn if which == "act" else self.dve_xn)(eng, n)

            def setup(self):
                self.qd, self.kd, self.reld = dense[0][:], dense[1][:], rel_dense[:]
                self.relscat_w = sem("a1_relscat_w")
                self.x_whole = [sem("a1_x0"), sem("a1_x1")]
                self.xl = sem("a1_xl")
                self.pe_fronts = {2: [self.pe_transpose_x], 3: each(self.pe_qk, (0, 1, 2)), 4: each(self.pe_qk, (3, 4)),
                                  5: each(self.pe_qk, (5,)) + [self.pe_rel], 7: each(self.pe_v, (0,)),
                                  8: each(self.pe_v, (1,))}
                self.act_fronts = {2: [self.act_xn], 3: each(self.act_q, (0, 1, 2)), 4: each(self.act_q, (3, 4)),
                                   5: each(self.act_q, (5,)), 6: [self.act_rel], 7: each(self.act_v, (0,)),
                                   8: each(self.act_v, (1,))}
                self.dve_fronts = {0: [self.dve_stats], 1: [self.dve_xhat], 2: [self.dve_xn], 3: each(self.dve_k, (0, 1, 2)),
                                   4: each(self.dve_k, (3, 4)), 5: each(self.dve_k, (5,)), 6: [self.dve_rel],
                                   7: each(self.dve_v, (0,)), 8: each(self.dve_v, (1,))}

        a0 = Attention0(0, lambda n: (ld_x0 if n.index0() else ld_x, 16), xdone[0], L0_UNITS, {6 * q + 5: [q] for q in range(3)})
        m0 = Mlp(0, ACT.Gelu, xdone[0], xdone[1], False)
        a1 = Attention1(1, lambda n: (xdone[1], n.at(1, 1)), xdone[2], [("main", h) for h in range(HEADS)],
                        {2 * q + 1: [q] for q in range(NPAIR)})
        m1 = Mlp(1, ACT.Gelu_apprx_tanh, xdone[2], xdone[3], True)
        a0.setup()
        a1.setup()
        stages = (a0, m0, a1, m1)

        def stage_start(eng, i):
            if i:
                eng.wait_ge(xdone[i - 1], B)

        ctx.enter_context(nc.allow_non_contiguous_dma(reason="bias vectors to columns, a few KB once"))
        block = ctx.enter_context(nc.Block())

        zero_dve = [K1[0], KP0, V0[0], V0[1]]
        zero_pool = [vb0, vb1, wproj0, wo1, KR0[0], KR0[1], QR0[0], QR0[1], VR0[0], VR0[1]]
        NZ = len(zero_dve) + len(zero_pool)
        vbc = [area[:, 0:3 * P].rearrange("p (q m) -> p q m", q=3),
               area[:, 3 * P:(3 + NPAIR) * P].rearrange("p (q m) -> p q m", q=NPAIR)]
        tab_bank = O_BANK
        relw_spec = ((WS, GH0, blk0), (WS, GH0, blk0), (H, 2, blk1), (W, 2, blk1))

        def spread(engine, i):
            win, heads, blk = relw_spec[i]
            for line in range(win):
                row = reltab[i][:, win - 1 - line:2 * win - 1 - line]
                yield engine.tensor_tensor(relw[i][:, line, :, :], row.unsqueeze(1).broadcast_to([CH, heads, win]),
                                           blk[:].unsqueeze(2).broadcast_to([CH, heads, win]), ALU.mult)

        def table_products(layer):
            for i in (2 * layer, 2 * layer + 1):
                n = reltab[i].shape[1]
                nc.tensor.matmul(tab_bank[0:CH, 32 * i:32 * i + n], relnat[i].rearrange("r h d -> r (h d)"),
                                 (flip, flip27)[layer == 0][:], start=True, stop=True).then_inc(prep_pe, 1)

        def pe_meanwhile(pe):
            pe.wait_ge(ld_w, 16 * len(rest))
            table_products(1)
            pe.wait_ge(prep_dve, 4)
            pe.wait_ge(prep_dve, 6)
            for l, (w, k) in enumerate(((wproj0, 3), (wo1, NPAIR))):
                for q in range(k):
                    mm = nc.tensor.matmul(O_BANK[:, l * C:(l + 1) * C], vbc[l][:, q, :], w[:, q, :],
                                          start=(q == 0), stop=(q == k - 1))
                mm.then_inc(prep_pe, 1)
            pe.wait_ge(obias_done, 2)
            pe.wait_ge(kpad_done, 1)

        def dve_meanwhile(dve):
            dve.wait_ge(prep_pe, 4)
            for i in (2, 3):
                nc.vector.tensor_copy(reltab[i][:], tab_bank[0:CH, 32 * i:32 * i + 31]).then_inc(prep_dve, 1)
            dve.wait_ge(ld_zeroed, 16 * len(late))
            for l, (v, k) in enumerate(((vb0, 3), (vb1, NPAIR))):
                nc.vector.tensor_copy(vbc[l], v[:].unsqueeze(2).broadcast_to([P, k, P])).then_inc(prep_dve, 1)
            nc.vector.tensor_scalar(KP0[0:D0], kpad0[:].unsqueeze(2).broadcast_to([D0, HEADS, N0]), D0 ** -0.5, None,
                                    ALU.mult).then_inc(kpad_done, 1)
            dve.wait_ge(prep_pe, 6)
            dve.wait_ge(ld_w, 16 * len(rest))
            for l in range(2):
                nc.vector.tensor_tensor(obias[l][:], O_BANK[:, l * C:(l + 1) * C], obias[l][:], ALU.add)\
                  .then_inc(obias_done, 1)

        attention1_weights = (wq1s, wk1s, wv1s)

        def weights_at(n):
            return {(0, 0): 0, (0, 1): 1, (B // 2 - 1, 0): 2}.get((n.pair, n.par))

        def act_weights1(act, n):
            if weights_at(n) is not None:
                whole, high, _ = attention1_weights[weights_at(n)]
                nc.scalar.copy(high, whole).then_inc(w1_high, 1)

        def pool_weights1(pool, n):
            if weights_at(n) is not None:
                whole, high, low = attention1_weights[weights_at(n)]
                pool.wait_ge(w1_high, weights_at(n) + 1)
                nc.gpsimd.tensor_tensor(low, whole, high.bitcast(F32), ALU.subtract).then_inc(w1_low, 1)

        def dve_tables1(dve, n):
            if n.pair == 0:
                dve.wait_ge(prep_dve, 4)
                for instruction in spread(nc.vector, 2 + n.par):
                    instruction.then_inc(relw_done, 1)

        @block.sync
        def _(sp):
            sp.dma_start(x_all[:, 0:NT, :], x_view[:, 0:NT, :]).then_inc(ld_x0, 16)
            for dst, src in for_norm:
                sp.dma_start(dst, src).then_inc(ld_norm, 16)
            for dst, src in first:
                sp.dma_start(dst, src).then_inc(ld_first, 16)
            sp.dma_start(x_all[:, NT:, :], x_view[:, NT:, :]).then_inc(ld_x, 16)
            sp.wait_ge(zeroed, NZ)
            for dst, src in late:
                sp.dma_start(dst, src).then_inc(ld_zeroed, 16)
            for dst, src in rest:
                sp.dma_start(dst, src).then_inc(ld_w, 16)
            sp.wait_ge(zeroed_more, 1)

            def load_later():
                sp.wait_ge(zeroed_more, 3)
                for dst, src in late_odd:
                    sp.dma_start(dst, src).then_inc(ld_odd, 16)
                for dst, src in later:
                    sp.dma_start(dst, src).then_inc(ld_later, 16)
                sp.wait_ge(ld_odd, 16 * len(late_odd))
            a0.sp(sp, load_later)
            stage_start(sp, 1)
            a1.sp(sp)
            with sp.Fori(0, B) as n:
                sp.wait_ge(xdone[3], n + 1)
                sp.dma_start(out_view[:, bass.ds(n * NT, NT), :], x_all[:, bass.ds(n * NT, NT), :]).then_inc(out_done, 16)
            sp.wait_ge(out_done, 16 * B)

        @block.gpsimd
        def _(pool):
            nc.gpsimd.memset(mhalf[:], -0.5).then_inc(prep_pool, 1)
            for z in zero_pool:
                nc.gpsimd.memset(z[:], 0.0).then_inc(zeroed, 1)
            pool.wait_ge(prep_pool, 1)

            def tables(pool):
                for z in (Q1[0], K1[1]):
                    nc.gpsimd.memset(z[:], 0.0).then_inc(zeroed_more, 1)
                pool.wait_ge(prep_dve, 2)
                for instruction in spread(nc.gpsimd, 1):
                    instruction.then_inc(relw_w0_done, 1)
                nc.gpsimd.memset(Q1[1][:], 0.0).then_inc(zeroed_more, 1)
                pool.wait_ge(ld_zeroed, 16 * len(late))
            a0.run_pool(pool, following=lambda e: m0.norm.pool_rstd(e, Img(0, 0)), before_front=tables)
            stage_start(pool, 1)
            pool.wait_ge(ld_later, 16 * len(later))
            m0.run_pool(pool, pool_weights1, lambda e: a1.norm.pool_rstd(e, Img(0, 0)))
            stage_start(pool, 2)
            for v in V1:
                nc.gpsimd.memset(v[:, :, :, D1:64], 0.0).then_inc(prep_pool, 1)
            a1.run_pool(pool, following=lambda e: m1.norm.pool_rstd(e, Img(0, 0)), started=True,
                        after_front=lambda e: m1.low_weights(e, nc.gpsimd))
            stage_start(pool, 3)
            m1.run_pool(pool)

        @block.tensor
        def _(pe):
            pe.wait_ge(ld_norm, 16 * len(for_norm))

            def tables(pe):
                pe.wait_ge(ld_first, 16 * len(first))
                table_products(0)
            a0.run(pe, "pe", pe_meanwhile, {2: tables}, following=lambda e, part: m0.start(e, "pe", a0, part))
            stage_start(pe, 1)
            pe.wait_ge(ld_later, 16 * len(later))
            m0.run(pe, "pe", following=lambda e, part: a1.start(e, "pe", m0, part))
            pe.wait_ge(relw_done, H + W)
            pe.wait_ge(w1_low, 3)

            def v_space(pe):
                stage_start(pe, 2)
                pe.wait_ge(prep_pool, 3)
            a1.run(pe, "pe", started=True, before_v=v_space, following=lambda e, part: m1.start(e, "pe", a1, part))
            stage_start(pe, 3)
            m1.run(pe, "pe")

        @block.scalar
        def _(act):
            act.wait_ge(ld_norm, 16 * len(for_norm))

            def loaded(act):
                act.wait_ge(ld_first, 16 * len(first))
                act.wait_ge(zeroed, NZ)

            def start_mlp0(act, part):
                act.wait_ge(ld_later, 16 * len(later))
                m0.start(act, "act", a0, part)
            a0.run(act, "act", between={2: loaded}, following=start_mlp0)
            stage_start(act, 1)
            m0.run(act, "act", act_weights1, following=lambda e, part: a1.start(e, "act", m0, part))
            a1.run(act, "act", m1.act_weights, started=True, following=lambda e, part: m1.start(e, "act", a1, part))
            stage_start(act, 3)
            m1.run(act, "act")

        @block.vector
        def _(dve):
            def zero(buffers):
                for z in buffers:
                    nc.vector.memset(z[:], 0.0).then_inc(zeroed, 1)
            zero(zero_dve[:1])
            dve.wait_ge(ld_norm, 16 * len(for_norm))

            def tables(dve):
                dve.wait_ge(ld_first, 16 * len(first))
                dve.wait_ge(zeroed, NZ)
                dve.wait_ge(prep_pe, 2)
                for i in (0, 1):
                    nc.vector.tensor_copy(reltab[i][:], tab_bank[0:CH, 32 * i:32 * i + 27]).then_inc(prep_dve, 1)
                dve.wait_ge(prep_dve, 2)
                for instruction in spread(nc.vector, 0):
                    instruction.then_inc(relw_h0_done, 1)

            def start_mlp0(dve, part):
                dve.wait_ge(ld_later, 16 * len(later))
                m0.start(dve, "dve", a0, part)
            a0.run(dve, "dve", dve_meanwhile, {0: lambda e: zero(zero_dve[1:2]), 1: lambda e: zero(zero_dve[2:]), 2: tables},
                   following=start_mlp0)
            stage_start(dve, 1)
            m0.run(dve, "dve", dve_tables1, following=lambda e, part: a1.start(e, "dve", m0, part))
            a1.run(dve, "dve", started=True, following=lambda e, part: m1.start(e, "dve", a1, part))
            stage_start(dve, 3)
            m1.run(dve, "dve")


def shape_constants():
    c = {"c_ident": np.eye(P), "c_flip31": np.eye(31)[::-1], "c_flip27": np.eye(27)[::-1]}
    ch = np.arange(CH)
    c["c_blk0"] = ch[:, None] // D0 == np.arange(GH0)
    c["c_blk1"] = ch[:, None] // D1 == np.arange(2)
    t = np.arange(T)
    c["c_hot0"] = np.concatenate([np.arange(WS)[:, None] == (t // W) % WS, np.arange(WS)[:, None] == (t % W) % WS])
    c["c_hot1"] = np.concatenate([np.arange(H)[:, None] == t // W, np.arange(W)[:, None] == t % W])
    grid = t.reshape(H, W)
    parts = [grid[:WS, WS:].ravel(), grid[WS:, :WS].ravel(), grid[WS:, WS:].ravel()]
    rem = np.concatenate(parts)
    window = np.repeat(np.arange(3), [len(p) for p in parts])
    mask = np.where(np.arange(3)[:, None] == window, 0.0, NEG)
    c["c_hotrem"] = np.concatenate([c["c_hot0"][:, rem], mask])
    c["c_qwin"] = np.concatenate([np.arange(3)[:, None] == window, np.zeros((3, RPAD - NREM))], axis=1)
    kh, kw = np.arange(N0) // WS, np.arange(N0) % WS
    pad = [kw >= EDGE, kh >= EDGE, (kh >= EDGE) | (kw >= EDGE)]
    c["c_hotpad"] = np.concatenate([np.arange(WS)[:, None] == kh, np.arange(WS)[:, None] == kw,
                                    np.where(np.stack(pad), 0.0, NEG)])
    return {k: np.ascontiguousarray(v, dtype=np.float32) for k, v in c.items()}


def kernel(**inputs):
    import concourse.bacc as bacc
    from concourse.bass_utils import run_bass_kernel_spmd

    nc = bacc.Bacc("TRN2", target_bir_lowering=False, num_devices=1)
    arrays = {k: np.ascontiguousarray(v) for k, v in inputs.items()}
    arrays.update(shape_constants())
    arrays = {f"in_{k}": v for k, v in arrays.items()}
    aps = {k[3:]: nc.dram_tensor(k, v.shape, mybir.dt.from_np(v.dtype), kind="ExternalInput").ap()
           for k, v in arrays.items()}
    out = nc.dram_tensor("out", (B, H, W, C), F32, kind="ExternalOutput").ap()
    build(nc, aps, out)
    r = run_bass_kernel_spmd(nc, [arrays], core_ids=[0])
    return r.results[0]["out"]
```
